# Optimizing a Trainium2 kernel written in Bass

```python
import numpy as np
import jax
import jax.numpy as jnp

def _softmax(x, axis=-1):
    return jax.nn.softmax(x, axis=axis)

def _gelu(x):
    return jax.nn.gelu(x, approximate=True)

def _silu(x):
    return jax.nn.silu(x)

def _sigmoid(x):
    return jax.nn.sigmoid(x)

def _layernorm(x, axis=-1, eps=1e-05):
    m = jnp.mean(x, axis=axis, keepdims=True)
    v = jnp.var(x, axis=axis, keepdims=True)
    return (x - m) / jnp.sqrt(v + eps)

def _scatter_add(tgt, idx, src, axis=0):
    return tgt.at[idx].add(src)

def _segment_sum(src, seg, n):
    return jax.ops.segment_sum(src, seg, n)
kernel_name = 'mk_sandwich_d2_jaxref_r4_6c1d9b'

def setup_inputs(seed: int=0):
    np.random.seed(seed)
    _w = jnp.asarray

    def _L0_attn_setup():
        import jax, jax.numpy as jnp
        import numpy as np
        EMBED_DIM = 256
        NUM_HEADS = 16
        HEAD_DIM = EMBED_DIM // NUM_HEADS
        BATCH = 4
        SEQ = 512
        key = jax.random.key(seed)
        ks = jax.random.split(key, 5)
        s_in = 1.0 / np.sqrt(EMBED_DIM)
        x = jax.random.normal(ks[0], (BATCH, SEQ, EMBED_DIM), dtype=jnp.float32)
        qkv_w = jax.random.uniform(ks[1], (3 * EMBED_DIM, EMBED_DIM), jnp.float32, -s_in, s_in)
        qkv_b = jax.random.uniform(ks[2], (3 * EMBED_DIM,), jnp.float32, -s_in, s_in)
        out_w = jax.random.uniform(ks[3], (EMBED_DIM, EMBED_DIM), jnp.float32, -s_in, s_in)
        out_b = jax.random.uniform(ks[4], (EMBED_DIM,), jnp.float32, -s_in, s_in)
        return {'x': x, 'qkv_w': qkv_w, 'qkv_b': qkv_b, 'out_w': out_w, 'out_b': out_b}
    _L0_attn_in = _L0_attn_setup()

    def _L0_ffn_setup():
        import jax, jax.numpy as jnp
        import numpy as np
        EMB = 256
        FF = 4 * EMB

        def _ternary(w):
            scale = jnp.maximum(jnp.mean(jnp.abs(w)), 1e-08)
            w_t = jnp.clip(jnp.round(w / scale), -1.0, 1.0)
            return w + jax.lax.stop_gradient(w_t - w)
        key = jax.random.key(seed)
        kx, k1, k2, kb1, kb2 = jax.random.split(key, 5)
        x = jax.random.normal(kx, (4, 512, EMB), dtype=jnp.float32)
        lim1 = 1.0 / np.sqrt(EMB)
        lim2 = 1.0 / np.sqrt(FF)
        W1 = jax.random.uniform(k1, (FF, EMB), jnp.float32, -lim1, lim1)
        b1 = jax.random.uniform(kb1, (FF,), jnp.float32, -lim1, lim1)
        W2 = jax.random.uniform(k2, (EMB, FF), jnp.float32, -lim2, lim2)
        b2 = jax.random.uniform(kb2, (EMB,), jnp.float32, -lim2, lim2)
        return {'x': x, 'W1': W1, 'b1': b1, 'W2': W2, 'b2': b2}
    _L0_ffn_in = _L0_ffn_setup()

    def _L1_attn_setup():
        import jax, jax.numpy as jnp
        import numpy as np
        B, S, DM, H, DH = (2, 512, 256, 16, 64)
        HID = H * DH

        def _xavier(key, shape):
            fan_out, fan_in = shape
            lim = float(np.sqrt(6.0 / (fan_in + fan_out)))
            return jax.random.uniform(key, shape, jnp.float32, -lim, lim)

        def _gla_scan(q, k, v, g):
            qt = jnp.moveaxis(q, 1, 0)
            kt = jnp.moveaxis(k, 1, 0)
            vt = jnp.moveaxis(v, 1, 0)
            gt = jnp.moveaxis(g, 1, 0)

            def step(s, inp):
                qi, ki, vi, gi = inp
                s = jnp.exp(gi)[:, :, None, None] * s + ki[..., :, None] * vi[..., None, :]
                o = jnp.einsum('bhk,bhkv->bhv', qi, s)
                return (s, o)
            s0 = jnp.zeros(q.shape[0:1] + q.shape[2:] + q.shape[-1:], q.dtype)
            _, o = jax.lax.scan(step, s0, (qt, kt, vt, gt))
            return jnp.moveaxis(o, 0, 1)
        key = jax.random.key(seed)
        ks = jax.random.split(key, 8)
        return {'x': jax.random.normal(ks[0], (B, S, DM), jnp.float32), 'Wq': _xavier(ks[1], (HID, DM)), 'Wk': _xavier(ks[2], (HID, DM)), 'Wv': _xavier(ks[3], (HID, DM)), 'Wo': _xavier(ks[4], (DM, HID)), 'Wg': _xavier(ks[5], (HID, DM)), 'Wog': _xavier(ks[6], (HID, DM)), 'Wd': _xavier(ks[7], (H, DM)), 'bd': jnp.full((H,), -2.0, jnp.float32), 'norm_w': jnp.ones((HID,), jnp.float32)}
    _L1_attn_in = _L1_attn_setup()

    def _L1_ffn_setup():
        import jax, jax.numpy as jnp
        import numpy as np
        B, S, D, E, H, K = (4, 512, 256, 8, 128, 2)
        key = jax.random.key(seed)
        ks = jax.random.split(key, 11)
        sc = 0.02
        return {'x': jax.random.normal(ks[0], (B, S, D), dtype=jnp.float32), 'gate_W': jax.random.normal(ks[1], (D, E), dtype=jnp.float32) * sc, 'W1': jax.random.normal(ks[2], (E, D, H), dtype=jnp.float32) * sc, 'b1': jnp.zeros((E, H), dtype=jnp.float32), 'W2': jax.random.normal(ks[3], (E, H, D), dtype=jnp.float32) * sc, 'b2': jnp.zeros((E, D), dtype=jnp.float32), 'Ws1': jax.random.normal(ks[4], (D, H), dtype=jnp.float32) * sc, 'bs1': jnp.zeros((H,), dtype=jnp.float32), 'Ws2': jax.random.normal(ks[5], (H, D), dtype=jnp.float32) * sc, 'bs2': jnp.zeros((D,), dtype=jnp.float32), 'route_scale': jnp.ones((), dtype=jnp.float32)}
    _L1_ffn_in = _L1_ffn_setup()
    _d = {'L0_attn_x': _L0_attn_in['x'], 'L0_attn_qkv_w': _L0_attn_in['qkv_w'], 'L0_attn_qkv_b': _L0_attn_in['qkv_b'], 'L0_attn_out_w': _L0_attn_in['out_w'], 'L0_attn_out_b': _L0_attn_in['out_b'], 'L0_ffn_W1': _L0_ffn_in['W1'], 'L0_ffn_b1': _L0_ffn_in['b1'], 'L0_ffn_W2': _L0_ffn_in['W2'], 'L0_ffn_b2': _L0_ffn_in['b2'], 'L1_attn_Wq': _L1_attn_in['Wq'], 'L1_attn_Wk': _L1_attn_in['Wk'], 'L1_attn_Wv': _L1_attn_in['Wv'], 'L1_attn_Wo': _L1_attn_in['Wo'], 'L1_attn_Wg': _L1_attn_in['Wg'], 'L1_attn_Wog': _L1_attn_in['Wog'], 'L1_attn_Wd': _L1_attn_in['Wd'], 'L1_attn_bd': _L1_attn_in['bd'], 'L1_attn_norm_w': _L1_attn_in['norm_w'], 'L1_ffn_gate_W': _L1_ffn_in['gate_W'], 'L1_ffn_W1': _L1_ffn_in['W1'], 'L1_ffn_b1': _L1_ffn_in['b1'], 'L1_ffn_W2': _L1_ffn_in['W2'], 'L1_ffn_b2': _L1_ffn_in['b2'], 'L1_ffn_Ws1': _L1_ffn_in['Ws1'], 'L1_ffn_bs1': _L1_ffn_in['bs1'], 'L1_ffn_Ws2': _L1_ffn_in['Ws2'], 'L1_ffn_bs2': _L1_ffn_in['bs2'], 'L1_ffn_route_scale': _L1_ffn_in['route_scale']}
    _x0 = _d['L0_attn_x']
    _d['L0_attn_x'] = jax.random.normal(jax.random.fold_in(jax.random.key(seed), 1), (4, 1024, 256), dtype=_x0.dtype)
    del _x0
    return _d

def reference(L0_attn_x, L0_attn_qkv_w, L0_attn_qkv_b, L0_attn_out_w, L0_attn_out_b, L0_ffn_W1, L0_ffn_b1, L0_ffn_W2, L0_ffn_b2, L1_attn_Wq, L1_attn_Wk, L1_attn_Wv, L1_attn_Wo, L1_attn_Wg, L1_attn_Wog, L1_attn_Wd, L1_attn_bd, L1_attn_norm_w, L1_ffn_gate_W, L1_ffn_W1, L1_ffn_b1, L1_ffn_W2, L1_ffn_b2, L1_ffn_Ws1, L1_ffn_bs1, L1_ffn_Ws2, L1_ffn_bs2, L1_ffn_route_scale):

    def _L0_attn_ref(x, qkv_w, qkv_b, out_w, out_b):
        import jax, jax.numpy as jnp
        import numpy as np
        EMBED_DIM = 256
        NUM_HEADS = 16
        HEAD_DIM = EMBED_DIM // NUM_HEADS
        BATCH = 4
        SEQ = 512
        B, S, E = x.shape
        qkv = x @ qkv_w.T + qkv_b
        qkv = qkv.reshape(B, S, 3, NUM_HEADS, HEAD_DIM)
        qkv = jnp.transpose(qkv, (2, 0, 3, 1, 4))
        q, k, v = (qkv[0], qkv[1], qkv[2])
        scale = jnp.sqrt(jnp.float32(HEAD_DIM))
        scores = jnp.einsum('bhqd,bhkd->bhqk', q, k) / scale
        attn = jax.nn.softmax(scores, axis=-1)
        out = jnp.einsum('bhqk,bhkd->bhqd', attn, v)
        out = jnp.transpose(out, (0, 2, 1, 3)).reshape(B, S, E)
        return out @ out_w.T + out_b

    def _L0_ffn_ref(x, W1, b1, W2, b2):
        import jax, jax.numpy as jnp
        import numpy as np
        EMB = 256
        FF = 4 * EMB

        def _ternary(w):
            scale = jnp.maximum(jnp.mean(jnp.abs(w)), 1e-08)
            w_t = jnp.clip(jnp.round(w / scale), -1.0, 1.0)
            return w + jax.lax.stop_gradient(w_t - w)
        h = jnp.einsum('bsd,fd->bsf', x, _ternary(W1)) + b1
        h = jax.nn.gelu(h, approximate=False)
        out = jnp.einsum('bsf,df->bsd', h, _ternary(W2)) + b2
        return out

    def _L1_attn_ref(x, Wq, Wk, Wv, Wo, Wg, Wog, Wd, bd, norm_w):
        import jax, jax.numpy as jnp
        import numpy as np
        B, S, DM, H, DH = (2, 512, 256, 16, 64)
        HID = H * DH

        def _xavier(key, shape):
            fan_out, fan_in = shape
            lim = float(np.sqrt(6.0 / (fan_in + fan_out)))
            return jax.random.uniform(key, shape, jnp.float32, -lim, lim)

        def _gla_scan(q, k, v, g):
            qt = jnp.moveaxis(q, 1, 0)
            kt = jnp.moveaxis(k, 1, 0)
            vt = jnp.moveaxis(v, 1, 0)
            gt = jnp.moveaxis(g, 1, 0)

            def step(s, inp):
                qi, ki, vi, gi = inp
                s = jnp.exp(gi)[:, :, None, None] * s + ki[..., :, None] * vi[..., None, :]
                o = jnp.einsum('bhk,bhkv->bhv', qi, s)
                return (s, o)
            s0 = jnp.zeros(q.shape[0:1] + q.shape[2:] + q.shape[-1:], q.dtype)
            _, o = jax.lax.scan(step, s0, (qt, kt, vt, gt))
            return jnp.moveaxis(o, 0, 1)
        b, s, _ = x.shape
        q = (x @ Wq.T).reshape(b, s, H, DH)
        k = (x @ Wk.T).reshape(b, s, H, DH)
        v = (x @ Wv.T).reshape(b, s, H, DH)
        log_decay = -jax.nn.softplus(x @ Wd.T + bd)
        gate = jax.nn.sigmoid((x @ Wg.T).reshape(b, s, H, DH))
        k_gated = k * gate
        out = _gla_scan(q, k_gated, v, log_decay)
        out = out.reshape(b, s, HID)
        eps = jnp.finfo(out.dtype).eps
        out = out * jax.lax.rsqrt(jnp.mean(out * out, -1, keepdims=True) + eps) * norm_w
        out = out * jax.nn.sigmoid(x @ Wog.T)
        return out @ Wo.T

    def _L1_ffn_ref(x, gate_W, W1, b1, W2, b2, Ws1, bs1, Ws2, bs2, route_scale):
        import jax, jax.numpy as jnp
        import numpy as np
        B, S, D, E, H, K = (4, 512, 256, 8, 128, 2)
        scores = jax.nn.sigmoid(x @ gate_W) * route_scale
        topk_scores, topk_idx = jax.lax.top_k(scores, K)
        topk_w = topk_scores / topk_scores.sum(-1, keepdims=True)
        onehot = jax.nn.one_hot(topk_idx, E, dtype=x.dtype)
        gate_full = jnp.einsum('bsk,bske->bse', topk_w, onehot)
        h = jax.nn.gelu(jnp.einsum('bsd,edh->bseh', x, W1) + b1, approximate=False)
        y = jnp.einsum('bseh,ehd->bsed', h, W2) + b2
        expert_out = jnp.einsum('bse,bsed->bsd', gate_full, y)
        shared = jax.nn.gelu(x @ Ws1 + bs1, approximate=False) @ Ws2 + bs2
        return expert_out + shared
    x = L0_attn_x
    x = x + _layernorm(_L0_attn_ref(_layernorm(x, axis=-1), L0_attn_qkv_w, L0_attn_qkv_b, L0_attn_out_w, L0_attn_out_b), axis=-1)
    x = x + _layernorm(_L0_ffn_ref(_layernorm(x, axis=-1), L0_ffn_W1, L0_ffn_b1, L0_ffn_W2, L0_ffn_b2), axis=-1)
    x = x + _layernorm(_L1_attn_ref(_layernorm(x, axis=-1), L1_attn_Wq, L1_attn_Wk, L1_attn_Wv, L1_attn_Wo, L1_attn_Wg, L1_attn_Wog, L1_attn_Wd, L1_attn_bd, L1_attn_norm_w), axis=-1)
    x = x + _layernorm(_L1_ffn_ref(_layernorm(x, axis=-1), L1_ffn_gate_W, L1_ffn_W1, L1_ffn_b1, L1_ffn_W2, L1_ffn_b2, L1_ffn_Ws1, L1_ffn_bs1, L1_ffn_Ws2, L1_ffn_bs2, L1_ffn_route_scale), axis=-1)
    return x

_drawn_inputs = setup_inputs


def setup_inputs(seed=0):
    import zlib

    import numpy as np

    out = dict(_drawn_inputs(seed))
    spreads = {'L1_attn_bd': (-2.0, 0.2),
     'L1_attn_norm_w': (1.0, 0.2),
     'L1_ffn_b1': (0.0, 0.1),
     'L1_ffn_b2': (0.0, 0.1),
     'L1_ffn_bs1': (0.0, 0.1),
     'L1_ffn_bs2': (0.0, 0.1)}
    factors = {'L0_ffn_b1': 5.316, 'L0_ffn_b2': 200.0}
    for name, (base, spread) in spreads.items():
        noise = np.random.default_rng([zlib.crc32(name.encode()), seed]).standard_normal(out[name].shape)
        drawn = base * np.exp(spread * noise) if base else spread * noise
        out[name] = jnp.asarray(drawn.astype(out[name].dtype))
    for name, factor in factors.items():
        out[name] = (out[name] * factor).astype(out[name].dtype)
    return out
```

```python
from contextlib import ExitStack

import numpy as np
import concourse.bass as bass
from concourse import mybir

F32 = mybir.dt.float32
BF16 = mybir.dt.bfloat16
ALU = mybir.AluOpType
ACT = mybir.ActivationFunctionType
AX = mybir.AxisListType

P = 128
BATCH, SEQ, D = 4, 1024, 256
TOKENS = BATCH * SEQ
ST = 512
NT = ST // P
NST = TOKENS // ST
KD = D // P
LN_EPS = 1e-5

AH, AD = 16, 16
HG = 4
NG = AH // HG
NBG = BATCH * NG
KT = SEQ // P
QH = SEQ // ST
VW = 32
Q_PART = (0, 0, 0, 1, 1, 2)
K_PART = (0, 1, 2, 0, 1, 0)
STACK = len(Q_PART) * AD
ROWS = STACK + 3

FF = 4 * D
FT = FF // P

GH, GD = 16, 64
HID = GH * GD
J = HID // P
RMS_EPS = float(np.finfo(np.float32).eps)

NE, EH = 8, 128


class Steps:

    def __init__(self, per):
        self.per, self.base, self.k = per, 0, 0

    def start(self, i):
        self.base, self.k = i * self.per, 0

    def inc(self):
        self.k += 1
        return 1

    def now(self):
        return self.base + self.k

    def end(self):
        assert self.k == self.per, (self.k, self.per)


def over_supertiles(eng, body):
    body(0, 0, False)
    body(1, 1, False)
    with eng.Fori(1, NST // 2 - 1) as k:
        body(2 * k, 0, False)
        body(2 * k + 1, 1, False)
    body(NST - 2, 0, False)
    body(NST - 1, 1, True)


def first(i, n):
    return isinstance(i, int) and i < n


def wait_past(eng, sem, value):
    if not isinstance(value, int) or value > 0:
        eng.wait_ge(sem, value)


def tokens(x):
    return x.rearrange("(i n p) c -> i p n c", p=P, n=NT)


def row(x):
    return x.rearrange("(a c) -> a c", a=1).to_broadcast([P, x.shape[0]])



LN = 2 * NT + 2


def normalize_tiles(nc, dve, x, xn, st, mv, rs, stats, s, rs_ready, rs_count, xn_ready):
    for n in range(NT):
        nc.vector.bn_stats(st[:, n, :], x[:, n, :]).then_inc(stats, s.inc())
    dve.wait_ge(stats, s.now())
    nc.vector.memset(rs[:, 0, :], LN_EPS).then_inc(stats, s.inc())
    for n in range(NT):
        nc.vector.bn_aggr(mv[:, n, :], st[:, n, :]).then_inc(stats, s.inc())
    dve.wait_ge(stats, s.now())
    nc.vector.tensor_tensor(rs[:, 0, :], mv[:, :, 1], rs[:, 0, :], ALU.add).then_inc(stats, s.inc())
    dve.wait_ge(rs_ready, rs_count)
    for n in range(NT):
        nc.vector.tensor_scalar(xn[:, n, :], x[:, n, :], mv[:, n, 0:1], rs[:, 1, n:n + 1],
                                ALU.subtract, ALU.mult).then_inc(xn_ready, 1)


def inverse_root(nc, pool, rs, half, stats, count, rs_ready):
    pool.wait_ge(stats, count)
    nc.gpsimd.tensor_tensor(rs[:, 1, :], rs[:, 0, :], half[:, 0:rs.shape[2]], ALU.pow).then_inc(rs_ready, 1)


def minus_half(nc, pool, half, half_set):
    nc.gpsimd.memset(half[:, :], -0.5).then_inc(half_set, 1)
    pool.wait_ge(half_set, 1)


def turn(nc, src, ps, ident, k):
    for n in range(NT):
        last = nc.tensor.transpose(ps[:, n * P:(n + 1) * P], src[:, n, k * P:(k + 1) * P], ident[:, :])
    return last


class Place:

    def __init__(self, nc, ctx, name):
        self.nc, self.ctx, self.name, self.taken = nc, ctx, name, []
        ctx.callback(self.clear)

    def clear(self):
        self.nc.clear_and_free_semaphores(self.taken)
        self.nc.all_engine_barrier()

    def sb(self, name, shape, dt=F32):
        return self.ctx.enter_context(self.nc.sbuf_tensor(f"{self.name}_sb_{name}", shape, dt))

    def ps(self, name, shape, dt=F32):
        return self.ctx.enter_context(self.nc.psum_tensor(f"{self.name}_ps_{name}", shape, dt))

    def sem(self, name):
        self.taken.append(self.nc.alloc_semaphore(f"{self.name}_{name}"))
        return self.taken[-1]

    def sems(self, name, n):
        return [self.sem(f"{name}{k}") for k in range(n)]


def phase_qkv(nc, x, w_t, bias, bias_cols, ident_d, parts, v_aug):
    with ExitStack() as ctx:
        m = Place(nc, ctx, "qkv")
        w = m.sb("w", [P, KD, 3 * D])
        ident = m.sb("ident", [P, P])
        b_in = m.sb("b_in", [P, 2 * KD])
        b_qk = m.sb("b_qk", [P, 2 * KD])
        b_v = m.sb("b_v", [P, D])
        xin = m.sb("xin", [P, 2, NT, D])
        xn = m.sb("xn", [P, NT, D])
        xT = m.sb("xT", [P, 2, KD, ST])
        st, mv, rs = m.sb("st", [P, NT, 6]), m.sb("mv", [P, NT, 2]), m.sb("rs", [P, 2, NT])
        half, half_set = m.sb("half", [P, NT]), m.sem("half_set")
        val = m.sb("val", [P, 4, ST])
        rest = m.sb("rest", [P, 4, ST])
        part = m.sb("part", [P, 4, 3, ST], BF16)
        va = m.sb("va", [P, 2, NT, AH, VW])
        psT = m.ps("psT", [P, KD, ST])
        psQ = m.ps("psQ", [P, 4, ST])
        psV = m.ps("psV", [P, NT, D])
        w_in, x_in = m.sem("w_in"), m.sems("x_in", 2)
        ln_step, xn_ready, turned, xT_ready = m.sem("ln_step"), m.sem("xn_ready"), m.sem("turned"), m.sem("xT_ready")
        rs_ready, bias_ready, va_ready0 = m.sem("rs_ready"), m.sem("bias_ready"), m.sem("va_const")
        qk_done, v_done, v_taken = m.sem("qk_done"), m.sem("v_done"), m.sem("v_taken")
        val_ready, mid_ready, rest_ready, lo_ready = (m.sem(s) for s in ("val_ready", "mid_ready", "rest_ready", "lo_ready"))
        part_out, v_out = m.sems("part_out", 4), m.sems("v_out", 2)
        xv = tokens(x)
        block = ctx.enter_context(nc.Block())

        @block.sync
        def _(sp):
            sp.dma_start(xin[:, 0, :, :], xv[0]).then_inc(x_in[0], 16)
            sp.dma_start(ident[:, :], ident_d).then_inc(w_in, 16)
            sp.dma_start(w[:, :, :], w_t.rearrange("(k p) o -> p k o", p=P)).then_inc(w_in, 16)
            sp.dma_start(b_in[:, :], bias_cols[:, 0:2 * KD]).then_inc(w_in, 16)
            sp.dma_start(b_v[:, :], row(bias[2 * D:3 * D])).then_inc(w_in, 16)

            def body(i, u, last):
                if not last:
                    if not first(i, 1):
                        sp.wait_ge(xn_ready, NT * i)
                    sp.dma_start(xin[:, 1 - u, :, :], xv[i + 1]).then_inc(x_in[1 - u], 16)
                for mt in range(4):
                    sp.wait_ge(lo_ready, 4 * i + mt + 1)
                    for g in range(2):
                        sp.dma_start(parts[mt // 2, i, 2 * (mt % 2) + g].rearrange("a c t -> c a t"),
                                     part[64 * g:64 * g + 64, mt, :, :]).then_inc(part_out[mt], 16)
                sp.wait_ge(v_taken, NT * (i + 1))
                for n in range(NT):
                    sp.dma_start(v_aug[i, n].rearrange("g p c -> p g c"),
                                 va[:, u, n, :, :].rearrange("p (g h) c -> p g (h c)", g=NG)).then_inc(v_out[u], 16)

            over_supertiles(sp, body)
            for s in part_out:
                sp.wait_ge(s, 32 * NST)
            for s in v_out:
                sp.wait_ge(s, 16 * NT * NST // 2)

        @block.vector
        def _(dve):
            s = Steps(LN)
            for u in range(2):
                nc.vector.memset(va[:, u, :, :, AD:AD + 1], 1.0).then_inc(va_ready0, 1)
                nc.vector.memset(va[:, u, :, :, AD + 1:VW], 0.0).then_inc(va_ready0, 1)
            dve.wait_ge(w_in, 64)
            nc.vector.tensor_scalar(b_qk[:, 0:KD], b_in[:, 0:KD], AD ** -0.5, None, ALU.mult).then_inc(bias_ready, 1)
            nc.vector.tensor_copy(b_qk[:, KD:2 * KD], b_in[:, KD:2 * KD]).then_inc(bias_ready, 1)
            dve.wait_ge(va_ready0, 4)

            def pre(i, u):
                s.start(i)
                dve.wait_ge(x_in[u], 8 * (i - u) + 16)
                if not first(i, 1):
                    dve.wait_ge(turned, KD * i)
                normalize_tiles(nc, dve, xin[:, u, :, :], xn, st, mv, rs, ln_step, s, rs_ready, i + 1, xn_ready)
                s.end()

            pre(0, 0)

            def body(i, u, last):
                if not last:
                    pre(i + 1, 1 - u)
                for mt in range(4):
                    dve.wait_ge(val_ready, 2 * (4 * i + mt) + 2)
                    if not first(i, 1):
                        dve.wait_ge(lo_ready, 4 * (i - 1) + mt + 1)
                    nc.vector.tensor_tensor(rest[:, mt, :], val[:, mt, :], part[:, mt, 0, :],
                                            ALU.subtract).then_inc(rest_ready, 1)
                for n in range(NT):
                    dve.wait_ge(v_done, 2 * i + n // 2 + 1)
                    if n == 0 and not first(i, 2):
                        dve.wait_ge(v_out[u], 8 * NT * (i - u))
                    nc.vector.tensor_tensor(va[:, u, n, :, 0:AD],
                                            psV[:, n, :].rearrange("p (h d) -> p h d", d=AD),
                                            b_v[:, :].rearrange("p (h d) -> p h d", d=AD),
                                            ALU.add).then_inc(v_taken, 1)

            over_supertiles(dve, body)

        @block.tensor
        def _(pe):
            pe.wait_ge(w_in, 64)

            def turn_in(i):
                pe.wait_ge(xn_ready, NT * (i + 1))
                if not first(i, 1):
                    pe.wait_ge(xT_ready, KD * i)
                for k in range(KD):
                    turn(nc, xn, psT[:, k, :], ident, k).then_inc(turned, 1)

            turn_in(0)

            def body(i, u, last):
                pe.wait_ge(xT_ready, KD * (i + 1))
                for mt in range(4):
                    if not first(i, 1):
                        pe.wait_ge(val_ready, 2 * (4 * (i - 1) + mt) + 2)
                    for k in range(KD):
                        mm = pe.matmul(psQ[:, mt, :], w[:, k, mt * P:(mt + 1) * P], xT[:, u, k, :],
                                       start=(k == 0), stop=(k == KD - 1))
                    mm.then_inc(qk_done, 1)
                if not last:
                    turn_in(i + 1)
                for n in range(NT):
                    if n % 2 == 0 and not first(i, 1):
                        pe.wait_ge(v_taken, NT * (i - 1) + n + 2)
                    for k in range(KD):
                        mm = pe.matmul(psV[:, n, :], xT[:, u, k, n * P:(n + 1) * P], w[:, k, 2 * D:3 * D],
                                       start=(k == 0), stop=(k == KD - 1))
                    if n % 2:
                        mm.then_inc(v_done, 1)

            over_supertiles(pe, body)

        @block.scalar
        def _(act):
            def take_turned(i, u):
                for k in range(KD):
                    act.wait_ge(turned, KD * i + k + 1)
                    nc.scalar.copy(xT[:, u, k, :], psT[:, k, :]).then_inc(xT_ready, 1)

            take_turned(0, 0)
            act.wait_ge(bias_ready, 2)

            def body(i, u, last):
                for mt in range(4):
                    act.wait_ge(qk_done, 4 * i + mt + 1)
                    if not first(i, 1):
                        act.wait_ge(part_out[mt], 32 * i)
                    scale = AD ** -0.5 if mt < KD else 1.0
                    nc.scalar.activation(val[:, mt, :], psQ[:, mt, :], ACT.Identity, bias=b_qk[:, mt:mt + 1],
                                         scale=scale).then_inc(val_ready, 1)
                    nc.scalar.activation(part[:, mt, 0, :], psQ[:, mt, :], ACT.Identity,
                                         bias=b_qk[:, mt:mt + 1], scale=scale).then_inc(val_ready, 1)
                    if mt:
                        act.wait_ge(rest_ready, 4 * i + mt)
                        nc.scalar.copy(part[:, mt - 1, 1, :], rest[:, mt - 1, :]).then_inc(mid_ready, 1)
                act.wait_ge(rest_ready, 4 * i + 4)
                nc.scalar.copy(part[:, 3, 1, :], rest[:, 3, :]).then_inc(mid_ready, 1)
                if not last:
                    take_turned(i + 1, 1 - u)

            over_supertiles(act, body)

        @block.gpsimd
        def _(pool):
            minus_half(nc, pool, half, half_set)
            inverse_root(nc, pool, rs, half, ln_step, LN, rs_ready)

            def body(i, u, last):
                if not last:
                    inverse_root(nc, pool, rs, half, ln_step, LN * (i + 2), rs_ready)
                for mt in range(4):
                    pool.wait_ge(mid_ready, 4 * i + mt + 1)
                    nc.gpsimd.tensor_tensor(part[:, mt, 2, :], rest[:, mt, :], part[:, mt, 1, :],
                                            ALU.subtract).then_inc(lo_ready, 1)

            over_supertiles(pool, body)


def phase_attention(nc, parts, v_aug, ident_d, att):
    with ExitStack() as ctx:
        m = Place(nc, ctx, "att")
        q = m.sb("q", [P, NG, QH, HG, ST], BF16)
        k = m.sb("k", [P, NG, HG, SEQ], BF16)
        v = m.sb("v", [P, NG, KT, HG * VW])
        ident, ident_b = m.sb("ident", [P, P]), m.sb("ident_b", [P, P], BF16)
        pt = m.sb("pt", [P, 2, HG, ST])
        mx = m.sb("mx", [P, HG, NT])
        mrest = m.sb("mrest", [P, HG * NT])
        mparts = m.sb("mparts", [P, 3, 32], BF16)
        mrow = m.sb("mrow", [3 * 32, P], BF16)
        osb = m.sb("osb", [P, ST])
        rden = m.sb("rden", [P, NT, HG])
        o = m.sb("o", [P, NT, HG, AD])
        psM = m.ps("psM", [P, 2, SEQ])
        psS = m.ps("psS", [P, 2, ST])
        psO = m.ps("psO", [P, ST])
        psX = m.ps("psX", [P, NT, P])
        psX_rows = psX[:, 0, :].bitcast(BF16)
        psX_heads = psX[:, :, :].rearrange("p n (j c) -> p n j c", c=VW)
        ident_in, ident_ready, ones_set = m.sem("ident_in"), m.sem("ident_ready"), m.sem("ones_set")
        stack_in = m.sems("stack_in", NG)
        maxima_done, maxima_free = m.sem("maxima_done"), m.sem("maxima_free")
        scores_done, exp_done = m.sem("scores_done"), m.sem("exp_done")
        pv_done = m.sem("pv_done")
        split, rows_turned, rows_ready, rows_in = (m.sem(s) for s in ("split", "rows_turned", "rows_ready", "rows_in"))
        osb_ready, o_turned, rden_ready, o_ready, o_out = (
            m.sem(s) for s in ("osb_ready", "o_turned", "rden_ready", "o_ready", "o_out"))
        att_v = tokens(att)
        CREDIT = 2
        TILES = HG * NT
        LOADS = 16 * (2 * QH * len(Q_PART) + QH)
        block = ctx.enter_context(nc.Block())

        def over_pairs(eng, body):
            for g in range(NG):
                body(0, g, False)
            with eng.Fori(1, BATCH - 1) as b:
                for g in range(NG):
                    body(b, g, False)
            for g in range(NG):
                body(BATCH - 1, g, g == NG - 1)

        def after(b, g):
            return (b, g + 1) if g < NG - 1 else (b + 1, 0)

        @block.sync
        def _(sp):
            sp.dma_start(ident[:, :], ident_d).then_inc(ident_in, 16)

            def load(b, g):
                for slot in range(len(Q_PART)):
                    rows = slice(AD * slot, AD * (slot + 1))
                    for s in range(QH):
                        for t, dst, which in ((0, q[rows, g, s, :, :], Q_PART),
                                              (1, k[rows, g, :, s * ST:(s + 1) * ST], K_PART)):
                            sp.dma_start(dst, parts[t, 2 * b + s, g, which[slot]].rearrange("(h c) t -> c h t", c=AD)
                                         ).then_inc(stack_in[g], 16)
                for s in range(QH):
                    sp.dma_start(v[:, g, s * NT:(s + 1) * NT, :],
                                 v_aug[2 * b + s, :, g].rearrange("n p c -> p n c")).then_inc(stack_in[g], 16)

            def rows(b, g, qh):
                u = 2 * (NG * b + g) + qh
                sp.wait_ge(rows_ready, u + 1)
                for a in range(3):
                    sp.dma_start(q[STACK + a:STACK + a + 1, g, qh, :, :].rearrange("p j t -> p (j t)"),
                                 mrow[32 * a:32 * a + TILES, :]).then_inc(rows_in, 16)

            def out(b, g, qh):
                sp.wait_ge(o_ready, 2 * (NG * b + g) + qh + 1)
                sp.dma_start(att_v[2 * b + qh][:, :, HG * AD * g:HG * AD * (g + 1)],
                             o[:, :, :, :].rearrange("p n j c -> p n (j c)")).then_inc(o_out, 16)

            for g in range(NG - 1):
                load(0, g)
            rows(0, 0, 0)

            def body(b, g, last):
                rows(b, g, 1)
                nb, ng = (b, NG - 1) if g == 0 else (b + 1, g - 1)
                if not (isinstance(nb, int) and nb >= BATCH):
                    sp.wait_ge(pv_done, CREDIT + 2 * KT * (NG * b + g))
                    load(nb, ng)
                if not last:
                    rows(*after(b, g), 0)
                out(b, g, 0)
                out(b, g, 1)

            over_pairs(sp, body)
            sp.wait_ge(o_out, 16 * 2 * NBG)

        @block.vector
        def _(dve):
            nc.vector.memset(k[STACK:P, :, :, :], 1.0).then_inc(ones_set, 1)
            nc.vector.memset(mparts[:, :, :], 0.0).then_inc(maxima_free, CREDIT)
            nc.vector.memset(mrest[:, :], 0.0).then_inc(exp_done, CREDIT)
            nc.vector.memset(rden[:, :, :], 0.0).then_inc(pv_done, CREDIT)
            dve.wait_ge(ident_in, 16)
            nc.vector.tensor_copy(ident_b[:, :], ident[:, :]).then_inc(ident_ready, 1)

            def maxima(b, g, qh, tiles):
                u = 2 * (NG * b + g) + qh
                for t in tiles:
                    dve.wait_ge(maxima_done, TILES * u + t + 1)
                    nc.vector.tensor_reduce(mx[:, t // NT, t % NT:t % NT + 1], psM[:, t % 2, :], AX.X,
                                            ALU.max).then_inc(maxima_free, 1)

            def split_maxima(b, g, qh):
                u = 2 * (NG * b + g) + qh
                x = mx[:, :, :].rearrange("p j n -> p (j n)")
                dve.wait_ge(maxima_free, CREDIT + TILES * (u + 1))
                wait_past(dve, rows_turned, u)
                nc.vector.tensor_scalar(mparts[:, 0, 0:TILES], x, -1.0, None, ALU.mult).then_inc(split, 1)
                dve.wait_ge(split, 4 * u + 1)
                nc.vector.scalar_tensor_tensor(mrest[:, :], x, -1.0, mparts[:, 0, 0:TILES], ALU.mult,
                                               ALU.subtract).then_inc(split, 1)
                dve.wait_ge(split, 4 * u + 2)
                nc.vector.tensor_copy(mparts[:, 1, 0:TILES], mrest[:, :]).then_inc(split, 1)
                dve.wait_ge(split, 4 * u + 3)
                nc.vector.tensor_tensor(mparts[:, 2, 0:TILES], mrest[:, :], mparts[:, 1, 0:TILES],
                                        ALU.subtract).then_inc(split, 1)

            def normalize(u):
                dve.wait_ge(o_turned, u + 1)
                nc.vector.reciprocal(rden[:, :, :], psX_heads[:, :, :, AD]).then_inc(rden_ready, 1)
                dve.wait_ge(rden_ready, u + 1)
                wait_past(dve, o_out, 16 * u)
                nc.vector.tensor_tensor(
                    o[:, :, :, :], psX_heads[:, :, :, 0:AD],
                    rden[:, :, :].rearrange("p n (j c) -> p n j c", c=1).to_broadcast([P, NT, HG, AD]),
                    ALU.mult).then_inc(o_ready, 1)

            for qh in range(QH):
                maxima(0, 0, qh, range(TILES))
                split_maxima(0, 0, qh)

            def body(b, g, last):
                u = 2 * (NG * b + g)
                nb, ng = after(b, g)
                if not last:
                    maxima(nb, ng, 0, range(TILES))
                    split_maxima(nb, ng, 0)
                    maxima(nb, ng, 1, range(TILES // 2))
                normalize(u)
                if not last:
                    maxima(nb, ng, 1, range(TILES // 2, TILES))
                    split_maxima(nb, ng, 1)
                normalize(u + 1)

            over_pairs(dve, body)

        @block.tensor
        def _(pe):
            def maxima_tile(b, g, qh, t):
                u = 2 * (NG * b + g) + qh
                j, n = t // NT, t % NT
                queries = q[0:STACK, g, qh, j, n * P:(n + 1) * P]

                def half(c):
                    if c == 0:
                        pe.wait_ge(maxima_free, TILES * u + t + 1)
                    mm = pe.matmul(psM[:, t % 2, c * ST:(c + 1) * ST], queries,
                                   k[0:STACK, g, j, c * ST:(c + 1) * ST], start=True, stop=True)
                    if c == 1:
                        mm.then_inc(maxima_done, 1)
                return half

            def scores(g, qh, u, s, j):
                t = 4 * (KT * u + s) + j
                pe.wait_ge(exp_done, t + 1)
                pe.matmul(psS[:, j % 2, :], k[0:ROWS, g, j, s * P:(s + 1) * P],
                          q[0:ROWS, g, qh, j, :], start=True, stop=True).then_inc(scores_done, 1)

            def values(g, u, s):
                pe.wait_ge(exp_done, CREDIT + 4 * (KT * u + s) + 4)
                if s == 0:
                    wait_past(pe, osb_ready, u)
                for j in range(HG):
                    mm = pe.matmul(psO[VW * j:VW * (j + 1), :], v[:, g, s, VW * j:VW * (j + 1)],
                                   pt[:, s % 2, j, :], start=(s == 0), stop=(s == KT - 1),
                                   tile_position=(0, VW * j))
                mm.then_inc(pv_done, 1)

            def turn_rows(u):
                pe.wait_ge(split, 4 * (u + 1))
                pe.transpose(psX_rows[0:3 * 32, 0:P], mparts[:, :, :].rearrange("p a t -> p (a t)"),
                             ident_b[:, :]).then_inc(rows_turned, 1)

            def turn_out(u):
                pe.wait_ge(osb_ready, u + 1)
                for n in range(NT):
                    mm = pe.transpose(psX[:, n, :], osb[:, n * P:(n + 1) * P], ident[:, :])
                mm.then_inc(o_turned, 1)

            pe.wait_ge(ident_ready, 1)
            pe.wait_ge(ones_set, 1)
            pe.wait_ge(stack_in[0], LOADS)
            for qh in range(QH):
                for t in range(TILES):
                    half = maxima_tile(0, 0, qh, t)
                    half(0)
                    half(1)
            turn_rows(0)

            def body(b, g, last):
                p = NG * b + g
                nb, ng = after(b, g)
                if not last:
                    pe.wait_ge(stack_in[ng], LOADS * (nb + 1))
                for qh in range(QH):
                    u = 2 * p + qh
                    pe.wait_ge(rows_in, 16 * 3 * (u + 1))
                    for s in range(KT):
                        if s == 2 and not (last and qh == 1):
                            pe.wait_ge(rows_ready, u + 1)
                            wait_past(pe, o_ready, 2 * p)
                            turn_rows(u + 1)
                        if s == 4 and qh == 1:
                            pe.wait_ge(rows_ready, u + 1 if last else u + 2)
                            turn_out(u - 1)
                        ms = []
                        if not last:
                            for t in (2 * s, 2 * s + 1):
                                half = maxima_tile(nb, ng, qh, t)
                                ms += [(half, 0), (half, 1)]
                        if s < KT - 1:
                            for j in range(HG):
                                scores(g, qh, u, s, j)
                                if ms:
                                    ms[j][0](ms[j][1])
                            if s:
                                values(g, u, s - 1)
                        else:
                            scores(g, qh, u, s, 0)
                            scores(g, qh, u, s, 1)
                            values(g, u, s - 1)
                            scores(g, qh, u, s, 2)
                            scores(g, qh, u, s, 3)
                            for half, c in ms:
                                half(c)
                            values(g, u, s)
                pe.wait_ge(o_ready, 2 * p + 1)
                turn_out(2 * p + 1)

            over_pairs(pe, body)

        @block.scalar
        def _(act):
            def copy_rows(u):
                act.wait_ge(rows_turned, u + 1)
                wait_past(act, rows_in, 16 * 3 * u)
                nc.scalar.copy(mrow[:, :], psX_rows[0:3 * 32, 0:P]).then_inc(rows_ready, 1)

            copy_rows(0)

            def body(b, g, last):
                for qh in range(QH):
                    u = 2 * (NG * b + g) + qh
                    for s in range(KT):
                        act.wait_ge(pv_done, KT * u + s + 1)
                        for j in range(HG):
                            act.wait_ge(scores_done, 4 * (KT * u + s) + j + 1)
                            nc.scalar.activation(pt[:, s % 2, j, :], psS[:, j % 2, :], ACT.Exp).then_inc(exp_done, 1)
                        if s == 3 and not (last and qh == 1):
                            copy_rows(u + 1)
                    act.wait_ge(pv_done, CREDIT + KT * (u + 1))
                    wait_past(act, o_turned, u)
                    nc.scalar.copy(osb[:, :], psO[:, :]).then_inc(osb_ready, 1)

            over_pairs(act, body)


def phase_project(nc, x, att, w_t, bias, ident_d, x_out):
    with ExitStack() as ctx:
        m = Place(nc, ctx, "proj")
        w = m.sb("w", [P, KD, D])
        ident = m.sb("ident", [P, P])
        b_out = m.sb("b_out", [P, D])
        xin, ain = m.sb("xin", [P, 2, NT, D]), m.sb("ain", [P, 2, NT, D])
        aT = m.sb("aT", [P, 2, KD, ST])
        st, mv, rs = m.sb("st", [P, NT, 6]), m.sb("mv", [P, NT, 2]), m.sb("rs", [P, 2, NT])
        half, half_set = m.sb("half", [P, NT]), m.sem("half_set")
        y, yn = m.sb("y", [P, NT, D]), m.sb("yn", [P, NT, D])
        xo = m.sb("xo", [P, 2, NT, D])
        psT = m.ps("psT", [P, KD, ST])
        psY = m.ps("psY", [P, 2, NT, D])
        w_in, x_in, a_in = m.sem("w_in"), m.sems("x_in", 2), m.sems("a_in", 2)
        turned, aT_ready, y_done, y_taken = (m.sem(s) for s in ("turned", "aT_ready", "y_done", "y_taken"))
        ln_step, rs_ready, yn_ready, xo_ready, x_outd = m.sem("ln_step"), m.sem("rs_ready"), m.sem("yn_ready"), m.sem("xo_ready"), m.sems("x_out", 2)
        xv, av, ov = tokens(x), tokens(att), tokens(x_out)
        block = ctx.enter_context(nc.Block())

        @block.sync
        def _(sp):
            sp.dma_start(ain[:, 0, :, :], av[0]).then_inc(a_in[0], 16)
            sp.dma_start(ident[:, :], ident_d).then_inc(w_in, 16)
            sp.dma_start(w[:, :, :], w_t.rearrange("(k p) o -> p k o", p=P)).then_inc(w_in, 16)
            sp.dma_start(b_out[:, :], row(bias)).then_inc(w_in, 16)
            sp.dma_start(xin[:, 0, :, :], xv[0]).then_inc(x_in[0], 16)

            def body(i, u, last):
                if not last:
                    if not first(i, 1):
                        sp.wait_ge(xo_ready, i)
                    sp.dma_start(ain[:, 1 - u, :, :], av[i + 1]).then_inc(a_in[1 - u], 16)
                    sp.dma_start(xin[:, 1 - u, :, :], xv[i + 1]).then_inc(x_in[1 - u], 16)
                sp.wait_ge(xo_ready, i + 1)
                sp.dma_start(ov[i], xo[:, u, :, :]).then_inc(x_outd[u], 16)

            over_supertiles(sp, body)
            for s in x_outd:
                sp.wait_ge(s, 16 * NST // 2)

        @block.tensor
        def _(pe):
            pe.wait_ge(w_in, 48)

            def turn_in(i, u):
                pe.wait_ge(a_in[u], 8 * (i - u) + 16)
                if not first(i, 1):
                    pe.wait_ge(aT_ready, KD * i)
                for k in range(KD):
                    turn(nc, ain[:, u, :, :], psT[:, k, :], ident, k).then_inc(turned, 1)

            turn_in(0, 0)

            def body(i, u, last):
                if not last:
                    turn_in(i + 1, 1 - u)
                pe.wait_ge(aT_ready, KD * (i + 1))
                if not first(i, 2):
                    pe.wait_ge(y_taken, NT * (i - 1))
                for n in range(NT):
                    for k in range(KD):
                        mm = pe.matmul(psY[:, u, n, :], aT[:, u, k, n * P:(n + 1) * P], w[:, k, :],
                                       start=(k == 0), stop=(k == KD - 1))
                mm.then_inc(y_done, 1)

            over_supertiles(pe, body)

        @block.scalar
        def _(act):
            def body(i, u, last):
                for k in range(KD):
                    act.wait_ge(turned, KD * i + k + 1)
                    if k == 0 and not first(i, 2):
                        act.wait_ge(y_done, i - 1)
                    nc.scalar.copy(aT[:, u, k, :], psT[:, k, :]).then_inc(aT_ready, 1)

            over_supertiles(act, body)

        @block.vector
        def _(dve):
            s = Steps(LN)
            dve.wait_ge(w_in, 48)

            def body(i, u, last):
                s.start(i)
                dve.wait_ge(y_done, i + 1)
                if not first(i, 1):
                    dve.wait_ge(yn_ready, NT * i)
                for n in range(NT):
                    nc.vector.tensor_tensor(y[:, n, :], psY[:, u, n, :], b_out[:, :], ALU.add).then_inc(y_taken, 1)
                dve.wait_ge(y_taken, NT * (i + 1))
                if not first(i, 1):
                    dve.wait_ge(xo_ready, i)
                normalize_tiles(nc, dve, y, yn, st, mv, rs, ln_step, s, rs_ready, i + 1, yn_ready)
                s.end()

            over_supertiles(dve, body)

        @block.gpsimd
        def _(pool):
            minus_half(nc, pool, half, half_set)

            def body(i, u, last):
                inverse_root(nc, pool, rs, half, ln_step, LN * (i + 1), rs_ready)
                pool.wait_ge(yn_ready, NT * (i + 1))
                pool.wait_ge(x_in[u], 8 * (i - u) + 16)
                if not first(i, 2):
                    pool.wait_ge(x_outd[u], 8 * (i - u))
                nc.gpsimd.tensor_tensor(xo[:, u, :, :], xin[:, u, :, :], yn[:, :, :], ALU.add).then_inc(xo_ready, 1)

            over_supertiles(pool, body)


def phase_ternary_ffn(nc, x, w1_t, b1_cols, w2_t, b2, ident_d, x_out):
    with ExitStack() as ctx:
        m = Place(nc, ctx, "ffn")
        w1, w2 = m.sb("w1", [P, KD, FF]), m.sb("w2", [P, FT, D])
        wx = m.sb("wx", [P, FF * KD])
        part_sum, total = m.sb("part_sum", [P, 2, 65]), m.sb("total", [P, 2, 2])
        ones, ident = m.sb("ones", [P, P]), m.sb("ident", [P, P])
        b_h, b_y = m.sb("b_h", [P, FT]), m.sb("b_y", [P, D])
        half, half_set = m.sb("half", [P, NT]), m.sem("half_set")
        xin = m.sb("xin", [P, 2, NT, D])
        xn = m.sb("xn", [P, NT, D])
        xT = m.sb("xT", [P, 2, KD, ST])
        hT = m.sb("hT", [P, FT, ST])
        st, mv, rs = m.sb("st", [P, NT, 6]), m.sb("mv", [P, NT, 2]), m.sb("rs", [P, 2, NT])
        st2, mv2, rs2 = m.sb("st2", [P, NT, 6]), m.sb("mv2", [P, NT, 2]), m.sb("rs2", [P, 2, NT])
        y, yn, xo = m.sb("y", [P, NT, D]), m.sb("yn", [P, NT, D]), m.sb("xo", [P, 2, NT, D])
        psT = m.ps("psT", [P, KD, ST])
        psH = m.ps("psH", [P, 4, ST])
        psY = m.ps("psY", [P, NT, D])
        const_in, w_in, x_in = m.sem("const_in"), m.sems("w_in", 2), m.sems("x_in", 2)
        ones_set, prep, summed, w_ready = m.sem("ones_set"), m.sem("prep"), m.sem("summed"), m.sem("w_ready")
        abs_ready = m.sem("abs_ready")
        stats, rs_ready, xn_ready = m.sem("stats"), m.sem("rs_ready"), m.sem("xn_ready")
        stats2, rs2_ready, yn_ready = m.sem("stats2"), m.sem("rs2_ready"), m.sem("yn_ready")
        turned, xT_ready = m.sem("turned"), m.sem("xT_ready")
        h_done, h_ready, y_done, y_taken = m.sem("h_done"), m.sem("h_ready"), m.sem("y_done"), m.sem("y_taken")
        xo_ready, x_outd = m.sem("xo_ready"), m.sems("x_out", 2)
        xv, ov = tokens(x), tokens(x_out)
        block = ctx.enter_context(nc.Block())

        @block.sync
        def _(sp):
            sp.dma_start(w1[:, :, :], w1_t.rearrange("(k p) o -> p k o", p=P)).then_inc(w_in[0], 16)
            sp.dma_start(xin[:, 0, :, :], xv[0]).then_inc(x_in[0], 16)
            sp.dma_start(ident[:, :], ident_d).then_inc(const_in, 16)
            sp.dma_start(w2[:, :, :], w2_t.rearrange("(k p) o -> p k o", p=P)).then_inc(w_in[1], 16)
            sp.dma_start(b_h[:, :], b1_cols).then_inc(const_in, 16)
            sp.dma_start(b_y[:, :], row(b2)).then_inc(const_in, 16)

            def body(i, u, last):
                if not last:
                    if not first(i, 1):
                        sp.wait_ge(xo_ready, i)
                    sp.dma_start(xin[:, 1 - u, :, :], xv[i + 1]).then_inc(x_in[1 - u], 16)
                sp.wait_ge(xo_ready, i + 1)
                sp.dma_start(ov[i], xo[:, u, :, :]).then_inc(x_outd[u], 16)

            over_supertiles(sp, body)
            for s in x_outd:
                sp.wait_ge(s, 16 * NST // 2)

        @block.vector
        def _(dve):
            s, s2, t = Steps(LN), Steps(LN), Steps(0)
            nc.vector.memset(ones[:, :], 1.0).then_inc(ones_set, 1)

            def pre(i, u):
                s.start(i)
                dve.wait_ge(x_in[u], 8 * (i - u) + 16)
                if not first(i, 1):
                    dve.wait_ge(turned, KD * i)
                normalize_tiles(nc, dve, xin[:, u, :, :], xn, st, mv, rs, stats, s, rs_ready, i + 1, xn_ready)
                s.end()

            def ternary(n, w):
                dve.wait_ge(abs_ready, n + 1)
                nc.vector.tensor_reduce(part_sum[:, n, 0:64], wx[:, :].rearrange("p (a b) -> p a b", a=64), AX.X,
                                        ALU.add).then_inc(prep, t.inc())
                dve.wait_ge(prep, t.now())
                nc.vector.tensor_reduce(part_sum[:, n, 64:65], part_sum[:, n, 0:64], AX.X,
                                        ALU.add).then_inc(prep, t.inc())
                dve.wait_ge(summed, n + 1)
                nc.vector.tensor_scalar(total[:, n, 0:1], psY[:, 2 * n, 0:1], 1.0 / (FF * D), 1e-8, ALU.mult,
                                        ALU.max).then_inc(prep, t.inc())
                dve.wait_ge(prep, t.now())
                nc.vector.tensor_scalar(total[:, n, 0:1], total[:, n, 0:1], 0.5, None, ALU.mult).then_inc(prep, t.inc())
                dve.wait_ge(prep, t.now())
                nc.vector.tensor_scalar(total[:, n, 1:2], total[:, n, 0:1], -1.0, None, ALU.mult).then_inc(prep, t.inc())
                dve.wait_ge(prep, t.now())
                nc.vector.tensor_scalar(wx[:, :], w, total[:, n, 0:1], None, ALU.is_gt).then_inc(prep, t.inc())
                dve.wait_ge(prep, t.now())
                nc.vector.scalar_tensor_tensor(wx[:, :], w, total[:, n, 1:2], wx[:, :], ALU.is_lt,
                                               ALU.subtract).then_inc(prep, t.inc())
                dve.wait_ge(prep, t.now())
                nc.vector.scalar_tensor_tensor(wx[:, :], wx[:, :], -1.0, w, ALU.mult,
                                               ALU.subtract).then_inc(prep, t.inc())
                dve.wait_ge(prep, t.now())
                nc.vector.tensor_tensor(w, wx[:, :], w, ALU.add).then_inc(w_ready, 1)

            ternary(0, w1[:, :, :].rearrange("p k o -> p (k o)"))
            pre(0, 0)
            ternary(1, w2[:, :, :].rearrange("p k o -> p (k o)"))
            dve.wait_ge(const_in, 48)

            def body(i, u, last):
                if not last:
                    pre(i + 1, 1 - u)
                s2.start(i)
                if not first(i, 1):
                    dve.wait_ge(yn_ready, NT * i)
                for n in range(NT):
                    dve.wait_ge(y_done, 2 * i + n // 2 + 1)
                    nc.vector.tensor_tensor(y[:, n, :], psY[:, n, :], b_y[:, :], ALU.add).then_inc(y_taken, 1)
                dve.wait_ge(y_taken, NT * (i + 1))
                if not first(i, 1):
                    dve.wait_ge(xo_ready, i)
                normalize_tiles(nc, dve, y, yn, st2, mv2, rs2, stats2, s2, rs2_ready, i + 1, yn_ready)
                s2.end()

            over_supertiles(dve, body)

        @block.tensor
        def _(pe):
            def turn_in(i):
                pe.wait_ge(xn_ready, NT * (i + 1))
                if not first(i, 1):
                    pe.wait_ge(xT_ready, KD * i)
                for k in range(KD):
                    turn(nc, xn, psT[:, k, :], ident, k).then_inc(turned, 1)

            def sum_weights(n):
                pe.wait_ge(prep, 8 * n + 2)
                pe.matmul(psY[:, 2 * n, 0:1], ones[:, :], part_sum[:, n, 64:65], start=True,
                          stop=True).then_inc(summed, 1)

            pe.wait_ge(ones_set, 1)
            pe.wait_ge(const_in, 48)
            sum_weights(0)
            turn_in(0)
            sum_weights(1)
            pe.wait_ge(w_ready, 1)

            def body(i, u, last):
                pe.wait_ge(xT_ready, KD * (i + 1))
                for f in range(FT):
                    if not (first(i, 1) and f < 4):
                        pe.wait_ge(h_ready, FT * i + f - 3)
                    for k in range(KD):
                        mm = pe.matmul(psH[:, f % 4, :], w1[:, k, f * P:(f + 1) * P], xT[:, u, k, :],
                                       start=(k == 0), stop=(k == KD - 1))
                    mm.then_inc(h_done, 1)
                if not last:
                    turn_in(i + 1)
                if first(i, 1):
                    pe.wait_ge(w_ready, 2)
                for n in range(NT):
                    if n % 2 == 0 and not first(i, 1):
                        pe.wait_ge(y_taken, NT * (i - 1) + n + 2)
                    for f in range(FT):
                        if n == 0:
                            pe.wait_ge(h_ready, FT * i + f + 1)
                        mm = pe.matmul(psY[:, n, :], hT[:, f, n * P:(n + 1) * P], w2[:, f, :],
                                       start=(f == 0), stop=(f == FT - 1))
                    if n % 2:
                        mm.then_inc(y_done, 1)

            over_supertiles(pe, body)

        @block.scalar
        def _(act):
            for n, w in ((0, w1), (1, w2)):
                act.wait_ge(w_in[n], 16)
                if n:
                    act.wait_ge(w_ready, n)
                nc.scalar.activation(wx[:, :], w[:, :, :].rearrange("p k o -> p (k o)"), ACT.Abs).then_inc(abs_ready, 1)

            def take_turned(i, u):
                for k in range(KD):
                    act.wait_ge(turned, KD * i + k + 1)
                    nc.scalar.copy(xT[:, u, k, :], psT[:, k, :]).then_inc(xT_ready, 1)

            take_turned(0, 0)
            act.wait_ge(const_in, 48)

            def body(i, u, last):
                for f in range(FT):
                    act.wait_ge(h_done, FT * i + f + 1)
                    if f == 0 and not first(i, 1):
                        act.wait_ge(y_done, 2 * i)
                    nc.scalar.activation(hT[:, f, :], psH[:, f % 4, :], ACT.Gelu,
                                         bias=b_h[:, f:f + 1]).then_inc(h_ready, 1)
                if not last:
                    take_turned(i + 1, 1 - u)

            over_supertiles(act, body)

        @block.gpsimd
        def _(pool):
            minus_half(nc, pool, half, half_set)
            inverse_root(nc, pool, rs, half, stats, LN, rs_ready)

            def body(i, u, last):
                if not last:
                    inverse_root(nc, pool, rs, half, stats, LN * (i + 2), rs_ready)
                inverse_root(nc, pool, rs2, half, stats2, LN * (i + 1), rs2_ready)
                pool.wait_ge(yn_ready, NT * (i + 1))
                if not first(i, 2):
                    pool.wait_ge(x_outd[u], 8 * (i - u))
                nc.gpsimd.tensor_tensor(xo[:, u, :, :], xin[:, u, :, :], yn[:, :, :], ALU.add).then_inc(xo_ready, 1)

            over_supertiles(pool, body)


def phase_experts(nc, x, gate_w, w1, b1_cols, w2, b2, ws1, bs1_col, ws2, bs2, route_scale, ident_d, x_out):
    BIG = 3.0e38
    with ExitStack() as ctx:
        m = Place(nc, ctx, "moe")
        wg = m.sb("wg", [P, KD, NE])
        wa, wb = m.sb("wa", [P, KD, NE + 1, EH]), m.sb("wb", [P, NE + 1, D])
        b_h, b_e, b_s = m.sb("b_h", [P, NE + 1]), m.sb("b_e", [NE, D]), m.sb("b_s", [P, D])
        r_scale, order = m.sb("r_scale", [P, 1]), m.sb("order", [P, NT, NE])
        ident = m.sb("ident", [P, P])
        half, half_set = m.sb("half", [P, NT]), m.sem("half_set")
        xin = m.sb("xin", [P, 2, NT, D])
        xn = m.sb("xn", [P, NT, D])
        xT = m.sb("xT", [P, 2, KD, ST])
        hT = m.sb("hT", [P, NE + 1, ST])
        st, mv, rs = m.sb("st", [P, NT, 6]), m.sb("mv", [P, NT, 2]), m.sb("rs", [P, 2, NT])
        st2, mv2, rs2 = m.sb("st2", [P, NT, 6]), m.sb("mv2", [P, NT, 2]), m.sb("rs2", [P, 2, NT])
        y, yn, xo = m.sb("y", [P, NT, D]), m.sb("yn", [P, NT, D]), m.sb("xo", [P, 2, NT, D])
        sig, score, pick, sel1, sel2, gates = (m.sb(s, [P, NT, NE]) for s in ("sig", "score", "pick", "sel1", "sel2", "gates"))
        best1, best2, rank = (m.sb(s, [P, NT]) for s in ("best1", "best2", "rank"))
        gT = m.sb("gT", [NE, ST])
        psT = m.ps("psT", [P, ST])
        psH = m.ps("psH", [P, 2, ST])
        psG = m.ps("psG", [P, ST])
        psY = m.ps("psY", [P, 4, 2, D])
        const_in, w_in, x_in = m.sem("const_in"), m.sem("w_in"), m.sems("x_in", 2)
        stats, rs_ready, xn_ready = m.sem("stats"), m.sem("rs_ready"), m.sem("xn_ready")
        stats2, rs2_ready, yn_ready = m.sem("stats2"), m.sem("rs2_ready"), m.sem("yn_ready")
        turned, xT_ready = m.sem("turned"), m.sem("xT_ready")
        logits_done, sig_ready, route, gates_ready = m.sem("logits_done"), m.sem("sig_ready"), m.sem("route"), m.sem("gates_ready")
        g_turned, gT_ready, order_set = m.sem("g_turned"), m.sem("gT_ready"), m.sem("order_set")
        h_done, h_ready, y_done, y_added = m.sem("h_done"), m.sem("h_ready"), m.sem("y_done"), m.sem("y_added")
        xo_ready, x_outd = m.sem("xo_ready"), m.sems("x_out", 2)
        xv, ov = tokens(x), tokens(x_out)
        N_CONST, UNITS = 16 * 9, 1 + NE // 2
        block = ctx.enter_context(nc.Block())

        @block.sync
        def _(sp):
            sp.dma_start(xin[:, 0, :, :], xv[0]).then_inc(x_in[0], 16)
            sp.dma_start(ident[:, :], ident_d).then_inc(const_in, 16)
            sp.dma_start(wg[:, :, :], gate_w.rearrange("(k p) e -> p k e", p=P)).then_inc(const_in, 16)
            sp.dma_start(r_scale[:, :], route_scale.to_broadcast([P, 1])).then_inc(const_in, 16)
            for k in range(KD):
                sp.dma_start(wa[:, k, 0:NE, :], w1[:, k * P:(k + 1) * P, :].rearrange("e p h -> p e h")).then_inc(w_in, 16)
            sp.dma_start(wa[:, :, NE, :], ws1.rearrange("(k p) h -> p k h", p=P)).then_inc(w_in, 16)
            sp.dma_start(b_h[:, 0:NE], b1_cols).then_inc(const_in, 16)
            sp.dma_start(b_h[:, NE:NE + 1], bs1_col).then_inc(const_in, 16)
            sp.dma_start(wb[:, 0:NE, :], w2.rearrange("e h d -> h e d")).then_inc(const_in, 16)
            sp.dma_start(wb[:, NE, :], ws2).then_inc(const_in, 16)
            sp.dma_start(b_e[:, :], b2).then_inc(const_in, 16)
            sp.dma_start(b_s[:, :], row(bs2)).then_inc(const_in, 16)

            def body(i, u, last):
                if not last:
                    if not first(i, 1):
                        sp.wait_ge(xo_ready, i)
                    sp.dma_start(xin[:, 1 - u, :, :], xv[i + 1]).then_inc(x_in[1 - u], 16)
                sp.wait_ge(xo_ready, i + 1)
                sp.dma_start(ov[i], xo[:, u, :, :]).then_inc(x_outd[u], 16)

            over_supertiles(sp, body)
            for s in x_outd:
                sp.wait_ge(s, 16 * NST // 2)

        @block.vector
        def _(dve):
            ROUTE = 1 + 5 + 2 + 5 + 4
            s, s2, r = Steps(LN), Steps(LN), Steps(ROUTE)
            for e in range(NE):
                nc.vector.memset(order[:, :, e:e + 1], float(NE - e)).then_inc(order_set, 1)

            def pre(i, u):
                s.start(i)
                dve.wait_ge(x_in[u], 8 * (i - u) + 16)
                if not first(i, 1):
                    dve.wait_ge(turned, KD * i)
                normalize_tiles(nc, dve, xin[:, u, :, :], xn, st, mv, rs, stats, s, rs_ready, i + 1, xn_ready)
                s.end()

            def wide(a):
                return a[:, :].rearrange("p (n e) -> p n e", e=1).to_broadcast([P, NT, NE])

            def choose(best, sel):
                nc.vector.tensor_reduce(best[:, :], score[:, :, :], AX.X, ALU.max).then_inc(route, r.inc())
                dve.wait_ge(route, r.now())
                nc.vector.tensor_tensor(pick[:, :, :], score[:, :, :], wide(best), ALU.is_ge).then_inc(route, r.inc())
                dve.wait_ge(route, r.now())
                nc.vector.tensor_tensor(pick[:, :, :], pick[:, :, :], order[:, :, :], ALU.mult).then_inc(route, r.inc())
                dve.wait_ge(route, r.now())
                nc.vector.tensor_reduce(rank[:, :], pick[:, :, :], AX.X, ALU.max).then_inc(route, r.inc())
                dve.wait_ge(route, r.now())
                nc.vector.tensor_tensor(sel[:, :, :], pick[:, :, :], wide(rank), ALU.is_ge).then_inc(route, r.inc())
                dve.wait_ge(route, r.now())

            def route_tokens(i):
                r.start(i)
                dve.wait_ge(sig_ready, i + 1)
                if not first(i, 1):
                    dve.wait_ge(g_turned, i)
                    dve.wait_ge(y_added, NT * (NE + 1) * i)
                nc.vector.tensor_scalar(score[:, :, :], sig[:, :, :], r_scale[:, 0:1], None,
                                        ALU.mult).then_inc(route, r.inc())
                dve.wait_ge(route, r.now())
                choose(best1, sel1)
                nc.vector.tensor_tensor(gates[:, :, :], score[:, :, :], sel1[:, :, :], ALU.mult).then_inc(route, r.inc())
                dve.wait_ge(route, r.now())
                nc.vector.scalar_tensor_tensor(score[:, :, :], sel1[:, :, :], -BIG, score[:, :, :], ALU.mult,
                                               ALU.add).then_inc(route, r.inc())
                dve.wait_ge(route, r.now())
                choose(best2, sel2)
                nc.vector.tensor_tensor(sel2[:, :, :], score[:, :, :], sel2[:, :, :], ALU.mult).then_inc(route, r.inc())
                nc.vector.tensor_tensor(rank[:, :], best1[:, :], best2[:, :], ALU.add).then_inc(route, r.inc())
                dve.wait_ge(route, r.now())
                nc.vector.reciprocal(best1[:, :], rank[:, :]).then_inc(route, r.inc())
                nc.vector.tensor_tensor(gates[:, :, :], gates[:, :, :], sel2[:, :, :], ALU.add).then_inc(route, r.inc())
                dve.wait_ge(route, r.now())
                nc.vector.tensor_tensor(gates[:, :, :], gates[:, :, :], wide(best1), ALU.mult).then_inc(gates_ready, 1)
                r.end()

            pre(0, 0)
            dve.wait_ge(const_in, N_CONST)
            dve.wait_ge(order_set, NE)

            def body(i, u, last):
                route_tokens(i)
                if not last:
                    pre(i + 1, 1 - u)
                s2.start(i)
                if not first(i, 1):
                    dve.wait_ge(yn_ready, NT * i)
                dve.wait_ge(gates_ready, i + 1)
                added = NT * (NE + 1) * i
                for n in range(NT):
                    for c in range(UNITS):
                        dve.wait_ge(y_done, UNITS * (NT * i + n) + c + 1)
                        bank = (UNITS * n + c) % 4
                        if c == 0:
                            nc.vector.tensor_tensor(y[:, n, :], psY[:, bank, 0, :], b_s[:, :],
                                                    ALU.add).then_inc(y_added, 1)
                            continue
                        for h in range(2):
                            e = 2 * (c - 1) + h
                            dve.wait_ge(y_added, added + (NE + 1) * n + e + 1)
                            nc.vector.scalar_tensor_tensor(y[:, n, :], psY[:, bank, h, :], gates[:, n, e:e + 1],
                                                           y[:, n, :], ALU.mult, ALU.add).then_inc(y_added, 1)
                dve.wait_ge(y_added, added + NT * (NE + 1))
                if not first(i, 1):
                    dve.wait_ge(xo_ready, i)
                normalize_tiles(nc, dve, y, yn, st2, mv2, rs2, stats2, s2, rs2_ready, i + 1, yn_ready)
                s2.end()

            over_supertiles(dve, body)

        @block.tensor
        def _(pe):
            def turn_in(i):
                pe.wait_ge(xn_ready, NT * (i + 1))
                for k in range(KD):
                    if not (first(i, 1) and k == 0):
                        pe.wait_ge(xT_ready, KD * i + k)
                    turn(nc, xn, psT, ident, k).then_inc(turned, 1)

            pe.wait_ge(const_in, N_CONST)
            turn_in(0)
            pe.wait_ge(w_in, 48)

            def body(i, u, last):
                pe.wait_ge(xT_ready, KD * (i + 1))
                if not first(i, 1):
                    pe.wait_ge(gT_ready, i)
                for n in range(NT):
                    for k in range(KD):
                        mm = pe.matmul(psG[:, n * NE:(n + 1) * NE], xT[:, u, k, n * P:(n + 1) * P], wg[:, k, :],
                                       start=(k == 0), stop=(k == KD - 1))
                mm.then_inc(logits_done, 1)
                for e in range(NE + 1):
                    c = (NE + 1) * i + e
                    if not (first(i, 1) and e < 2):
                        pe.wait_ge(h_ready, c - 1)
                    for k in range(KD):
                        mm = pe.matmul(psH[:, (e + u) % 2, :], wa[:, k, e, :], xT[:, u, k, :],
                                       start=(k == 0), stop=(k == KD - 1))
                    mm.then_inc(h_done, 1)
                pe.wait_ge(gates_ready, i + 1)
                for n in range(NT):
                    mm = pe.transpose(psG[0:NE, n * P:(n + 1) * P], gates[:, n, :], ident[:, :])
                mm.then_inc(g_turned, 1)
                if not last:
                    turn_in(i + 1)
                pe.wait_ge(h_ready, (NE + 1) * (i + 1))
                pe.wait_ge(gT_ready, i + 1)
                for n in range(NT):
                    cols = slice(n * P, (n + 1) * P)
                    for c in range(UNITS):
                        g = UNITS * n + c
                        bank = g % 4
                        if not (first(i, 1) and g < 4):
                            g4 = g - 4 if g >= 4 else UNITS * NT + g - 4
                            before = (NE + 1) * (g4 // UNITS) + 2 * (g4 % UNITS) + 1
                            pe.wait_ge(y_added, NT * (NE + 1) * (i if g >= 4 else i - 1) + before)
                        if c == 0:
                            pe.matmul(psY[:, bank, 0, :], hT[:, NE, cols], wb[:, NE, :], start=True, stop=False)
                            mm = pe.matmul(psY[:, bank, 0, :], gT[:, cols], b_e[:, :], start=False, stop=True)
                        else:
                            for h in range(2):
                                e = 2 * (c - 1) + h
                                mm = pe.matmul(psY[:, bank, h, :], hT[:, e, cols], wb[:, e, :], start=True, stop=True)
                        mm.then_inc(y_done, 1)

            over_supertiles(pe, body)

        @block.scalar
        def _(act):
            def take_turned(i, u):
                for k in range(KD):
                    act.wait_ge(turned, KD * i + k + 1)
                    nc.scalar.copy(xT[:, u, k, :], psT[:, :]).then_inc(xT_ready, 1)

            take_turned(0, 0)
            act.wait_ge(const_in, N_CONST)

            def body(i, u, last):
                act.wait_ge(logits_done, i + 1)
                if not first(i, 1):
                    act.wait_ge(gates_ready, i)
                nc.scalar.activation(sig[:, :, :], psG[:, 0:NT * NE].rearrange("p (n e) -> p n e", e=NE),
                                     ACT.Sigmoid).then_inc(sig_ready, 1)
                for e in range(NE + 1):
                    act.wait_ge(h_done, (NE + 1) * i + e + 1)
                    if e == 0 and not first(i, 1):
                        act.wait_ge(y_done, UNITS * NT * i)
                    nc.scalar.activation(hT[:, e, :], psH[:, (e + u) % 2, :], ACT.Gelu,
                                         bias=b_h[:, e:e + 1]).then_inc(h_ready, 1)
                act.wait_ge(g_turned, i + 1)
                nc.scalar.copy(gT[:, :], psG[0:NE, :]).then_inc(gT_ready, 1)
                if not last:
                    take_turned(i + 1, 1 - u)

            over_supertiles(act, body)

        @block.gpsimd
        def _(pool):
            minus_half(nc, pool, half, half_set)
            inverse_root(nc, pool, rs, half, stats, LN, rs_ready)

            def body(i, u, last):
                if not last:
                    inverse_root(nc, pool, rs, half, stats, LN * (i + 2), rs_ready)
                inverse_root(nc, pool, rs2, half, stats2, LN * (i + 1), rs2_ready)
                pool.wait_ge(yn_ready, NT * (i + 1))
                if not first(i, 2):
                    pool.wait_ge(x_outd[u], 8 * (i - u))
                nc.gpsimd.tensor_tensor(xo[:, u, :, :], xin[:, u, :, :], yn[:, :, :], ALU.add).then_inc(xo_ready, 1)

            over_supertiles(pool, body)


NHG = GH // 4
NC = NT
MASKED = -1.0e30


def gla_constants():
    s, t = np.arange(P)[:, None], np.arange(P)[None, :]
    heads = np.zeros((3, 32, J, P), np.float32)
    for h in range(GH):
        heads[:, h, h // 2, GD * (h % 2):GD * (h % 2 + 1)] = 1.0
    minus = np.zeros((NHG, 32, 4), np.float32)
    for a in range(3):
        for r in range(4):
            minus[:, 12 + 4 * a + r, r] = -1.0
    return {
        "up_to": (s <= t).astype(np.float32),
        "after": (s > t).astype(np.float32),
        "masked": np.where(s > t, np.float32(MASKED), np.float32(0)).astype(np.float32),
        "heads": heads.reshape(3 * 32, J * P),
        "minus": minus.reshape(NHG * 32, 4),
    }


def phase_gla(nc, x, wq_t, wk_t, wv_t, wg_t, wog_t, wo_t, wd_t, bd, norm_cols, ident_d, const, x_out):
    with ExitStack() as ctx:
        m = Place(nc, ctx, "gla")
        wq, wk, wv, wg, wog = (m.sb(s, [P, KD, HID]) for s in ("wq", "wk", "wv", "wg", "wog"))
        wo, wd = m.sb("wo", [P, J, D]), m.sb("wd", [P, KD, GH])
        b_d, norm_w = m.sb("b_d", [P, GH]), m.sb("norm_w", [P, J])
        ident, up_to, after = m.sb("ident", [P, P]), m.sb("up_to", [P, P]), m.sb("after", [P, P])
        ident_b, masked_b = m.sb("ident_b", [P, P], BF16), m.sb("masked_b", [P, 4, P], BF16)
        heads_b = m.sb("heads_b", [96, J, P], BF16)
        minus = m.sb("minus", [P, 4])
        ones = m.sb("ones", [P, 1])
        half, half_set = m.sb("half", [P, NT]), m.sem("half_set")
        xin = m.sb("xin", [P, 2, NT, D])
        xn = m.sb("xn", [P, NT, D])
        xT = m.sb("xT", [P, 2, KD, ST])
        st, mv, rs = m.sb("st", [P, NT, 6]), m.sb("mv", [P, NT, 2]), m.sb("rs", [P, 2, NT])
        st2, mv2, rs2 = m.sb("st2", [P, NT, 6]), m.sb("mv2", [P, NT, 2]), m.sb("rs2", [P, 2, NT])
        rs3 = m.sb("rs3", [P, 2, 1])
        y, xo = m.sb("y", [P, NT, D]), m.sb("xo", [P, 2, NT, D])
        z, zabs, zexp, glog = (m.sb(s, [P, NC, GH]) for s in ("z", "zabs", "zexp", "glog"))
        to_end = m.sb("to_end", [P, NC, GH])
        gparts = m.sb("gparts", [96, ST], BF16)
        gmid, grest = m.sb("gmid", [GH, ST], BF16), m.sb("grest", [GH, ST])
        rows_t = m.sb("rows_t", [P, NC, 4, P], BF16)
        rows_s = m.sb("rows_s", [P, ST], BF16)
        q, og = m.sb("q", [P, J, ST]), m.sb("og", [P, J, ST])
        sg = m.sb("sg", [P, 2, ST])
        kg, v = m.sb("kg", [P, 2, HID]), m.sb("v", [P, 2, HID])
        kT = m.sb("kT", [P, 2, J, P])
        kw = m.sb("kw", [P, HID])
        eg, qe = m.sb("eg", [P, J, P]), m.sb("qe", [P, J, P])
        dm, ad = m.sb("dm", [P, 2, 4, P]), m.sb("ad", [P, 2, 4, P])
        osq, yT, osum = m.sb("osq", [P, J, P]), m.sb("yT", [P, J, P]), m.sb("osum", [P, P])
        state, decayed = m.sb("state", [P, J, P]), m.sb("decayed", [P, J, P])
        psP = m.ps("psP", [P, 2, ST])
        psA, psD = m.ps("psA", [P, 4, P]), m.ps("psD", [P, 4, P])
        psO = m.ps("psO", [P, 2, 4, P])
        psX = m.ps("psX", [P, 4, P])
        psW = m.ps("psW", [P, ST])

        const_in, wkgv_in, w_in, x_in = m.sem("const_in"), m.sem("wkgv_in"), m.sem("w_in"), m.sems("x_in", 2)
        const_set, zero_set = m.sem("const_set"), m.sem("zero_set")
        stats, rs_ready, xn_ready, turned, xT_ready = (m.sem(s) for s in ("stats", "rs_ready", "xn_ready", "turned", "xT_ready"))
        stats2, rs2_ready, yn_ready = m.sem("stats2"), m.sem("rs2_ready"), m.sem("yn_ready")
        z_done, decay, soft, g_rows_done, w_done, to_end_ready, gsplit, rows_in = (
            m.sem(s) for s in ("z_done", "decay", "soft", "g_rows_done", "after_done", "to_end_ready", "gsplit", "rows_in"))
        q_done, q_ready, og_done, og_sig, og_ready = (m.sem(s) for s in ("q_done", "q_ready", "og_done", "og_sig", "og_ready"))
        g_done, sig_ready, k_done, kg_ready, v_done, v_ready = (
            m.sem(s) for s in ("g_done", "sig_ready", "k_done", "kg_ready", "v_done", "v_ready"))
        kt_done, kt_ready, kw_ready = m.sem("kt_done"), m.sem("kt_ready"), m.sem("kw_ready")
        d_done, d_ready, qe_ready, a_done, ad_ready = (m.sem(s) for s in ("d_done", "d_ready", "qe_ready", "a_done", "ad_ready"))
        o_done, yT_ready, osq_ready, osum_ready = (m.sem(s) for s in ("o_done", "yT_ready", "osq_ready", "osum_ready"))
        kv_done, decayed_ready, state_ready, state_zero = (
            m.sem(s) for s in ("kv_done", "decayed_ready", "state_ready", "state_zero"))
        out_done, square_ready, rs3_ready, y_ready = (m.sem(s) for s in ("out_done", "square_ready", "rs3_ready", "y_ready"))
        xo_ready, x_outd = m.sem("xo_ready"), m.sems("x_out", 2)
        xv, ov = tokens(x), tokens(x_out)
        N_CONST, N_ROWS = 16 * 8, 16 * 24
        D_USES = 2 + NHG
        block = ctx.enter_context(nc.Block())

        def wide(a, n):
            return a.to_broadcast([*a.shape[:-1], n])

        @block.sync
        def _(sp):
            sp.dma_start(xin[:, 0, :, :], xv[0]).then_inc(x_in[0], 16)
            sp.dma_start(ident[:, :], ident_d).then_inc(const_in, 16)
            for w, d in ((wg, wg_t), (wk, wk_t), (wv, wv_t)):
                sp.dma_start(w[:, :, :], d.rearrange("(k p) o -> p k o", p=P)).then_inc(wkgv_in, 16)
            sp.dma_start(up_to[:, :], const["up_to"]).then_inc(const_in, 16)
            sp.dma_start(after[:, :], const["after"]).then_inc(const_in, 16)
            sp.dma_start(kg[:, 0, 0:P], const["masked"]).then_inc(const_in, 16)
            sp.dma_start(og[0:96, 0:2, :].rearrange("p a b -> p (a b)"), const["heads"]).then_inc(const_in, 16)
            sp.dma_start(minus[:, :], const["minus"]).then_inc(const_in, 16)
            sp.dma_start(b_d[:, :], row(bd)).then_inc(const_in, 16)
            sp.dma_start(norm_w[:, :], norm_cols).then_inc(const_in, 16)
            for w, d in ((wd, wd_t), (wq, wq_t), (wog, wog_t), (wo, wo_t)):
                sp.dma_start(w[:, :, :], d.rearrange("(k p) o -> p k o", p=P)).then_inc(w_in, 16)

            def body(i, u, last):
                sp.wait_ge(gsplit, 5 * (i + 1))
                for a in range(3):
                    for r in range(4):
                        sp.dma_start(rows_t[4 * a + r:4 * a + r + 97:32, :, r, :],
                                     gparts[32 * a + r:32 * a + r + 13:4, :].rearrange("p (n t) -> p n t", t=P)
                                     ).then_inc(rows_in, 16)
                    for hg in range(NHG):
                        sp.dma_start(rows_s[32 * hg + 12 + 4 * a:32 * hg + 16 + 4 * a, :],
                                     gparts[32 * a + 4 * hg:32 * a + 4 * hg + 4, :]).then_inc(rows_in, 16)
                if not first(i, 1):
                    sp.wait_ge(xo_ready, i)
                    sp.dma_start(ov[i - 1], xo[:, 1 - u, :, :]).then_inc(x_outd[1 - u], 16)
                if not last:
                    sp.dma_start(xin[:, 1 - u, :, :], xv[i + 1]).then_inc(x_in[1 - u], 16)

            over_supertiles(sp, body)
            sp.wait_ge(xo_ready, NST)
            sp.dma_start(ov[NST - 1], xo[:, 1, :, :]).then_inc(x_outd[1], 16)
            for s in x_outd:
                sp.wait_ge(s, 16 * NST // 2)

        @block.tensor
        def _(pe):
            def turn_in(i, after_kt):
                pe.wait_ge(xn_ready, NT * (i + 1))
                for k in range(KD):
                    if k:
                        pe.wait_ge(xT_ready, KD * i + k)
                    elif after_kt is not None:
                        pe.wait_ge(kt_ready, after_kt)
                    turn(nc, xn, psX[:, :, :].rearrange("p j t -> p (j t)"), ident, k).then_inc(turned, 1)

            def project(bank, w, half, u, n, done):
                for k in range(KD):
                    mm = pe.matmul(psP[:, bank, :], xT[:, u, k, n * P:(n + 1) * P],
                                   w[:, k, half * ST:(half + 1) * ST], start=(k == 0), stop=(k == KD - 1))
                mm.then_inc(done, 1)

            def gates_and_keys(i, u, n):
                c = NC * i + n
                for h in range(2):
                    if h:
                        pe.wait_ge(sig_ready, 2 * c + 1)
                    elif n == 1:
                        pe.wait_ge(og_sig, J * (i + 1))
                    elif not (first(i, 1) and n == 0):
                        pe.wait_ge(v_ready, 2 * c - 1)
                    project(0, wg, h, u, n, g_done)
                    if h:
                        pe.wait_ge(kg_ready, 2 * c + 1)
                    elif n != 1 and not (first(i, 1) and n == 0):
                        pe.wait_ge(v_ready, 2 * c)
                    project(1, wk, h, u, n, k_done)

            def values(i, u, n, h):
                c = NC * i + n
                pe.wait_ge(sig_ready if h == 0 else kg_ready, 2 * c + 2)
                project(h, wv, h, u, n, v_done)

            def out_project(c):
                pe.wait_ge(yT_ready, 2 * c + 2)
                pe.wait_ge(y_ready, c)
                for j in range(J):
                    pe.matmul(psW[:, 0:D], yT[:, j, :], wo[:, j, :], start=(j == 0), stop=(j == J - 1))
                pe.wait_ge(osum_ready, c + 1)
                pe.matmul(psW[:, D:D + 1], osum[:, :], ones[:, :], start=True, stop=True).then_inc(out_done, 1)

            def supertile(i, u):
                c = NC * i
                if not first(i, 1):
                    out_project(c - 1)
                    pe.wait_ge(y_ready, c)
                pe.wait_ge(xT_ready, KD * (i + 1))
                for n in range(NC):
                    for k in range(KD):
                        mm = pe.matmul(psW[:, n * GH:(n + 1) * GH], xT[:, u, k, n * P:(n + 1) * P], wd[:, k, :],
                                       start=(k == 0), stop=(k == KD - 1))
                mm.then_inc(z_done, 1)

                def tile(j, w, done, taken):
                    if j >= 2:
                        pe.wait_ge(taken, J * i + j - 1)
                    for k in range(KD):
                        mm = pe.matmul(psP[:, j % 2, :], w[:, k, j * P:(j + 1) * P], xT[:, u, k, :],
                                       start=(k == 0), stop=(k == KD - 1))
                    mm.then_inc(done, 1)

                for j in range(J):
                    if j < 2:
                        pe.wait_ge(v_ready, 2 * c + j + 1)
                    tile(j, wq, q_done, q_ready)
                    if j == 3:
                        pe.wait_ge(decay, 4 * (i + 1))
                        for n in range(NC):
                            mm = pe.matmul(psW[0:GH, n * P:(n + 1) * P], glog[:, n, :], up_to[:, :],
                                           start=True, stop=True)
                        mm.then_inc(g_rows_done, 1)
                        if not first(i, 1):
                            pe.wait_ge(state_ready, 2 * c)
                        for n in range(NC):
                            mm = pe.matmul(psX[:, 0, n * GH:(n + 1) * GH], after[:, :], glog[:, n, :],
                                           start=True, stop=True)
                        mm.then_inc(w_done, 1)
                for j in range(J):
                    if j < 2:
                        pe.wait_ge(q_ready, J * i + 7 + j)
                    tile(j, wog, og_done, og_sig)

            def slot(i, u, n, last):
                c = NC * i + n
                ahead = not (last and n == NC - 1)
                nxt = (i, u, n + 1) if n < NC - 1 else (i + 1, 1 - u, 0)
                if ahead:
                    if n == NC - 1:
                        pe.wait_ge(xT_ready, KD * (i + 2))
                    gates_and_keys(*nxt)
                for g in range(2):
                    pe.wait_ge(kg_ready, 2 * c + g + 1)
                    if g:
                        pe.wait_ge(kt_ready, 2 * c + 1)
                    elif n == 0:
                        pe.wait_ge(to_end_ready, i + 1)
                    else:
                        pe.wait_ge(state_ready, 2 * c)
                    for jj in range(4):
                        j = 4 * g + jj
                        mm = pe.transpose(psX[:, jj, :], kg[:, n % 2, j * P:(j + 1) * P], ident[:, :])
                    mm.then_inc(kt_done, 1)
                if n == 1 and not last:
                    turn_in(i + 1, 2 * c + 2)
                if n:
                    out_project(c - 1)
                else:
                    pe.wait_ge(gsplit, 5 * (i + 1))
                for g in range(2):
                    if not (first(i, 1) and n == 0 and g == 0):
                        pe.wait_ge(d_ready, D_USES * c + g)
                    for jj in range(4):
                        mm = pe.matmul(psD[:, jj, :], heads_b[:, 4 * g + jj, :], gparts[:, n * P:(n + 1) * P],
                                       start=True, stop=True)
                    mm.then_inc(d_done, 1)
                if n == 0:
                    pe.wait_ge(rows_in, N_ROWS * (i + 1))
                    pe.wait_ge(q_ready, J * (i + 1))

                def outputs(hg):
                    g = hg // 2
                    pe.wait_ge(ad_ready, NHG * c + hg + 1)
                    if hg % 2 == 0:
                        pe.wait_ge(qe_ready, 2 * c + g + 1)
                        pe.wait_ge(v_ready, 2 * c + g + 1)
                        if n == 0 and u == 0:
                            pe.wait_ge(state_zero, i + 2)
                        else:
                            pe.wait_ge(state_ready, 2 * c - 1 + g)
                        if not (first(i, 1) and n == 0):
                            pe.wait_ge(osq_ready, 2 * c - 1 + g)
                    for jj in range(2):
                        j = 2 * hg + jj
                        for odd in range(2):
                            h = 2 * j + odd
                            pe.matmul(psO[GD * odd:GD * (odd + 1), g, j % 4, :],
                                      v[:, n % 2, h * GD:(h + 1) * GD], ad[:, hg % 2, 2 * jj + odd, :],
                                      start=True, stop=False, skip_group_check=True)
                        mm = pe.matmul(psO[:, g, j % 4, :], state[:, j, :], qe[:, j, :], start=False, stop=True,
                                       skip_group_check=True)
                    mm.then_inc(o_done, 1)

                def update(g):
                    if g:
                        pe.wait_ge(state_ready, 2 * c + 1)
                    else:
                        pe.wait_ge(kw_ready, c + 1)
                        pe.wait_ge(v_ready, 2 * c + 2)
                        pe.wait_ge(kt_ready, 2 * c + 2)
                        if n == 1 and not last:
                            pe.wait_ge(xT_ready, KD * (i + 2))
                    for jj in range(4):
                        j = 4 * g + jj
                        mm = pe.matmul(psX[:, jj, :], kw[:, j * P:(j + 1) * P], v[:, n % 2, j * P:(j + 1) * P],
                                       start=True, stop=True)
                    mm.then_inc(kv_done, 1)

                for hg in range(NHG):
                    pe.wait_ge(d_ready, D_USES * c + 2 + hg)
                    base = 32 * hg
                    pe.matmul(psD[:, :, :], ident_b[:, :], masked_b[:, :, :], start=True, stop=False)
                    pe.matmul(psD[:, :, :], rows_s[base:base + 24, n * P:(n + 1) * P],
                              rows_t[base:base + 24, n, :, :], start=False, stop=True,
                              tile_position=(base, 0)).then_inc(d_done, 1)
                    if not (first(i, 1) and n == 0 and hg == 0):
                        pe.wait_ge(ad_ready, NHG * c + hg)
                    pe.wait_ge(kt_ready, 2 * c + hg // 2 + 1)
                    for r in range(4):
                        j = 2 * hg + r // 2
                        mm = pe.matmul(psA[:, r, :], kT[:, r % 2, j, :], q[:, j, n * P:(n + 1) * P],
                                       start=True, stop=True)
                    mm.then_inc(a_done, 1)
                    if hg < 2 and ahead:
                        values(*nxt, hg)
                    if hg:
                        outputs(hg - 1)
                update(0)
                outputs(NHG - 1)
                update(1)

            pe.wait_ge(const_in, N_CONST)
            pe.wait_ge(const_set, 7)
            turn_in(0, None)
            pe.wait_ge(wkgv_in, 48)
            pe.wait_ge(xT_ready, KD)
            gates_and_keys(0, 0, 0)
            for h in range(2):
                values(0, 0, 0, h)
            pe.wait_ge(w_in, 64)
            pe.wait_ge(zero_set, 1)

            def body(i, u, last):
                supertile(i, u)
                for n in range(NC):
                    slot(i, u, n, last)

            over_supertiles(pe, body)
            out_project(NC * NST - 1)

        @block.scalar
        def _(act):
            def take_turned(i, u):
                for k in range(KD):
                    act.wait_ge(turned, KD * i + k + 1)
                    nc.scalar.copy(xT[:, u, k, :], psX[:, :, :].rearrange("p j t -> p (j t)")).then_inc(xT_ready, 1)

            def sigmoids(i, n):
                c = NC * i + n
                for h in range(2):
                    act.wait_ge(g_done, 2 * c + h + 1)
                    if not (first(i, 1) and n == 0):
                        act.wait_ge(kg_ready, 2 * c - 1 + h)
                    nc.scalar.activation(sg[:, h, :], psP[:, 0, :], ACT.Sigmoid).then_inc(sig_ready, 1)

            def take_values(i, n, h):
                act.wait_ge(v_done, 2 * (NC * i + n) + h + 1)
                nc.scalar.copy(v[:, n % 2, h * ST:(h + 1) * ST], psP[:, h, :]).then_inc(v_ready, 1)

            def supertile(i, u):
                c = NC * i
                act.wait_ge(decay, 4 * i + 2)
                nc.scalar.activation(zexp[:, :, :], zabs[:, :, :], ACT.Exp, scale=-1.0).then_inc(soft, 1)
                act.wait_ge(soft, 2 * i + 1)
                nc.scalar.activation(zexp[:, :, :], zexp[:, :, :], ACT.Ln, bias=1.0).then_inc(soft, 1)
                if not first(i, 1):
                    act.wait_ge(qe_ready, 2 * c)
                for j in range(J):
                    act.wait_ge(q_done, J * i + j + 1)
                    nc.scalar.copy(q[:, j, :], psP[:, j % 2, :]).then_inc(q_ready, 1)
                    if j == 3:
                        act.wait_ge(w_done, i + 1)
                        if not first(i, 1):
                            act.wait_ge(kw_ready, c)
                        nc.scalar.activation(to_end[:, :, :].rearrange("p n h -> p (n h)"), psX[:, 0, 0:NC * GH],
                                             ACT.Exp).then_inc(to_end_ready, 1)
                if not first(i, 1):
                    act.wait_ge(yT_ready, 2 * c)
                for j in range(J):
                    act.wait_ge(og_done, J * i + j + 1)
                    nc.scalar.activation(og[:, j, :], psP[:, j % 2, :], ACT.Sigmoid).then_inc(og_sig, 1)

            def slot(i, u, n, last):
                c = NC * i + n
                ahead = not (last and n == NC - 1)
                nxt = (i, n + 1) if n < NC - 1 else (i + 1, 0)
                if ahead:
                    sigmoids(*nxt)
                for g in range(2):
                    act.wait_ge(kt_done, 2 * c + g + 1)
                    for odd in range(2):
                        rows = slice(GD * odd, GD * (odd + 1))
                        last_copy = nc.scalar.copy(kT[rows, odd, 4 * g:4 * g + 4, :], psX[rows, :, :])
                    last_copy.then_inc(kt_ready, 1)
                if n == 1 and not last:
                    take_turned(i + 1, 1 - u)
                for g in range(2):
                    act.wait_ge(d_done, D_USES * c + g + 1)
                    if g == 0 and not (first(i, 1) and n == 0):
                        act.wait_ge(decayed_ready, c)
                        act.wait_ge(qe_ready, 2 * c)
                    nc.scalar.activation(eg[:, 4 * g:4 * g + 4, :], psD[:, :, :], ACT.Exp).then_inc(d_ready, 1)
                for hg in range(NHG):
                    act.wait_ge(d_done, D_USES * c + 3 + hg)
                    if not (first(i, 1) and n == 0 and hg < 2):
                        act.wait_ge(ad_ready, NHG * c + hg - 1)
                    nc.scalar.activation(dm[:, hg % 2, :, :], psD[:, :, :], ACT.Exp).then_inc(d_ready, 1)
                    if hg < 2 and ahead:
                        take_values(*nxt, hg)
                for g in range(2):
                    act.wait_ge(yT_ready, 2 * c + g + 1)
                    if g == 0 and not (first(i, 1) and n == 0):
                        act.wait_ge(osum_ready, c)
                    nc.scalar.activation(osq[:, 4 * g:4 * g + 4, :], psO[:, g, :, :], ACT.Square).then_inc(osq_ready, 1)

            take_turned(0, 0)
            act.wait_ge(const_set, 7)
            sigmoids(0, 0)
            for h in range(2):
                take_values(0, 0, h)
            act.wait_ge(zero_set, 1)

            def body(i, u, last):
                supertile(i, u)
                for n in range(NC):
                    slot(i, u, n, last)

            over_supertiles(act, body)

        @block.vector
        def _(dve):
            s, s2, t, dec = Steps(LN), Steps(LN), Steps(5), Steps(4)

            def pre(i, u):
                s.start(i)
                dve.wait_ge(x_in[u], 8 * (i - u) + 16)
                if not first(i, 1):
                    dve.wait_ge(turned, KD * i)
                normalize_tiles(nc, dve, xin[:, u, :, :], xn, st, mv, rs, stats, s, rs_ready, i + 1, xn_ready)
                s.end()

            def gated_keys(i, n):
                c = NC * i + n
                for h in range(2):
                    dve.wait_ge(k_done, 2 * c + h + 1)
                    dve.wait_ge(sig_ready, 2 * c + h + 1)
                    if h == 0 and not (first(i, 1) and n < 2):
                        dve.wait_ge(kw_ready, c - 1)
                    nc.vector.tensor_tensor(kg[:, n % 2, h * ST:(h + 1) * ST], psP[:, 1, :], sg[:, h, :],
                                            ALU.mult).then_inc(kg_ready, 1)

            def mean_square(c):
                dve.wait_ge(out_done, c + 1)
                nc.vector.tensor_scalar(rs3[:, 0, :], psW[:, D:D + 1], 1.0 / HID, RMS_EPS, ALU.mult,
                                        ALU.add).then_inc(square_ready, 1)

            def take_out(c, n, i_of_y):
                dve.wait_ge(rs3_ready, c + 1)
                if n == 0 and not first(i_of_y, 1):
                    dve.wait_ge(xo_ready, i_of_y)
                nc.vector.tensor_scalar(y[:, n, :], psW[:, 0:D], rs3[:, 1, :], None, ALU.mult).then_inc(y_ready, 1)

            def norm_y(i):
                s2.start(i)
                dve.wait_ge(y_ready, NC * (i + 1))
                normalize_tiles(nc, dve, y, y, st2, mv2, rs2, stats2, s2, rs2_ready, i + 1, yn_ready)
                s2.end()

            def supertile(i, u):
                c = NC * i
                if not first(i, 1):
                    mean_square(c - 1)
                    take_out(c - 1, NC - 1, i - 1)
                dec.start(i)
                dve.wait_ge(z_done, i + 1)
                nc.vector.tensor_tensor(z[:, :, :], psW[:, 0:NC * GH].rearrange("p (n h) -> p n h", h=GH),
                                        b_d[:, :].rearrange("p (n h) -> p n h", n=1).to_broadcast([P, NC, GH]),
                                        ALU.add).then_inc(decay, dec.inc())
                dve.wait_ge(decay, dec.now())
                if not first(i, 1):
                    dve.wait_ge(soft, 2 * i)
                nc.vector.scalar_tensor_tensor(zabs[:, :, :], z[:, :, :], -1.0, z[:, :, :], ALU.mult,
                                               ALU.max).then_inc(decay, dec.inc())
                dve.wait_ge(soft, 2 * i + 2)
                nc.vector.scalar_tensor_tensor(z[:, :, :], z[:, :, :], 0.0, zexp[:, :, :], ALU.max,
                                               ALU.add).then_inc(decay, dec.inc())
                dve.wait_ge(decay, dec.now())
                nc.vector.tensor_scalar(glog[:, :, :], z[:, :, :], -1.0, None, ALU.mult).then_inc(decay, dec.inc())
                dec.end()
                t.start(i)
                dve.wait_ge(g_rows_done, i + 1)
                nc.vector.tensor_copy(gparts[0:GH, :], psW[0:GH, :]).then_inc(gsplit, t.inc())
                dve.wait_ge(gsplit, t.now())
                nc.vector.tensor_tensor(grest[:, :], psW[0:GH, :], gparts[0:GH, :], ALU.subtract).then_inc(gsplit, t.inc())
                dve.wait_ge(gsplit, t.now())
                nc.vector.tensor_copy(gmid[:, :], grest[:, :]).then_inc(gsplit, t.inc())
                dve.wait_ge(gsplit, t.now())
                nc.vector.tensor_copy(gparts[32:32 + GH, :], gmid[:, :]).then_inc(gsplit, t.inc())
                nc.vector.tensor_tensor(gparts[64:64 + GH, :], grest[:, :], gmid[:, :], ALU.subtract).then_inc(gsplit, t.inc())
                t.end()
                if not first(i, 1):
                    norm_y(i - 1)

            def slot(i, u, n, last):
                c = NC * i + n
                ahead = not (last and n == NC - 1)
                nxt = (i, n + 1) if n < NC - 1 else (i + 1, 0)
                if ahead:
                    gated_keys(*nxt)
                if n:
                    mean_square(c - 1)
                for g in range(2):
                    js = slice(4 * g, 4 * g + 4)
                    dve.wait_ge(d_ready, D_USES * c + g + 1)
                    if n == 0 and g == 0:
                        dve.wait_ge(q_ready, J * (i + 1))
                    nc.vector.tensor_tensor(qe[:, js, :], q[:, js, n * P:(n + 1) * P], eg[:, js, :],
                                            ALU.mult).then_inc(qe_ready, 1)
                if n:
                    take_out(c - 1, n - 1, i)

                def weighted(hg):
                    dve.wait_ge(a_done, NHG * c + hg + 1)
                    dve.wait_ge(d_ready, D_USES * c + 3 + hg)
                    if not (first(i, 1) and n == 0 and hg < 2):
                        dve.wait_ge(o_done, NHG * c + hg - 1)
                    nc.vector.tensor_tensor(ad[:, hg % 2, :, :], psA[:, :, :], dm[:, hg % 2, :, :],
                                            ALU.mult).then_inc(ad_ready, 1)

                def take_outputs(g):
                    js = slice(4 * g, 4 * g + 4)
                    dve.wait_ge(o_done, NHG * c + 2 * g + 2)
                    if n == 0 and g == 0:
                        dve.wait_ge(og_ready, J * (i + 1))
                    if g == 0 and not (first(i, 1) and n == 0):
                        dve.wait_ge(out_done, c)
                    nc.vector.tensor_tensor(yT[:, js, :], psO[:, g, :, :], og[:, js, n * P:(n + 1) * P],
                                            ALU.mult).then_inc(yT_ready, 1)

                def update(g):
                    js = slice(4 * g, 4 * g + 4)
                    dve.wait_ge(kv_done, 2 * c + g + 1)
                    dve.wait_ge(o_done, NHG * c + 2 * g + 2)
                    if g == 0:
                        dve.wait_ge(decayed_ready, c + 1)
                    for odd in range(2):
                        r = slice(GD * odd, GD * (odd + 1))
                        last_add = nc.vector.tensor_tensor(state[r, js, r], psX[r, :, r], decayed[r, js, r], ALU.add)
                    last_add.then_inc(state_ready, 1)

                weighted(0)
                weighted(1)
                weighted(2)
                take_outputs(0)
                weighted(3)
                update(0)
                take_outputs(1)
                update(1)
                dve.wait_ge(osq_ready, 2 * c + 2)
                nc.vector.tensor_reduce(osum[:, :], osq[:, :, :].rearrange("p j t -> p t j"), AX.X,
                                        ALU.add).then_inc(osum_ready, 1)
                if n == 0 and not last:
                    pre(i + 1, 1 - u)

            nc.vector.memset(ones[:, :], 1.0).then_inc(const_set, 1)
            nc.vector.memset(rows_s[:, :], 1.0).then_inc(const_set, 1)
            pre(0, 0)
            dve.wait_ge(const_in, N_CONST)
            nc.vector.tensor_copy(ident_b[:, :], ident[:, :]).then_inc(const_set, 1)
            nc.vector.tensor_copy(masked_b[:, :, :], kg[:, 0, 0:P].rearrange("p (a t) -> p a t", a=1)
                                  .to_broadcast([P, 4, P])).then_inc(const_set, 1)
            nc.vector.tensor_copy(heads_b[:, :, :].rearrange("p j t -> p (j t)"),
                                  og[0:96, 0:2, :].rearrange("p a b -> p (a b)")).then_inc(const_set, 1)
            nc.vector.memset(gparts[:, :], 0.0).then_inc(const_set, 1)
            nc.vector.tensor_copy(
                rows_t[:, :, :, :],
                minus[:, :].rearrange("p (n r t) -> p n r t", n=1, t=1).to_broadcast([P, NC, 4, P])
            ).then_inc(const_set, 1)
            dve.wait_ge(const_set, 7)
            gated_keys(0, 0)

            def body(i, u, last):
                supertile(i, u)
                for n in range(NC):
                    slot(i, u, n, last)

            over_supertiles(dve, body)
            mean_square(NC * NST - 1)
            take_out(NC * NST - 1, NC - 1, NST - 1)
            norm_y(NST - 1)

        @block.gpsimd
        def _(pool):
            def root_square(c):
                pool.wait_ge(square_ready, c + 1)
                nc.gpsimd.tensor_tensor(rs3[:, 1, :], rs3[:, 0, :], half[:, 0:1], ALU.pow).then_inc(rs3_ready, 1)

            def residual(i, u):
                inverse_root(nc, pool, rs2, half, stats2, LN * (i + 1), rs2_ready)
                pool.wait_ge(yn_ready, NT * (i + 1))
                if not first(i, 2):
                    pool.wait_ge(x_outd[u], 8 * (i - u))
                nc.gpsimd.tensor_tensor(xo[:, u, :, :], xin[:, u, :, :], y[:, :, :], ALU.add).then_inc(xo_ready, 1)

            def supertile(i, u):
                c = NC * i
                if not first(i, 1):
                    root_square(c - 1)
                if u == 0:
                    if not first(i, 1):
                        pool.wait_ge(state_ready, 2 * c)
                    nc.gpsimd.memset(state[:, :, :], 0.0).then_inc(state_zero, 2)
                if not first(i, 1):
                    residual(i - 1, 1 - u)
                for j in range(J):
                    pool.wait_ge(og_sig, J * i + j + 1)
                    nc.gpsimd.tensor_tensor(og[:, j, :], og[:, j, :], norm_w[:, j:j + 1].to_broadcast([P, ST]),
                                            ALU.mult).then_inc(og_ready, 1)

            def slot(i, u, n, last):
                c = NC * i + n
                pool.wait_ge(kg_ready, 2 * c + 2)
                if n == 0:
                    pool.wait_ge(to_end_ready, i + 1)
                if not (first(i, 1) and n == 0):
                    pool.wait_ge(kv_done, 2 * c)
                nc.gpsimd.tensor_tensor(kw[:, :].rearrange("p (h d) -> p h d", d=GD),
                                        kg[:, n % 2, :].rearrange("p (h d) -> p h d", d=GD),
                                        to_end[:, n, :].rearrange("p (h d) -> p h d", d=1).to_broadcast([P, GH, GD]),
                                        ALU.mult).then_inc(kw_ready, 1)
                if n:
                    root_square(c - 1)
                pool.wait_ge(d_ready, D_USES * c + 2)
                if n == 0 and u == 0:
                    pool.wait_ge(state_zero, i + 2)
                else:
                    pool.wait_ge(state_ready, 2 * c)
                nc.gpsimd.tensor_tensor(decayed[:, :, :], state[:, :, :], eg[:, :, P - 1:P].to_broadcast([P, J, P]),
                                        ALU.mult).then_inc(decayed_ready, 1)
                if n == 0 and not last:
                    inverse_root(nc, pool, rs, half, stats, LN * (i + 2), rs_ready)

            minus_half(nc, pool, half, half_set)
            inverse_root(nc, pool, rs, half, stats, LN, rs_ready)
            nc.gpsimd.memset(kT[:, :, :, :], 0.0).then_inc(zero_set, 1)
            pool.wait_ge(const_in, N_CONST)

            def body(i, u, last):
                supertile(i, u)
                for n in range(NC):
                    slot(i, u, n, last)

            over_supertiles(pool, body)
            root_square(NC * NST - 1)
            residual(NST - 1, 1)


def sandwich(nc, x, qkv_w_t, qkv_b, qkv_b_cols, out_w_t, out_b, ffn_w1_t, ffn_b1_cols, ffn_w2_t, ffn_b2,
             wq_t, wk_t, wv_t, wo_t, wg_t, wog_t, wd_t, bd, norm_cols,
             gate_w, moe_w1, moe_b1_cols, moe_w2, moe_b2, ws1, bs1_col, ws2, bs2, route_scale,
             ident, up_to, after, masked, heads, minus, out):
    def scratch(name, shape, dt=F32):
        return nc.dram_tensor(name, shape, dt, kind="Internal").ap()

    parts = scratch("qk_parts", [2, NST, NG, 3, HG * AD, ST], BF16)
    v_aug = scratch("values", [NST, NT, NG, P, HG * VW])
    att = scratch("attended", [TOKENS, D])
    x1, x2, x3 = (scratch(f"stream{k}", [TOKENS, D]) for k in (1, 2, 3))
    const = {"up_to": up_to, "after": after, "masked": masked, "heads": heads, "minus": minus}
    phase_qkv(nc, x, qkv_w_t, qkv_b, qkv_b_cols, ident, parts, v_aug)
    phase_attention(nc, parts, v_aug, ident, att)
    phase_project(nc, x, att, out_w_t, out_b, ident, x1)
    phase_ternary_ffn(nc, x1, ffn_w1_t, ffn_b1_cols, ffn_w2_t, ffn_b2, ident, x2)
    phase_gla(nc, x2, wq_t, wk_t, wv_t, wg_t, wog_t, wo_t, wd_t, bd, norm_cols, ident, const, x3)
    phase_experts(nc, x3, gate_w, moe_w1, moe_b1_cols, moe_w2, moe_b2, ws1, bs1_col, ws2, bs2, route_scale,
                  ident, out)



def kernel(**inputs):
    import concourse.bacc as bacc
    from concourse.bass_utils import run_bass_kernel_spmd

    a = {name: np.asarray(v) for name, v in inputs.items()}
    l0a, l0f, l1a, l1f = "L0_attn_", "L0_ffn_", "L1_attn_", "L1_ffn_"

    def columns(v):
        return v.reshape(-1, P).T

    laid_out = {
        "x": a[l0a + "x"].reshape(TOKENS, D),
        "qkv_w_t": a[l0a + "qkv_w"].T,
        "qkv_b": a[l0a + "qkv_b"],
        "qkv_b_cols": columns(a[l0a + "qkv_b"]),
        "out_w_t": a[l0a + "out_w"].T,
        "out_b": a[l0a + "out_b"],
        "ffn_w1_t": a[l0f + "W1"].T,
        "ffn_b1_cols": columns(a[l0f + "b1"]),
        "ffn_w2_t": a[l0f + "W2"].T,
        "ffn_b2": a[l0f + "b2"],
        **{w.lower() + "_t": a[l1a + w].T for w in ("Wq", "Wk", "Wv", "Wo", "Wg", "Wog", "Wd")},
        "bd": a[l1a + "bd"],
        "norm_cols": columns(a[l1a + "norm_w"]),
        "gate_w": a[l1f + "gate_W"],
        "moe_w1": a[l1f + "W1"],
        "moe_b1_cols": a[l1f + "b1"].T,
        "moe_w2": a[l1f + "W2"],
        "moe_b2": a[l1f + "b2"],
        "ws1": a[l1f + "Ws1"],
        "bs1_col": a[l1f + "bs1"].reshape(EH, 1),
        "ws2": a[l1f + "Ws2"],
        "bs2": a[l1f + "bs2"],
        "route_scale": a[l1f + "route_scale"].reshape(1, 1),
        "ident": np.eye(P, dtype=np.float32),
        **gla_constants(),
    }
    nc = bacc.Bacc("TRN2", target_bir_lowering=False, num_devices=1)
    arrays, args = {}, {}
    for name, v in laid_out.items():
        v = np.ascontiguousarray(v)
        arrays[f"in_{name}"] = v
        args[name] = nc.dram_tensor(f"in_{name}", v.shape, mybir.dt.from_np(v.dtype), kind="ExternalInput").ap()
    out = nc.dram_tensor("out", [TOKENS, D], F32, kind="ExternalOutput").ap()
    sandwich(nc, **args, out=out)
    r = run_bass_kernel_spmd(nc, [arrays], core_ids=[0])
    return r.results[0]["out"].reshape(BATCH, SEQ, D)
```

```python
from contextlib import ExitStack

import numpy as np
import concourse.bass as bass
from concourse import mybir

F32 = mybir.dt.float32
F32R = mybir.dt.float32r
BF16 = mybir.dt.bfloat16
ALU = mybir.AluOpType
ACT = mybir.ActivationFunctionType
AX = mybir.AxisListType

P = 128
BATCH, SEQ, D = 4, 1024, 256
TOKENS = BATCH * SEQ
ST = 512
NT = ST // P
NST = TOKENS // ST
KD = D // P
LN_EPS = 1e-5

AH, AD = 16, 16
HG = 4
NG = AH // HG
NBG = BATCH * NG
KT = SEQ // P
QH = SEQ // ST
VW = 32
Q_PART = (0, 0, 0, 1, 1, 2)
K_PART = (0, 1, 2, 0, 1, 0)
STACK = len(Q_PART) * AD
ROWS = STACK + 3

FF = 4 * D
FT = FF // P

GH, GD = 16, 64
HID = GH * GD
J = HID // P
RMS_EPS = float(np.finfo(np.float32).eps)

NE, EH = 8, 128


class Steps:

    def __init__(self, per):
        self.per, self.base, self.k = per, 0, 0

    def start(self, i):
        self.base, self.k = i * self.per, 0

    def inc(self):
        self.k += 1
        return 1

    def now(self):
        return self.base + self.k

    def end(self):
        assert self.k == self.per, (self.k, self.per)


def over_supertiles(eng, body):
    body(0, 0, False)
    body(1, 1, False)
    with eng.Fori(1, NST // 2 - 1) as k:
        body(2 * k, 0, False)
        body(2 * k + 1, 1, False)
    body(NST - 2, 0, False)
    body(NST - 1, 1, True)


def first(i, n):
    return isinstance(i, int) and i < n


def wait_past(eng, sem, value):
    if not isinstance(value, int) or value > 0:
        eng.wait_ge(sem, value)


def tokens(x):
    return x.rearrange("(i n p) c -> i p n c", p=P, n=NT)


def row(x):
    return x.rearrange("(a c) -> a c", a=1).to_broadcast([P, x.shape[0]])



LN = 2 * NT + 2


def tile_stats(nc, dve, x, st, mv, rs, stats, s):
    for n in range(NT):
        nc.vector.bn_stats(st[:, n, :], x[:, n, :]).then_inc(stats, s.inc())
    dve.wait_ge(stats, s.now())
    nc.vector.memset(rs[:, 0, :], LN_EPS).then_inc(stats, s.inc())
    for n in range(NT):
        nc.vector.bn_aggr(mv[:, n, :], st[:, n, :]).then_inc(stats, s.inc())
    dve.wait_ge(stats, s.now())
    nc.vector.tensor_tensor(rs[:, 0, :], mv[:, :, 1], rs[:, 0, :], ALU.add).then_inc(stats, s.inc())


def normalize_with(nc, dve, x, xn, mv, rs, rs_ready, rs_count, xn_ready):
    dve.wait_ge(rs_ready, rs_count)
    for n in range(NT):
        nc.vector.tensor_scalar(xn[:, n, :], x[:, n, :], mv[:, n, 0:1], rs[:, 1, n:n + 1],
                                ALU.subtract, ALU.mult).then_inc(xn_ready, 1)


def normalize_tiles(nc, dve, x, xn, st, mv, rs, stats, s, rs_ready, rs_count, xn_ready):
    tile_stats(nc, dve, x, st, mv, rs, stats, s)
    normalize_with(nc, dve, x, xn, mv, rs, rs_ready, rs_count, xn_ready)


def inverse_root(nc, pool, rs, half, stats, count, rs_ready):
    pool.wait_ge(stats, count)
    nc.gpsimd.tensor_tensor(rs[:, 1, :], rs[:, 0, :], half[:, 0:rs.shape[2]], ALU.pow).then_inc(rs_ready, 1)


def minus_half(nc, pool, half, half_set):
    nc.gpsimd.memset(half[:, :], -0.5).then_inc(half_set, 1)
    pool.wait_ge(half_set, 1)


def turn(nc, src, ps, ident, k):
    for n in range(NT):
        last = nc.tensor.transpose(ps[:, n * P:(n + 1) * P], src[:, n, k * P:(k + 1) * P], ident[:, :])
    return last


class Place:

    def __init__(self, nc, ctx, name):
        self.nc, self.ctx, self.name, self.taken = nc, ctx, name, []
        ctx.callback(self.clear)

    def clear(self):
        self.nc.clear_and_free_semaphores(self.taken)
        self.nc.all_engine_barrier()

    def sb(self, name, shape, dt=F32):
        return self.ctx.enter_context(self.nc.sbuf_tensor(f"{self.name}_sb_{name}", shape, dt))

    def ps(self, name, shape, dt=F32):
        return self.ctx.enter_context(self.nc.psum_tensor(f"{self.name}_ps_{name}", shape, dt))

    def sem(self, name):
        self.taken.append(self.nc.alloc_semaphore(f"{self.name}_{name}"))
        return self.taken[-1]

    def sems(self, name, n):
        return [self.sem(f"{name}{k}") for k in range(n)]


def phase_qkv(nc, x, w_t, bias, bias_cols, ident_d, parts, v_aug):
    with ExitStack() as ctx:
        m = Place(nc, ctx, "qkv")
        w = m.sb("w", [P, KD, 3 * D])
        ident = m.sb("ident", [P, P])
        b_in = m.sb("b_in", [P, 2 * KD])
        b_qk = m.sb("b_qk", [P, 2 * KD])
        b_v = m.sb("b_v", [P, D])
        xin = m.sb("xin", [P, 2, NT, D])
        xn = m.sb("xn", [P, NT, D])
        xT = m.sb("xT", [P, 2, KD, ST])
        st, mv, rs = m.sb("st", [P, NT, 6]), m.sb("mv", [P, NT, 2]), m.sb("rs", [P, 2, NT])
        half, half_set = m.sb("half", [P, NT]), m.sem("half_set")
        val = m.sb("val", [P, 4, ST])
        rest = m.sb("rest", [P, 4, ST])
        part = m.sb("part", [P, 4, 3, ST], BF16)
        va = m.sb("va", [P, 2, NT, AH, VW])
        psT = m.ps("psT", [P, KD, ST])
        psQ = m.ps("psQ", [P, 4, ST])
        psV = m.ps("psV", [P, NT, D])
        w_in, x_in = m.sem("w_in"), m.sems("x_in", 2)
        ln_step, xn_ready, turned, xT_ready = m.sem("ln_step"), m.sem("xn_ready"), m.sem("turned"), m.sem("xT_ready")
        rs_ready, bias_ready, va_ready0 = m.sem("rs_ready"), m.sem("bias_ready"), m.sem("va_const")
        qk_done, v_done, v_taken = m.sem("qk_done"), m.sem("v_done"), m.sem("v_taken")
        val_ready, mid_ready, rest_ready, lo_ready = (m.sem(s) for s in ("val_ready", "mid_ready", "rest_ready", "lo_ready"))
        part_out, v_out = m.sems("part_out", 4), m.sems("v_out", 2)
        xv = tokens(x)
        block = ctx.enter_context(nc.Block())

        @block.sync
        def _(sp):
            sp.dma_start(xin[:, 0, :, :], xv[0]).then_inc(x_in[0], 16)
            sp.dma_start(ident[:, :], ident_d).then_inc(w_in, 16)
            sp.dma_start(w[:, :, :], w_t.rearrange("(k p) o -> p k o", p=P)).then_inc(w_in, 16)
            sp.dma_start(b_in[:, :], bias_cols[:, 0:2 * KD]).then_inc(w_in, 16)
            sp.dma_start(b_v[:, :], row(bias[2 * D:3 * D])).then_inc(w_in, 16)
            sp.dma_start(xin[:, 1, :, :], xv[1]).then_inc(x_in[1], 16)

            def body(i, u, last):
                if not (isinstance(i, int) and i >= NST - 2):
                    sp.wait_ge(xn_ready, NT * (i + 1))
                    sp.dma_start(xin[:, u, :, :], xv[i + 2]).then_inc(x_in[u], 16)
                for mt in range(4):
                    sp.wait_ge(lo_ready, 4 * i + mt + 1)
                    for g in range(2):
                        sp.dma_start(parts[mt // 2, i, 2 * (mt % 2) + g].rearrange("a c t -> c a t"),
                                     part[64 * g:64 * g + 64, mt, :, :]).then_inc(part_out[mt], 16)
                sp.wait_ge(v_taken, NT * (i + 1))
                for n in range(NT):
                    sp.dma_start(v_aug[i, n].rearrange("g p c -> p g c"),
                                 va[:, u, n, :, :].rearrange("p (g h) c -> p g (h c)", g=NG)).then_inc(v_out[u], 16)

            over_supertiles(sp, body)
            for s in part_out:
                sp.wait_ge(s, 32 * NST)
            for s in v_out:
                sp.wait_ge(s, 16 * NT * NST // 2)

        @block.vector
        def _(dve):
            s = Steps(LN)
            for u in range(2):
                nc.vector.memset(va[:, u, :, :, AD:AD + 1], 1.0).then_inc(va_ready0, 1)
                nc.vector.memset(va[:, u, :, :, AD + 1:VW], 0.0).then_inc(va_ready0, 1)
            dve.wait_ge(w_in, 64)
            nc.vector.tensor_scalar(b_qk[:, 0:KD], b_in[:, 0:KD], AD ** -0.5, None, ALU.mult).then_inc(bias_ready, 1)
            nc.vector.tensor_copy(b_qk[:, KD:2 * KD], b_in[:, KD:2 * KD]).then_inc(bias_ready, 1)
            dve.wait_ge(va_ready0, 4)

            def pre(i, u):
                s.start(i)
                dve.wait_ge(x_in[u], 8 * (i - u) + 16)
                if not first(i, 1):
                    dve.wait_ge(turned, KD * i)
                normalize_tiles(nc, dve, xin[:, u, :, :], xn, st, mv, rs, ln_step, s, rs_ready, i + 1, xn_ready)
                s.end()

            pre(0, 0)

            def body(i, u, last):
                if not last:
                    pre(i + 1, 1 - u)
                for mt in range(4):
                    dve.wait_ge(val_ready, 2 * (4 * i + mt) + 2)
                    if not first(i, 1):
                        dve.wait_ge(lo_ready, 4 * (i - 1) + mt + 1)
                    nc.vector.tensor_tensor(rest[:, mt, :], val[:, mt, :], part[:, mt, 0, :],
                                            ALU.subtract).then_inc(rest_ready, 1)
                for n in range(NT):
                    dve.wait_ge(v_done, 2 * i + n // 2 + 1)
                    if n == 0 and not first(i, 2):
                        dve.wait_ge(v_out[u], 8 * NT * (i - u))
                    nc.vector.tensor_tensor(va[:, u, n, :, 0:AD],
                                            psV[:, n, :].rearrange("p (h d) -> p h d", d=AD),
                                            b_v[:, :].rearrange("p (h d) -> p h d", d=AD),
                                            ALU.add).then_inc(v_taken, 1)

            over_supertiles(dve, body)

        @block.tensor
        def _(pe):
            pe.wait_ge(w_in, 64)

            def turn_in(i):
                pe.wait_ge(xn_ready, NT * (i + 1))
                if not first(i, 1):
                    pe.wait_ge(xT_ready, KD * i)
                for k in range(KD):
                    turn(nc, xn, psT[:, k, :], ident, k).then_inc(turned, 1)

            turn_in(0)

            def body(i, u, last):
                pe.wait_ge(xT_ready, KD * (i + 1))
                for mt in range(4):
                    if not first(i, 1):
                        pe.wait_ge(val_ready, 2 * (4 * (i - 1) + mt) + 2)
                    for k in range(KD):
                        mm = pe.matmul(psQ[:, mt, :], w[:, k, mt * P:(mt + 1) * P], xT[:, u, k, :],
                                       start=(k == 0), stop=(k == KD - 1))
                    mm.then_inc(qk_done, 1)
                if not last:
                    turn_in(i + 1)
                for n in range(NT):
                    if n % 2 == 0 and not first(i, 1):
                        pe.wait_ge(v_taken, NT * (i - 1) + n + 2)
                    for k in range(KD):
                        mm = pe.matmul(psV[:, n, :], xT[:, u, k, n * P:(n + 1) * P], w[:, k, 2 * D:3 * D],
                                       start=(k == 0), stop=(k == KD - 1))
                    if n % 2:
                        mm.then_inc(v_done, 1)

            over_supertiles(pe, body)

        @block.scalar
        def _(act):
            def take_turned(i, u):
                for k in range(KD):
                    act.wait_ge(turned, KD * i + k + 1)
                    nc.scalar.copy(xT[:, u, k, :], psT[:, k, :]).then_inc(xT_ready, 1)

            take_turned(0, 0)
            act.wait_ge(bias_ready, 2)

            def body(i, u, last):
                for mt in range(4):
                    act.wait_ge(qk_done, 4 * i + mt + 1)
                    if not first(i, 1):
                        act.wait_ge(part_out[mt], 32 * i)
                    scale = AD ** -0.5 if mt < KD else 1.0
                    nc.scalar.activation(val[:, mt, :], psQ[:, mt, :], ACT.Identity, bias=b_qk[:, mt:mt + 1],
                                         scale=scale).then_inc(val_ready, 1)
                    nc.scalar.activation(part[:, mt, 0, :], psQ[:, mt, :], ACT.Identity,
                                         bias=b_qk[:, mt:mt + 1], scale=scale).then_inc(val_ready, 1)
                    if mt:
                        act.wait_ge(rest_ready, 4 * i + mt)
                        nc.scalar.copy(part[:, mt - 1, 1, :], rest[:, mt - 1, :]).then_inc(mid_ready, 1)
                act.wait_ge(rest_ready, 4 * i + 4)
                nc.scalar.copy(part[:, 3, 1, :], rest[:, 3, :]).then_inc(mid_ready, 1)
                if not last:
                    take_turned(i + 1, 1 - u)

            over_supertiles(act, body)

        @block.gpsimd
        def _(pool):
            minus_half(nc, pool, half, half_set)
            inverse_root(nc, pool, rs, half, ln_step, LN, rs_ready)

            def body(i, u, last):
                if not last:
                    inverse_root(nc, pool, rs, half, ln_step, LN * (i + 2), rs_ready)
                for mt in range(4):
                    pool.wait_ge(mid_ready, 4 * i + mt + 1)
                    nc.gpsimd.tensor_tensor(part[:, mt, 2, :], rest[:, mt, :], part[:, mt, 1, :],
                                            ALU.subtract).then_inc(lo_ready, 1)

            over_supertiles(pool, body)


def phase_attention(nc, parts, v_aug, ident_d, att):
    with ExitStack() as ctx:
        m = Place(nc, ctx, "att")
        q = m.sb("q", [P, NG, QH, HG, ST], BF16)
        k = m.sb("k", [P, NG, HG, SEQ], BF16)
        v = m.sb("v", [P, NG, KT, HG * VW])
        ident, ident_b = m.sb("ident", [P, P]), m.sb("ident_b", [P, P], BF16)
        pt = m.sb("pt", [P, 2, HG, ST])
        mx = m.sb("mx", [P, HG, NT])
        mrest = m.sb("mrest", [P, HG * NT])
        mparts = m.sb("mparts", [P, 3, 32], BF16)
        mrow = m.sb("mrow", [3 * 32, P], BF16)
        osb = m.sb("osb", [P, ST])
        rden = m.sb("rden", [P, NT, HG])
        o = m.sb("o", [P, NT, HG, AD])
        psM = m.ps("psM", [P, 2, SEQ])
        psS = m.ps("psS", [P, 2, ST])
        psO = m.ps("psO", [P, ST])
        psX = m.ps("psX", [P, NT, P])
        psX_rows = psX[:, 0, :].bitcast(BF16)
        psX_heads = psX[:, :, :].rearrange("p n (j c) -> p n j c", c=VW)
        ident_in, ident_ready, ones_set = m.sem("ident_in"), m.sem("ident_ready"), m.sem("ones_set")
        stack_in = m.sems("stack_in", NG)
        maxima_done, maxima_free = m.sem("maxima_done"), m.sem("maxima_free")
        scores_done, exp_done = m.sem("scores_done"), m.sem("exp_done")
        pv_done = m.sem("pv_done")
        split, rows_turned, rows_ready, rows_in = (m.sem(s) for s in ("split", "rows_turned", "rows_ready", "rows_in"))
        osb_ready, o_turned, rden_ready, o_ready, o_out = (
            m.sem(s) for s in ("osb_ready", "o_turned", "rden_ready", "o_ready", "o_out"))
        att_v = tokens(att)
        CREDIT = 2
        OUT_STEP = 5
        OUT_AFTER = 2 * (OUT_STEP + 1)
        TILES = HG * NT
        LOADS = 16 * (2 * QH * len(Q_PART) + QH)
        block = ctx.enter_context(nc.Block())

        def over_pairs(eng, body):
            for g in range(NG):
                body(0, g, False)
            with eng.Fori(1, BATCH - 1) as b:
                for g in range(NG):
                    body(b, g, False)
            for g in range(NG):
                body(BATCH - 1, g, g == NG - 1)

        def after(b, g):
            return (b, g + 1) if g < NG - 1 else (b + 1, 0)

        @block.sync
        def _(sp):
            sp.dma_start(ident[:, :], ident_d).then_inc(ident_in, 16)

            def load(b, g):
                for slot in range(len(Q_PART)):
                    rows = slice(AD * slot, AD * (slot + 1))
                    for s in range(QH):
                        for t, dst, which in ((0, q[rows, g, s, :, :], Q_PART),
                                              (1, k[rows, g, :, s * ST:(s + 1) * ST], K_PART)):
                            sp.dma_start(dst, parts[t, 2 * b + s, g, which[slot]].rearrange("(h c) t -> c h t", c=AD)
                                         ).then_inc(stack_in[g], 16)
                for s in range(QH):
                    sp.dma_start(v[:, g, s * NT:(s + 1) * NT, :],
                                 v_aug[2 * b + s, :, g].rearrange("n p c -> p n c")).then_inc(stack_in[g], 16)

            def rows(b, g, qh):
                u = 2 * (NG * b + g) + qh
                sp.wait_ge(rows_ready, u + 1)
                for a in range(3):
                    sp.dma_start(q[STACK + a:STACK + a + 1, g, qh, :, :].rearrange("p j t -> p (j t)"),
                                 mrow[32 * a:32 * a + TILES, :]).then_inc(rows_in, 16)

            def out(b, g, qh):
                sp.wait_ge(o_ready, 2 * (NG * b + g) + qh + 1)
                sp.dma_start(att_v[2 * b + qh][:, :, HG * AD * g:HG * AD * (g + 1)],
                             o[:, :, :, :].rearrange("p n j c -> p n (j c)")).then_inc(o_out, 16)

            for g in range(NG - 1):
                load(0, g)
            rows(0, 0, 0)

            def body(b, g, last):
                rows(b, g, 1)
                nb, ng = (b, NG - 1) if g == 0 else (b + 1, g - 1)
                if not (isinstance(nb, int) and nb >= BATCH):
                    sp.wait_ge(pv_done, CREDIT + 2 * KT * (NG * b + g))
                    load(nb, ng)
                if not last:
                    rows(*after(b, g), 0)
                out(b, g, 0)
                out(b, g, 1)

            over_pairs(sp, body)
            sp.wait_ge(o_out, 16 * 2 * NBG)

        @block.vector
        def _(dve):
            nc.vector.memset(k[STACK:P, :, :, :], 1.0).then_inc(ones_set, 1)
            nc.vector.memset(mparts[:, :, :], 0.0).then_inc(maxima_free, CREDIT)
            nc.vector.memset(mrest[:, :], 0.0).then_inc(exp_done, CREDIT)
            nc.vector.memset(rden[:, :, :], 0.0).then_inc(pv_done, CREDIT)
            dve.wait_ge(ident_in, 16)
            nc.vector.tensor_copy(ident_b[:, :], ident[:, :]).then_inc(ident_ready, 1)

            def maxima(b, g, qh, tiles):
                u = 2 * (NG * b + g) + qh
                for t in tiles:
                    dve.wait_ge(maxima_done, TILES * u + t + 1)
                    nc.vector.tensor_reduce(mx[:, t // NT, t % NT:t % NT + 1], psM[:, t % 2, :], AX.X,
                                            ALU.max).then_inc(maxima_free, 1)

            def split_maxima(b, g, qh):
                u = 2 * (NG * b + g) + qh
                x = mx[:, :, :].rearrange("p j n -> p (j n)")
                dve.wait_ge(maxima_free, CREDIT + TILES * (u + 1))
                wait_past(dve, rows_turned, u)
                nc.vector.tensor_scalar(mparts[:, 0, 0:TILES], x, -1.0, None, ALU.mult).then_inc(split, 1)
                dve.wait_ge(split, 4 * u + 1)
                nc.vector.scalar_tensor_tensor(mrest[:, :], x, -1.0, mparts[:, 0, 0:TILES], ALU.mult,
                                               ALU.subtract).then_inc(split, 1)
                dve.wait_ge(split, 4 * u + 2)
                nc.vector.tensor_copy(mparts[:, 1, 0:TILES], mrest[:, :]).then_inc(split, 1)
                dve.wait_ge(split, 4 * u + 3)
                nc.vector.tensor_tensor(mparts[:, 2, 0:TILES], mrest[:, :], mparts[:, 1, 0:TILES],
                                        ALU.subtract).then_inc(split, 1)

            def normalize(u):
                dve.wait_ge(o_turned, u + 1)
                nc.vector.reciprocal(rden[:, :, :], psX_heads[:, :, :, AD]).then_inc(rden_ready, 1)
                dve.wait_ge(rden_ready, u + 1)
                wait_past(dve, o_out, 16 * u)
                nc.vector.tensor_tensor(
                    o[:, :, :, :], psX_heads[:, :, :, 0:AD],
                    rden[:, :, :].rearrange("p n (j c) -> p n j c", c=1).to_broadcast([P, NT, HG, AD]),
                    ALU.mult).then_inc(o_ready, 1)

            for qh in range(QH):
                maxima(0, 0, qh, range(TILES))
                split_maxima(0, 0, qh)

            def body(b, g, last):
                nb, ng = after(b, g)
                for qh in range(QH):
                    if not last:
                        maxima(nb, ng, qh, range(OUT_AFTER))
                    if not (isinstance(b, int) and b == 0 and g == 0 and qh == 0):
                        normalize(2 * (NG * b + g) + qh - 1)
                    if not last:
                        maxima(nb, ng, qh, range(OUT_AFTER, TILES))
                        split_maxima(nb, ng, qh)

            over_pairs(dve, body)
            normalize(2 * NBG - 1)

        @block.tensor
        def _(pe):
            def maxima_tile(b, g, qh, t):
                u = 2 * (NG * b + g) + qh
                j, n = t // NT, t % NT
                queries = q[0:STACK, g, qh, j, n * P:(n + 1) * P]

                def half(c):
                    if c == 0:
                        pe.wait_ge(maxima_free, TILES * u + t + 1)
                    mm = pe.matmul(psM[:, t % 2, c * ST:(c + 1) * ST], queries,
                                   k[0:STACK, g, j, c * ST:(c + 1) * ST], start=True, stop=True)
                    if c == 1:
                        mm.then_inc(maxima_done, 1)
                return half

            def scores(g, qh, u, s, j):
                t = 4 * (KT * u + s) + j
                pe.wait_ge(exp_done, t + 1)
                pe.matmul(psS[:, j % 2, :], k[0:ROWS, g, j, s * P:(s + 1) * P],
                          q[0:ROWS, g, qh, j, :], start=True, stop=True).then_inc(scores_done, 1)

            def values(g, u, s):
                pe.wait_ge(exp_done, CREDIT + 4 * (KT * u + s) + 4)
                if s == 0:
                    wait_past(pe, osb_ready, u)
                for j in range(HG):
                    mm = pe.matmul(psO[VW * j:VW * (j + 1), :], v[:, g, s, VW * j:VW * (j + 1)],
                                   pt[:, s % 2, j, :], start=(s == 0), stop=(s == KT - 1),
                                   tile_position=(0, VW * j))
                mm.then_inc(pv_done, 1)

            def turn_rows(u):
                pe.wait_ge(split, 4 * (u + 1))
                pe.transpose(psX_rows[0:3 * 32, 0:P], mparts[:, :, :].rearrange("p a t -> p (a t)"),
                             ident_b[:, :]).then_inc(rows_turned, 1)

            def turn_out(u):
                pe.wait_ge(osb_ready, u + 1)
                for n in range(NT):
                    mm = pe.transpose(psX[:, n, :], osb[:, n * P:(n + 1) * P], ident[:, :])
                mm.then_inc(o_turned, 1)

            pe.wait_ge(ident_ready, 1)
            pe.wait_ge(ones_set, 1)
            pe.wait_ge(stack_in[0], LOADS)
            for qh in range(QH):
                for t in range(TILES):
                    half = maxima_tile(0, 0, qh, t)
                    half(0)
                    half(1)
            turn_rows(0)

            def body(b, g, last):
                p = NG * b + g
                nb, ng = after(b, g)
                start = isinstance(b, int) and b == 0 and g == 0
                if not last:
                    pe.wait_ge(stack_in[ng], LOADS * (nb + 1))
                for qh in range(QH):
                    u = 2 * p + qh
                    final = last and qh == 1
                    pe.wait_ge(rows_in, 16 * 3 * (u + 1))
                    for s in range(KT):
                        if s == 2 and not final:
                            pe.wait_ge(rows_ready, u + 1)
                            if not (start and qh == 0):
                                wait_past(pe, o_ready, u - 1)
                            turn_rows(u + 1)
                        if s == OUT_STEP and not (start and qh == 0):
                            pe.wait_ge(rows_ready, u + 1 if final else u + 2)
                            turn_out(u - 1)
                        for j in range(HG):
                            scores(g, qh, u, s, j)
                            if not last:
                                maxima_tile(nb, ng, qh, 2 * s + j // 2)(j % 2)
                            if j == 1:
                                if s:
                                    values(g, u, s - 1)
                                elif not (start and qh == 0):
                                    values(g if qh else (g - 1) % NG, u - 1, KT - 1)

            over_pairs(pe, body)
            values(NG - 1, 2 * NBG - 1, KT - 1)
            pe.wait_ge(o_ready, 2 * NBG - 1)
            turn_out(2 * NBG - 1)

        @block.scalar
        def _(act):
            def copy_rows(u):
                act.wait_ge(rows_turned, u + 1)
                wait_past(act, rows_in, 16 * 3 * u)
                nc.scalar.copy(mrow[:, :], psX_rows[0:3 * 32, 0:P]).then_inc(rows_ready, 1)

            copy_rows(0)

            def copy_outputs(u):
                act.wait_ge(pv_done, CREDIT + KT * (u + 1))
                wait_past(act, o_turned, u)
                nc.scalar.copy(osb[:, :], psO[:, :]).then_inc(osb_ready, 1)

            def body(b, g, last):
                for qh in range(QH):
                    u = 2 * (NG * b + g) + qh
                    for s in range(KT):
                        act.wait_ge(pv_done, KT * u + s + 1)
                        for j in range(HG):
                            act.wait_ge(scores_done, 4 * (KT * u + s) + j + 1)
                            nc.scalar.activation(pt[:, s % 2, j, :], psS[:, j % 2, :], ACT.Exp).then_inc(exp_done, 1)
                            if s == 0 and j == 2 and not (isinstance(b, int) and b == 0 and g == 0 and qh == 0):
                                copy_outputs(u - 1)
                        if s == 3 and not (last and qh == 1):
                            copy_rows(u + 1)

            over_pairs(act, body)
            copy_outputs(2 * NBG - 1)


def phase_project_ffn(nc, x, att, wo_t, bo, w1_t, b1_cols, w2_t, b2, ident_d, x_out):
    with ExitStack() as ctx:
        m = Place(nc, ctx, "ffn")
        wo, b_o = m.sb("wo", [P, KD, D]), m.sb("b_o", [P, D])
        w1, w2 = m.sb("w1", [P, KD * FF]), m.sb("w2", [P, FT * D])
        t1, t2 = m.sb("t1", [P, KD, FF], F32R), m.sb("t2", [P, FT, D], F32R)
        wx = m.sb("wx", [P, FF * KD])
        part_sum, total = m.sb("part_sum", [P, 2, 65]), m.sb("total", [P, 2, 2])
        ones, ident = m.sb("ones", [P, P]), m.sb("ident", [P, P])
        b_h, b_y = m.sb("b_h", [P, FT]), m.sb("b_y", [P, D])
        half, half_set = m.sb("half", [P, NT]), m.sem("half_set")
        xin, ain = m.sb("xin", [P, NT, D]), m.sb("ain", [P, 2, NT, D])
        aT = m.sb("aT", [P, KD, ST])
        st1, mv1, rs1 = m.sb("st1", [P, NT, 6]), m.sb("mv1", [P, NT, 2]), m.sb("rs1", [P, 2, NT])
        st2, mv2, rs2 = m.sb("st2", [P, NT, 6]), m.sb("mv2", [P, NT, 2]), m.sb("rs2", [P, 2, NT])
        st3, mv3, rs3 = m.sb("st3", [P, NT, 6]), m.sb("mv3", [P, NT, 2]), m.sb("rs3", [P, 2, NT])
        a, an, x1 = m.sb("a", [P, NT, D]), m.sb("an", [P, NT, D]), m.sb("x1", [P, 2, NT, D])
        xn = m.sb("xn", [P, NT, D])
        xhi, xlo = m.sb("xhi", [P, 2, KD, ST], F32R), m.sb("xlo", [P, 2, KD, ST], F32R)
        h = m.sb("h", [P, 4, ST])
        hhi, hlo = m.sb("hhi", [P, 2, FT, ST], F32R), m.sb("hlo", [P, 2, FT, ST], F32R)
        y, yn, xo = m.sb("y", [P, NT, D]), m.sb("yn", [P, NT, D]), m.sb("xo", [P, 2, NT, D])
        psT = m.ps("psT", [P, KD, ST])
        psA = m.ps("psA", [P, NT, D])
        psH = m.ps("psH", [P, 2, ST])
        psY = m.ps("psY", [P, NT, D])
        const_in, w_in, x_in, a_in = m.sem("const_in"), m.sems("w_in", 2), m.sem("x_in"), m.sems("a_in", 2)
        ones_set, prep, summed, w_ready = m.sem("ones_set"), m.sem("prep"), m.sem("summed"), m.sem("w_ready")
        abs_ready = m.sem("abs_ready")
        a_turned, aT_ready, a_done, a_taken = m.sem("a_turned"), m.sem("aT_ready"), m.sem("a_done"), m.sem("a_taken")
        stats1, rs1_ready, an_ready, x1_ready = m.sem("stats1"), m.sem("rs1_ready"), m.sem("an_ready"), m.sem("x1_ready")
        stats2, rs2_ready, xn_ready = m.sem("stats2"), m.sem("rs2_ready"), m.sem("xn_ready")
        stats3, rs3_ready, yn_ready = m.sem("stats3"), m.sem("rs3_ready"), m.sem("yn_ready")
        x_turned, xhi_ready, xlo_ready = m.sem("x_turned"), m.sem("xhi_ready"), m.sem("xlo_ready")
        h_done, hhi_ready = m.sem("h_done"), m.sem("hhi_ready")
        hlo_even, hlo_odd = m.sem("hlo_even"), m.sem("hlo_odd")
        y_done, y_taken, residual_ready = m.sem("y_done"), m.sem("y_taken"), m.sem("residual_ready")
        xo_ready, x_outd = m.sem("xo_ready"), m.sems("x_out", 2)
        xv, av, ov = tokens(x), tokens(att), tokens(x_out)
        F2 = FT // 2
        N_CONST = 16 * 5
        block = ctx.enter_context(nc.Block())

        @block.sync
        def _(sp):
            sp.dma_start(ain[:, 0, :, :], av[0]).then_inc(a_in[0], 16)
            sp.dma_start(ident[:, :], ident_d).then_inc(const_in, 16)
            sp.dma_start(wo[:, :, :], wo_t.rearrange("(k p) o -> p k o", p=P)).then_inc(const_in, 16)
            sp.dma_start(b_o[:, :], row(bo)).then_inc(const_in, 16)
            sp.dma_start(w1[:, :].rearrange("p (k o) -> p k o", k=KD), w1_t.rearrange("(k p) o -> p k o", p=P)
                         ).then_inc(w_in[0], 16)
            sp.dma_start(xin[:, :, :], xv[0]).then_inc(x_in, 16)
            sp.dma_start(ain[:, 1, :, :], av[1]).then_inc(a_in[1], 16)
            sp.dma_start(w2[:, :].rearrange("p (k o) -> p k o", k=FT), w2_t.rearrange("(k p) o -> p k o", p=P)
                         ).then_inc(w_in[1], 16)
            sp.dma_start(b_h[:, :], b1_cols).then_inc(const_in, 16)
            sp.dma_start(b_y[:, :], row(b2)).then_inc(const_in, 16)

            sp.wait_ge(x1_ready, 1)
            sp.dma_start(xin[:, :, :], xv[1]).then_inc(x_in, 16)

            def body(i, u, last):
                more = not (isinstance(i, int) and i >= NST - 2)
                if more:
                    sp.wait_ge(a_turned, KD * (i + 1))
                    sp.dma_start(ain[:, u, :, :], av[i + 2]).then_inc(a_in[u], 16)
                if not first(i, 2):
                    sp.wait_ge(xo_ready, i - 1)
                    sp.dma_start(ov[i - 2], xo[:, u, :, :]).then_inc(x_outd[u], 16)
                if more:
                    sp.wait_ge(x1_ready, i + 2)
                    sp.dma_start(xin[:, :, :], xv[i + 2]).then_inc(x_in, 16)

            over_supertiles(sp, body)
            for i in (NST - 2, NST - 1):
                sp.wait_ge(xo_ready, i + 1)
                sp.dma_start(ov[i], xo[:, i % 2, :, :]).then_inc(x_outd[i % 2], 16)
            for s in x_outd:
                sp.wait_ge(s, 16 * NST // 2)

        @block.vector
        def _(dve):
            s1, s2, s3, t = Steps(LN), Steps(LN), Steps(LN), Steps(0)
            nc.vector.memset(ones[:, :], 1.0).then_inc(ones_set, 1)

            def take_projected(i):
                s1.start(i)
                dve.wait_ge(a_done, i + 1)
                if not first(i, 1):
                    dve.wait_ge(an_ready, NT * i)
                for n in range(NT):
                    nc.vector.tensor_tensor(a[:, n, :], psA[:, n, :], b_o[:, :], ALU.add).then_inc(a_taken, 1)
                dve.wait_ge(a_taken, NT * (i + 1))
                tile_stats(nc, dve, a, st1, mv1, rs1, stats1, s1)
                s1.end()

            def normalize_projected(i):
                if not first(i, 1):
                    dve.wait_ge(x1_ready, i)
                normalize_with(nc, dve, a, an, mv1, rs1, rs1_ready, i + 1, an_ready)

            def stats_of_x1(i, u):
                s2.start(i)
                dve.wait_ge(x1_ready, i + 1)
                tile_stats(nc, dve, x1[:, u, :, :], st2, mv2, rs2, stats2, s2)
                s2.end()

            def normalize_x1(i, u):
                if not first(i, 1):
                    dve.wait_ge(x_turned, KD * i)
                normalize_with(nc, dve, x1[:, u, :, :], xn, mv2, rs2, rs2_ready, i + 1, xn_ready)

            def take_turned(i, u):
                for k in range(KD):
                    dve.wait_ge(xhi_ready, KD * i + k + 1)
                    if k == 0 and not first(i, 2):
                        dve.wait_ge(h_done, FT * (i - 1))
                    nc.vector.tensor_tensor(xlo[:, u, k, :], psT[:, k, :], xhi[:, u, k, :],
                                            ALU.subtract).then_inc(xlo_ready, 1)

            def split_hidden(i, u, f):
                if f % 2 == 0:
                    dve.wait_ge(hhi_ready, FT * i + f + 1)
                    if f == 0 and not first(i, 2):
                        dve.wait_ge(y_done, 2 * (i - 1))
                    nc.vector.tensor_tensor(hlo[:, u, f, :], h[:, f % 4, :], hhi[:, u, f, :],
                                            ALU.subtract).then_inc(hlo_even, 1)

            def ternary(n, w, tern):
                dve.wait_ge(abs_ready, n + 1)
                nc.vector.tensor_reduce(part_sum[:, n, 0:64], wx[:, :].rearrange("p (a b) -> p a b", a=64), AX.X,
                                        ALU.add).then_inc(prep, t.inc())
                dve.wait_ge(prep, t.now())
                nc.vector.tensor_reduce(part_sum[:, n, 64:65], part_sum[:, n, 0:64], AX.X,
                                        ALU.add).then_inc(prep, t.inc())
                dve.wait_ge(summed, n + 1)
                nc.vector.tensor_scalar(total[:, n, 0:1], psY[:, 2 * n, 0:1], 1.0 / (FF * D), 1e-8, ALU.mult,
                                        ALU.max).then_inc(prep, t.inc())
                dve.wait_ge(prep, t.now())
                nc.vector.tensor_scalar(total[:, n, 0:1], total[:, n, 0:1], 0.5, None, ALU.mult).then_inc(prep, t.inc())
                dve.wait_ge(prep, t.now())
                nc.vector.tensor_scalar(total[:, n, 1:2], total[:, n, 0:1], -1.0, None, ALU.mult).then_inc(prep, t.inc())
                dve.wait_ge(prep, t.now())
                nc.vector.tensor_scalar(wx[:, :], w[:, :], total[:, n, 1:2], None, ALU.is_lt).then_inc(prep, t.inc())
                dve.wait_ge(prep, t.now())
                nc.vector.scalar_tensor_tensor(tern, w[:, :], total[:, n, 0:1], wx[:, :], ALU.is_gt,
                                               ALU.subtract).then_inc(w_ready, 1)

            dve.wait_ge(const_in, N_CONST)
            take_projected(0)
            normalize_projected(0)
            ternary(0, w1, t1[:, :, :].rearrange("p k o -> p (k o)"))
            stats_of_x1(0, 0)
            normalize_x1(0, 0)
            take_turned(0, 0)
            take_projected(1)
            ternary(1, w2, t2[:, :, :].rearrange("p k o -> p (k o)"))

            def take_y(i, pair):
                dve.wait_ge(y_done, 2 * i + pair + 1)
                if pair == 0 and not first(i, 1):
                    dve.wait_ge(yn_ready, NT * i)
                tiles = slice(2 * pair, 2 * pair + 2)
                nc.vector.tensor_tensor(y[:, tiles, :], psY[:, tiles, :],
                                        b_y[:, :].rearrange("p (n c) -> p n c", n=1).to_broadcast([P, 2, D]),
                                        ALU.add).then_inc(y_taken, 1)

            def stats_of_y(i):
                s3.start(i)
                dve.wait_ge(y_taken, 2 * (i + 1))
                tile_stats(nc, dve, y, st3, mv3, rs3, stats3, s3)
                s3.end()

            def normalize_y(i):
                if not first(i, 1):
                    dve.wait_ge(xo_ready, i)
                normalize_with(nc, dve, y, yn, mv3, rs3, rs3_ready, i + 1, yn_ready)

            def body(i, u, last):
                if not last:
                    normalize_projected(i + 1)
                for f in range(FT):
                    split_hidden(i, u, f)
                    if f == 2 and not last:
                        stats_of_x1(i + 1, 1 - u)
                    if f == 4 and not last:
                        normalize_x1(i + 1, 1 - u)
                    if f == 5 and not first(i, 1):
                        take_y(i - 1, 0)
                if not last:
                    take_turned(i + 1, 1 - u)
                if not first(i, 1):
                    take_y(i - 1, 1)
                    stats_of_y(i - 1)
                if not (isinstance(i, int) and i >= NST - 2):
                    take_projected(i + 2)
                if not first(i, 1):
                    normalize_y(i - 1)

            over_supertiles(dve, body)
            take_y(NST - 1, 0)
            take_y(NST - 1, 1)
            stats_of_y(NST - 1)
            normalize_y(NST - 1)

        @block.tensor
        def _(pe):
            def turn_projected(i, u):
                pe.wait_ge(a_in[u], 8 * (i - u) + 16)
                if first(i, 2):
                    wait_past(pe, aT_ready, KD * i)
                else:
                    pe.wait_ge(xlo_ready, KD * (i - 1))
                for k in range(KD):
                    turn(nc, ain[:, u, :, :], psT[:, k, :], ident, k).then_inc(a_turned, 1)

            def multiply_projected(i):
                pe.wait_ge(aT_ready, KD * (i + 1))
                if not first(i, 1):
                    pe.wait_ge(a_taken, NT * i)
                for n in range(NT):
                    for k in range(KD):
                        mm = pe.matmul(psA[:, n, :], aT[:, k, n * P:(n + 1) * P], wo[:, k, :],
                                       start=(k == 0), stop=(k == KD - 1))
                mm.then_inc(a_done, 1)

            def turn_x(i):
                pe.wait_ge(xn_ready, NT * (i + 1))
                pe.wait_ge(aT_ready, KD * NST if isinstance(i, int) and i == NST - 1 else KD * (i + 2))
                for k in range(KD):
                    turn(nc, xn, psT[:, k, :], ident, k).then_inc(x_turned, 1)

            def sum_weights(n):
                pe.wait_ge(prep, 6 * n + 2)
                pe.matmul(psY[:, 2 * n, 0:1], ones[:, :], part_sum[:, n, 64:65], start=True,
                          stop=True).then_inc(summed, 1)

            def hidden(i, u, f):
                if not (first(i, 1) and f < 2):
                    pe.wait_ge(hhi_ready, FT * i + f - 1)
                for k in range(KD):
                    w = t1[:, k, f * P:(f + 1) * P]
                    pe.matmul(psH[:, f % 2, :], w, xhi[:, u, k, :], start=(k == 0), stop=False)
                    mm = pe.matmul(psH[:, f % 2, :], w, xlo[:, u, k, :], start=False, stop=(k == KD - 1))
                mm.then_inc(h_done, 1)

            def y_part(i, u, n, part):
                cols = slice(n * P, (n + 1) * P)
                if part == 0 and n % 2 == 0 and not first(i, 1):
                    pe.wait_ge(y_taken, 2 * (i - 1) + n // 2 + 1)
                for f in range(F2 * part, F2 * (part + 1)):
                    if n == 0:
                        pe.wait_ge(hlo_odd if f % 2 else hlo_even, F2 * i + f // 2 + 1)
                    pe.matmul(psY[:, n, :], hhi[:, u, f, cols], t2[:, f, :], start=(f == 0), stop=False)
                    mm = pe.matmul(psY[:, n, :], hlo[:, u, f, cols], t2[:, f, :], start=False, stop=(f == FT - 1))
                if part and n % 2:
                    mm.then_inc(y_done, 1)

            pe.wait_ge(const_in, N_CONST)
            turn_projected(0, 0)
            multiply_projected(0)
            turn_projected(1, 1)
            pe.wait_ge(ones_set, 1)
            sum_weights(0)
            turn_x(0)
            multiply_projected(1)
            sum_weights(1)
            pe.wait_ge(w_ready, 1)
            pe.wait_ge(xlo_ready, KD)

            def body(i, u, last):
                more = not (isinstance(i, int) and i >= NST - 2)
                if not first(i, 1):
                    pe.wait_ge(xlo_ready, KD * (i + 1))
                hidden(i, u, 0)
                for f in range(1, FT):
                    hidden(i, u, f)
                    if f == 3 and more:
                        turn_projected(i + 2, u)
                    if not first(i, 1) and f < FT - 1:
                        y_part(i - 1, 1 - u, (f - 1) // 2, (f - 1) % 2)
                if first(i, 1):
                    pe.wait_ge(w_ready, 2)
                if not last:
                    turn_x(i + 1)
                if not first(i, 1):
                    y_part(i - 1, 1 - u, NT - 1, 0)
                    y_part(i - 1, 1 - u, NT - 1, 1)
                if more:
                    multiply_projected(i + 2)

            over_supertiles(pe, body)
            for n in range(NT):
                for part in range(2):
                    y_part(NST - 1, 1, n, part)

        @block.scalar
        def _(act):
            def copy_projected(i):
                for k in range(KD):
                    act.wait_ge(a_turned, KD * i + k + 1)
                    if k == 0 and not first(i, 1):
                        act.wait_ge(a_done, i)
                    nc.scalar.copy(aT[:, k, :], psT[:, k, :]).then_inc(aT_ready, 1)

            def take_turned(i, u):
                for k in range(KD):
                    act.wait_ge(x_turned, KD * i + k + 1)
                    nc.scalar.copy(xhi[:, u, k, :], psT[:, k, :]).then_inc(xhi_ready, 1)

            def copy_residual(i, u):
                act.wait_ge(x1_ready, i + 1)
                if not first(i, 2):
                    act.wait_ge(x_outd[u], 8 * (i - u))
                nc.scalar.copy(xo[:, u, :, :], x1[:, u, :, :]).then_inc(residual_ready, 1)

            copy_projected(0)
            copy_projected(1)
            for n, w in ((0, w1), (1, w2)):
                act.wait_ge(w_in[n], 16)
                if n:
                    act.wait_ge(w_ready, n)
                nc.scalar.activation(wx[:, :], w[:, :], ACT.Abs).then_inc(abs_ready, 1)
                if n == 0:
                    take_turned(0, 0)

            def body(i, u, last):
                more = not (isinstance(i, int) and i >= NST - 2)
                for f in range(FT):
                    act.wait_ge(h_done, FT * i + f + 1)
                    if not (first(i, 1) and f < 4):
                        act.wait_ge(hlo_odd if f % 2 else hlo_even, F2 * i + f // 2 - 1)
                    nc.scalar.activation(h[:, f % 4, :], psH[:, f % 2, :], ACT.Gelu, bias=b_h[:, f:f + 1])
                    if f == 0 and not first(i, 2):
                        act.wait_ge(y_done, 2 * (i - 1))
                    nc.scalar.activation(hhi[:, u, f, :], psH[:, f % 2, :], ACT.Gelu,
                                         bias=b_h[:, f:f + 1]).then_inc(hhi_ready, 1)
                    if f == 3 and more:
                        copy_projected(i + 2)
                if not last:
                    take_turned(i + 1, 1 - u)
                copy_residual(i, u)

            over_supertiles(act, body)

        @block.gpsimd
        def _(pool):
            def roots(rs, stats, i, ready):
                inverse_root(nc, pool, rs, half, stats, LN * (i + 1), ready)

            def add_projected(i, u):
                pool.wait_ge(an_ready, NT * (i + 1))
                pool.wait_ge(x_in, 16 * (i + 1))
                if not first(i, 2):
                    pool.wait_ge(residual_ready, i - 1)
                    pool.wait_ge(xn_ready, NT * (i - 1))
                nc.gpsimd.tensor_tensor(x1[:, u, :, :], xin[:, :, :], an[:, :, :], ALU.add).then_inc(x1_ready, 1)

            def split_hidden(i, u, f):
                pool.wait_ge(hhi_ready, FT * i + f + 1)
                nc.gpsimd.tensor_tensor(hlo[:, u, f, :], h[:, f % 4, :], hhi[:, u, f, :], ALU.subtract).then_inc(hlo_odd, 1)

            def add_out(i, u):
                pool.wait_ge(yn_ready, NT * (i + 1))
                pool.wait_ge(residual_ready, i + 1)
                nc.gpsimd.tensor_tensor(xo[:, u, :, :], xo[:, u, :, :], yn[:, :, :], ALU.add).then_inc(xo_ready, 1)

            minus_half(nc, pool, half, half_set)
            roots(rs1, stats1, 0, rs1_ready)
            add_projected(0, 0)
            roots(rs2, stats2, 0, rs2_ready)
            roots(rs1, stats1, 1, rs1_ready)

            def body(i, u, last):
                if not last:
                    add_projected(i + 1, 1 - u)
                split_hidden(i, u, 1)
                if not last:
                    roots(rs2, stats2, i + 1, rs2_ready)
                if not first(i, 2):
                    add_out(i - 2, u)
                split_hidden(i, u, 3)
                split_hidden(i, u, 5)
                split_hidden(i, u, 7)
                if not first(i, 1):
                    roots(rs3, stats3, i - 1, rs3_ready)
                if not (isinstance(i, int) and i >= NST - 2):
                    roots(rs1, stats1, i + 2, rs1_ready)

            over_supertiles(pool, body)
            add_out(NST - 2, 0)
            roots(rs3, stats3, NST - 1, rs3_ready)
            add_out(NST - 1, 1)


def phase_experts(nc, x, gate_w, w1, b1_cols, w2, b2, ws1, bs1_col, ws2, bs2, route_scale, ident_d, x_out):
    BIG = 3.0e38
    with ExitStack() as ctx:
        m = Place(nc, ctx, "moe")
        wg = m.sb("wg", [P, KD, NE])
        wa, wb = m.sb("wa", [P, KD, NE + 1, EH]), m.sb("wb", [P, NE + 1, D])
        wa_hi, wa_lo = m.sb("wa_hi", [P, KD, NE + 1, EH], F32R), m.sb("wa_lo", [P, KD, NE + 1, EH], F32R)
        wb_hi, wb_lo = m.sb("wb_hi", [P, NE + 1, D], F32R), m.sb("wb_lo", [P, NE + 1, D], F32R)
        b_h, b_e, b_s = m.sb("b_h", [P, NE + 1]), m.sb("b_e", [NE, D]), m.sb("b_s", [P, D])
        r_scale, order = m.sb("r_scale", [P, 1]), m.sb("order", [P, NT, NE])
        ident = m.sb("ident", [P, P])
        half, half_set = m.sb("half", [P, NT]), m.sem("half_set")
        xin = m.sb("xin", [P, 2, NT, D])
        xn = m.sb("xn", [P, NT, D])
        xT = m.sb("xT", [P, KD, ST])
        xhi, xlo = m.sb("xhi", [P, 2, KD, ST], F32R), m.sb("xlo", [P, 2, KD, ST], F32R)
        h = m.sb("h", [P, 3, ST])
        hhi, hlo = m.sb("hhi", [P, 2, NE + 1, ST], F32R), m.sb("hlo", [P, 2, NE + 1, ST], F32R)
        st, mv, rs = m.sb("st", [P, NT, 6]), m.sb("mv", [P, NT, 2]), m.sb("rs", [P, 2, NT])
        st2, mv2, rs2 = m.sb("st2", [P, NT, 6]), m.sb("mv2", [P, NT, 2]), m.sb("rs2", [P, 2, NT])
        y, yn, xo = m.sb("y", [P, 2, NT, D]), m.sb("yn", [P, NT, D]), m.sb("xo", [P, 2, NT, D])
        sig, score, pick, sel1, sel2 = (m.sb(s, [P, NT, NE]) for s in ("sig", "score", "pick", "sel1", "sel2"))
        gates, gT = m.sb("gates", [P, 2, NT, NE]), m.sb("gT", [NE, 2, ST])
        best1, best2, rank = (m.sb(s, [P, NT]) for s in ("best1", "best2", "rank"))
        psT = m.ps("psT", [P, ST])
        psH = m.ps("psH", [P, 2, ST])
        psG = m.ps("psG", [P, ST])
        psX = (psT, psG)
        psY = m.ps("psY", [P, 4, 2, D])
        ident_in, const_in, w_in, x_in = m.sem("ident_in"), m.sem("const_in"), m.sems("w_in", 2), m.sems("x_in", 2)
        w_hi_ready, w_lo_ready = m.sem("w_hi_ready"), m.sem("w_lo_ready")
        stats, rs_ready, xn_ready = m.sem("stats"), m.sem("rs_ready"), m.sem("xn_ready")
        stats2, rs2_ready, yn_ready = m.sem("stats2"), m.sem("rs2_ready"), m.sem("yn_ready")
        turned, xT_ready, xlo_ready = m.sem("turned"), m.sem("xT_ready"), m.sem("xlo_ready")
        logits_done, sig_ready, route, gates_ready = m.sem("logits_done"), m.sem("sig_ready"), m.sem("route"), m.sem("gates_ready")
        g_turned, gT_ready, order_set = m.sem("g_turned"), m.sem("gT_ready"), m.sem("order_set")
        h_done, h_ready, hlo_ready = m.sem("h_done"), m.sem("h_ready"), m.sem("hlo_ready")
        y_done, y_added, y_summed, residual_ready = (m.sem(s) for s in ("y_done", "y_added", "y_summed", "residual_ready"))
        xo_ready, x_outd = m.sem("xo_ready"), m.sems("x_out", 2)
        xv, ov = tokens(x), tokens(x_out)
        E = NE + 1
        N_CONST, UNITS = 16 * 6, 1 + NE // 2
        block = ctx.enter_context(nc.Block())

        @block.sync
        def _(sp):
            sp.dma_start(xin[:, 0, :, :], xv[0]).then_inc(x_in[0], 16)
            sp.dma_start(ident[:, :], ident_d).then_inc(ident_in, 16)
            for k in range(KD):
                sp.dma_start(wa[:, k, 0:NE, :], w1[:, k * P:(k + 1) * P, :].rearrange("e p h -> p e h")).then_inc(w_in[0], 16)
            sp.dma_start(wa[:, :, NE, :], ws1.rearrange("(k p) h -> p k h", p=P)).then_inc(w_in[0], 16)
            sp.dma_start(wg[:, :, :], gate_w.rearrange("(k p) e -> p k e", p=P)).then_inc(const_in, 16)
            sp.dma_start(r_scale[:, :], route_scale.to_broadcast([P, 1])).then_inc(const_in, 16)
            sp.dma_start(b_h[:, 0:NE], b1_cols).then_inc(const_in, 16)
            sp.dma_start(b_h[:, NE:NE + 1], bs1_col).then_inc(const_in, 16)
            sp.dma_start(b_e[:, :], b2).then_inc(const_in, 16)
            sp.dma_start(b_s[:, :], row(bs2)).then_inc(const_in, 16)
            sp.dma_start(wb[:, 0:NE, :], w2.rearrange("e h d -> h e d")).then_inc(w_in[1], 16)
            sp.dma_start(wb[:, NE, :], ws2).then_inc(w_in[1], 16)
            sp.dma_start(xin[:, 1, :, :], xv[1]).then_inc(x_in[1], 16)

            def body(i, u, last):
                if not first(i, 2):
                    sp.wait_ge(xo_ready, i - 1)
                    sp.dma_start(ov[i - 2], xo[:, u, :, :]).then_inc(x_outd[u], 16)
                if not (isinstance(i, int) and i >= NST - 2):
                    sp.wait_ge(residual_ready, i + 1)
                    sp.dma_start(xin[:, u, :, :], xv[i + 2]).then_inc(x_in[u], 16)

            over_supertiles(sp, body)
            for i in (NST - 2, NST - 1):
                sp.wait_ge(xo_ready, i + 1)
                sp.dma_start(ov[i], xo[:, i % 2, :, :]).then_inc(x_outd[i % 2], 16)
            for s in x_outd:
                sp.wait_ge(s, 16 * NST // 2)

        @block.vector
        def _(dve):
            ROUTE = 1 + 5 + 2 + 5 + 4
            s, s2, r = Steps(LN), Steps(LN), Steps(ROUTE)
            for e in range(NE):
                nc.vector.memset(order[:, :, e:e + 1], float(NE - e)).then_inc(order_set, 1)

            def pre(i, u):
                s.start(i)
                dve.wait_ge(x_in[u], 8 * (i - u) + 16)
                if not first(i, 1):
                    dve.wait_ge(turned, KD * i)
                normalize_tiles(nc, dve, xin[:, u, :, :], xn, st, mv, rs, stats, s, rs_ready, i + 1, xn_ready)
                s.end()

            def wide(a):
                return a[:, :].rearrange("p (n e) -> p n e", e=1).to_broadcast([P, NT, NE])

            def choose(best, sel):
                nc.vector.tensor_reduce(best[:, :], score[:, :, :], AX.X, ALU.max).then_inc(route, r.inc())
                dve.wait_ge(route, r.now())
                nc.vector.tensor_tensor(pick[:, :, :], score[:, :, :], wide(best), ALU.is_ge).then_inc(route, r.inc())
                dve.wait_ge(route, r.now())
                nc.vector.tensor_tensor(pick[:, :, :], pick[:, :, :], order[:, :, :], ALU.mult).then_inc(route, r.inc())
                dve.wait_ge(route, r.now())
                nc.vector.tensor_reduce(rank[:, :], pick[:, :, :], AX.X, ALU.max).then_inc(route, r.inc())
                dve.wait_ge(route, r.now())
                nc.vector.tensor_tensor(sel[:, :, :], pick[:, :, :], wide(rank), ALU.is_ge).then_inc(route, r.inc())
                dve.wait_ge(route, r.now())

            def route_tokens(i, u):
                r.start(i)
                dve.wait_ge(sig_ready, i + 1)
                nc.vector.tensor_scalar(score[:, :, :], sig[:, :, :], r_scale[:, 0:1], None,
                                        ALU.mult).then_inc(route, r.inc())
                dve.wait_ge(route, r.now())
                choose(best1, sel1)
                if not first(i, 2):
                    dve.wait_ge(y_added, NT * E * (i - 1))
                    dve.wait_ge(g_turned, i - 1)
                nc.vector.tensor_tensor(gates[:, u, :, :], score[:, :, :], sel1[:, :, :], ALU.mult).then_inc(route, r.inc())
                dve.wait_ge(route, r.now())
                nc.vector.scalar_tensor_tensor(score[:, :, :], sel1[:, :, :], -BIG, score[:, :, :], ALU.mult,
                                               ALU.add).then_inc(route, r.inc())
                dve.wait_ge(route, r.now())
                choose(best2, sel2)
                nc.vector.tensor_tensor(sel2[:, :, :], score[:, :, :], sel2[:, :, :], ALU.mult).then_inc(route, r.inc())
                nc.vector.tensor_tensor(rank[:, :], best1[:, :], best2[:, :], ALU.add).then_inc(route, r.inc())
                dve.wait_ge(route, r.now())
                nc.vector.reciprocal(best1[:, :], rank[:, :]).then_inc(route, r.inc())
                nc.vector.tensor_tensor(gates[:, u, :, :], gates[:, u, :, :], sel2[:, :, :], ALU.add).then_inc(route, r.inc())
                dve.wait_ge(route, r.now())
                nc.vector.tensor_tensor(gates[:, u, :, :], gates[:, u, :, :], wide(best1), ALU.mult).then_inc(gates_ready, 1)
                r.end()

            def take_turned(i, u):
                for k in range(KD):
                    dve.wait_ge(xT_ready, KD * i + k + 1)
                    if k == 0 and not first(i, 2):
                        dve.wait_ge(h_done, E * (i - 1))
                    nc.vector.tensor_tensor(xlo[:, u, k, :], psX[k][:, :], xhi[:, u, k, :], ALU.subtract).then_inc(xlo_ready, 1)

            def add_outputs(i, u, n):
                added = NT * E * i + E * n
                if n == 0:
                    if not first(i, 1):
                        dve.wait_ge(yn_ready, NT * i)
                    dve.wait_ge(gates_ready, i + 1)
                for c in range(UNITS):
                    dve.wait_ge(y_done, UNITS * (NT * i + n) + c + 1)
                    bank = (UNITS * n + c) % 4
                    if c == 0:
                        nc.vector.tensor_tensor(y[:, 0, n, :], psY[:, bank, 0, :], b_s[:, :],
                                                ALU.add).then_inc(y_added, 1)
                        continue
                    for hf in range(2):
                        e = 2 * (c - 1) + hf
                        if e == 1:
                            nc.vector.tensor_scalar(y[:, 1, n, :], psY[:, bank, 1, :], gates[:, u, n, 1:2], None,
                                                    ALU.mult).then_inc(y_added, 1)
                            continue
                        dve.wait_ge(y_added, added + (e if e else 1))
                        nc.vector.scalar_tensor_tensor(y[:, hf, n, :], psY[:, bank, hf, :], gates[:, u, n, e:e + 1],
                                                       y[:, hf, n, :], ALU.mult, ALU.add).then_inc(y_added, 1)

            def normalize_y(i):
                s2.start(i)
                dve.wait_ge(y_added, NT * E * (i + 1))
                nc.vector.tensor_tensor(y[:, 0, :, :], y[:, 0, :, :], y[:, 1, :, :], ALU.add).then_inc(y_summed, 1)
                dve.wait_ge(y_summed, i + 1)
                if not first(i, 1):
                    dve.wait_ge(xo_ready, i)
                normalize_tiles(nc, dve, y[:, 0, :, :], yn, st2, mv2, rs2, stats2, s2, rs2_ready, i + 1, yn_ready)
                s2.end()

            pre(0, 0)
            for n, (w, hi, lo) in enumerate(((wa, wa_hi, wa_lo), (wb, wb_hi, wb_lo))):
                dve.wait_ge(w_hi_ready, n + 1)
                shape = "p k e h -> p (k e h)" if n == 0 else "p e h -> p (e h)"
                everything = (slice(None),) * len(w.shape)
                nc.vector.tensor_tensor(lo[everything].rearrange(shape), w[everything].rearrange(shape),
                                        hi[everything].rearrange(shape), ALU.subtract).then_inc(w_lo_ready, 1)
                if n == 0:
                    take_turned(0, 0)
            dve.wait_ge(const_in, N_CONST)
            dve.wait_ge(order_set, NE)

            def body(i, u, last):
                before = not first(i, 1)
                if before:
                    add_outputs(i - 1, 1 - u, 0)
                route_tokens(i, u)
                if before:
                    add_outputs(i - 1, 1 - u, 1)
                if not last:
                    pre(i + 1, 1 - u)
                if before:
                    add_outputs(i - 1, 1 - u, 2)
                if not last:
                    take_turned(i + 1, 1 - u)
                if before:
                    add_outputs(i - 1, 1 - u, 3)
                    normalize_y(i - 1)

            over_supertiles(dve, body)
            for n in range(NT):
                add_outputs(NST - 1, 1, n)
            normalize_y(NST - 1)

        @block.tensor
        def _(pe):
            def turn_in(i, k):
                if k == 0:
                    pe.wait_ge(xn_ready, NT * (i + 1))
                if not first(i, 1):
                    if k == 0:
                        pe.wait_ge(xlo_ready, KD * i)
                    else:
                        pe.wait_ge(gT_ready, i)
                turn(nc, xn, psX[k], ident, k).then_inc(turned, 1)

            def hidden(i, u, e):
                c = E * i + e
                if not (first(i, 1) and e < 2):
                    pe.wait_ge(h_ready, c - 1)
                for k in range(KD):
                    for p, (w, v) in enumerate(((wa_hi, xhi), (wa_hi, xlo), (wa_lo, xhi))):
                        mm = pe.matmul(psH[:, (e + u) % 2, :], w[:, k, e, :], v[:, u, k, :],
                                       start=(k == 0 and p == 0), stop=(k == KD - 1 and p == 2))
                mm.then_inc(h_done, 1)

            def outputs(i, u, g):
                n, c = g // UNITS, g % UNITS
                cols, bank = slice(n * P, (n + 1) * P), g % 4
                if g == 0:
                    pe.wait_ge(hlo_ready, E * (i + 1))
                    pe.wait_ge(gT_ready, i + 1)
                if not (first(i, 1) and g < 4):
                    g4 = g - 4 if g >= 4 else UNITS * NT + g - 4
                    before = E * (g4 // UNITS) + 2 * (g4 % UNITS) + 1
                    pe.wait_ge(y_added, NT * E * (i if g >= 4 else i - 1) + before)

                def product(hf, e, start):
                    for p, (v, w) in enumerate(((hhi, wb_hi), (hlo, wb_hi), (hhi, wb_lo))):
                        mm = pe.matmul(psY[:, bank, hf, :], v[:, u, e, cols], w[:, e, :], start=(start and p == 0),
                                       stop=(p == 2))
                    return mm

                if c == 0:
                    pe.matmul(psY[:, bank, 0, :], gT[:, u, cols], b_e[:, :], start=True, stop=False)
                    mm = product(0, NE, False)
                else:
                    for hf in range(2):
                        mm = product(hf, 2 * (c - 1) + hf, True)
                mm.then_inc(y_done, 1)

            pe.wait_ge(ident_in, 16)
            for k in range(KD):
                turn_in(0, k)
            pe.wait_ge(const_in, N_CONST)
            pe.wait_ge(w_lo_ready, 1)

            def body(i, u, last):
                before = not first(i, 1)
                pe.wait_ge(xT_ready, KD * (i + 1))
                pe.wait_ge(xlo_ready, KD * (i + 1))
                for n in range(NT):
                    for k in range(KD):
                        mm = pe.matmul(psG[:, n * NE:(n + 1) * NE], xT[:, k, n * P:(n + 1) * P], wg[:, k, :],
                                       start=(k == 0), stop=(k == KD - 1))
                mm.then_inc(logits_done, 1)
                for e in range(E):
                    hidden(i, u, e)
                    if before:
                        if e:
                            outputs(i - 1, 1 - u, 2 * e - 2)
                            outputs(i - 1, 1 - u, 2 * e - 1)
                    if e == 6:
                        pe.wait_ge(gates_ready, i + 1)
                        for n in range(NT):
                            mm = pe.transpose(psG[0:NE, n * P:(n + 1) * P], gates[:, u, n, :], ident[:, :])
                        mm.then_inc(g_turned, 1)
                    if e >= 7 and not last:
                        turn_in(i + 1, e - 7)
                if first(i, 1):
                    pe.wait_ge(w_lo_ready, 2)
                if before:
                    for g in range(2 * NE, UNITS * NT):
                        outputs(i - 1, 1 - u, g)

            over_supertiles(pe, body)
            for g in range(UNITS * NT):
                outputs(NST - 1, 1, g)

        @block.scalar
        def _(act):
            def take_turned(i, u, k):
                act.wait_ge(turned, KD * i + k + 1)
                if k == 0 and not first(i, 1):
                    act.wait_ge(logits_done, i)
                nc.scalar.copy(xT[:, k, :], psX[k][:, :])
                nc.scalar.copy(xhi[:, u, k, :], psX[k][:, :]).then_inc(xT_ready, 1)

            for n, (w, hi) in enumerate(((wa, wa_hi), (wb, wb_hi))):
                act.wait_ge(w_in[n], 48 if n == 0 else 32)
                everything = (slice(None),) * len(w.shape)
                nc.scalar.copy(hi[everything], w[everything]).then_inc(w_hi_ready, 1)
                if n == 0:
                    for k in range(KD):
                        take_turned(0, 0, k)
            act.wait_ge(const_in, N_CONST)

            def body(i, u, last):
                act.wait_ge(logits_done, i + 1)
                if not first(i, 1):
                    act.wait_ge(gates_ready, i)
                nc.scalar.activation(sig[:, :, :], psG[:, 0:NT * NE].rearrange("p (n e) -> p n e", e=NE),
                                     ACT.Sigmoid).then_inc(sig_ready, 1)
                for e in range(E):
                    act.wait_ge(h_done, E * i + e + 1)
                    if not (first(i, 1) and e < 3):
                        act.wait_ge(hlo_ready, E * i + e - 2)
                    if e == 0 and not first(i, 2):
                        act.wait_ge(y_done, UNITS * NT * (i - 1))
                    nc.scalar.activation(h[:, e % 3, :], psH[:, (e + u) % 2, :], ACT.Gelu, bias=b_h[:, e:e + 1])
                    nc.scalar.activation(hhi[:, u, e, :], psH[:, (e + u) % 2, :], ACT.Gelu,
                                         bias=b_h[:, e:e + 1]).then_inc(h_ready, 1)
                    if e == 6:
                        act.wait_ge(g_turned, i + 1)
                        if not first(i, 2):
                            act.wait_ge(y_done, UNITS * NT * (i - 1))
                        nc.scalar.copy(gT[:, u, :], psG[0:NE, :]).then_inc(gT_ready, 1)
                    if e >= 7 and not last:
                        take_turned(i + 1, 1 - u, e - 7)
                act.wait_ge(x_in[u], 8 * (i - u) + 16)
                if not first(i, 2):
                    act.wait_ge(x_outd[u], 8 * (i - u))
                nc.scalar.copy(xo[:, u, :, :], xin[:, u, :, :]).then_inc(residual_ready, 1)

            over_supertiles(act, body)

        @block.gpsimd
        def _(pool):
            def add_out(i, u):
                pool.wait_ge(yn_ready, NT * (i + 1))
                pool.wait_ge(residual_ready, i + 1)
                nc.gpsimd.tensor_tensor(xo[:, u, :, :], xo[:, u, :, :], yn[:, :, :], ALU.add).then_inc(xo_ready, 1)

            minus_half(nc, pool, half, half_set)
            inverse_root(nc, pool, rs, half, stats, LN, rs_ready)

            def body(i, u, last):
                if not first(i, 2):
                    add_out(i - 2, u)
                for e in range(E):
                    if e == 5 and not last:
                        inverse_root(nc, pool, rs, half, stats, LN * (i + 2), rs_ready)
                    pool.wait_ge(h_ready, E * i + e + 1)
                    if e == 0 and not first(i, 2):
                        pool.wait_ge(y_done, UNITS * NT * (i - 1))
                    nc.gpsimd.tensor_tensor(hlo[:, u, e, :], h[:, e % 3, :], hhi[:, u, e, :],
                                            ALU.subtract).then_inc(hlo_ready, 1)
                if not first(i, 1):
                    inverse_root(nc, pool, rs2, half, stats2, LN * i, rs2_ready)

            over_supertiles(pool, body)
            add_out(NST - 2, 0)
            inverse_root(nc, pool, rs2, half, stats2, LN * NST, rs2_ready)
            add_out(NST - 1, 1)


NHG = GH // 4
NC = NT
MASKED = -1.0e30


def gla_constants():
    s, t = np.arange(P)[:, None], np.arange(P)[None, :]
    heads = np.zeros((3, 32, J, P), np.float32)
    for h in range(GH):
        heads[:, h, h // 2, GD * (h % 2):GD * (h % 2 + 1)] = 1.0
    minus = np.zeros((NHG, 32, 4), np.float32)
    for a in range(3):
        for r in range(4):
            minus[:, 12 + 4 * a + r, r] = -1.0
    return {
        "up_to": (s <= t).astype(np.float32),
        "after": (s > t).astype(np.float32),
        "masked": np.where(s > t, np.float32(MASKED), np.float32(0)).astype(np.float32),
        "heads": heads.reshape(3 * 32, J * P),
        "minus": minus.reshape(NHG * 32, 4),
    }


def phase_gla(nc, x, wq_t, wk_t, wv_t, wg_t, wog_t, wo_t, wd_t, bd, norm_cols, ident_d, const, x_out):
    with ExitStack() as ctx:
        m = Place(nc, ctx, "gla")
        wq, wk, wv, wg, wog = (m.sb(s, [P, KD, HID]) for s in ("wq", "wk", "wv", "wg", "wog"))
        wo, wd = m.sb("wo", [P, J, D]), m.sb("wd", [P, KD, GH])
        b_d, norm_w = m.sb("b_d", [P, GH]), m.sb("norm_w", [P, J])
        ident, up_to, after = m.sb("ident", [P, P]), m.sb("up_to", [P, P]), m.sb("after", [P, P])
        ident_b, masked_b = m.sb("ident_b", [P, P], BF16), m.sb("masked_b", [P, 4, P], BF16)
        heads_b = m.sb("heads_b", [96, J, P], BF16)
        minus = m.sb("minus", [P, 4])
        ones = m.sb("ones", [P, 1])
        half, half_set = m.sb("half", [P, NT]), m.sem("half_set")
        xin = m.sb("xin", [P, 2, NT, D])
        xn = m.sb("xn", [P, NT, D])
        xT = m.sb("xT", [P, 2, KD, ST])
        st, mv, rs = m.sb("st", [P, NT, 6]), m.sb("mv", [P, NT, 2]), m.sb("rs", [P, 2, NT])
        st2, mv2, rs2 = m.sb("st2", [P, NT, 6]), m.sb("mv2", [P, NT, 2]), m.sb("rs2", [P, 2, NT])
        rs3 = m.sb("rs3", [P, 2, 1])
        y, xo = m.sb("y", [P, NT, D]), m.sb("xo", [P, 2, NT, D])
        z, zabs, zexp, glog = (m.sb(s, [P, NC, GH]) for s in ("z", "zabs", "zexp", "glog"))
        to_end = m.sb("to_end", [P, NC, GH])
        gparts = m.sb("gparts", [96, ST], BF16)
        gmid, grest = m.sb("gmid", [GH, ST], BF16), m.sb("grest", [GH, ST])
        rows_t = m.sb("rows_t", [P, NC, 4, P], BF16)
        rows_s = m.sb("rows_s", [P, ST], BF16)
        q, og = m.sb("q", [P, J, ST]), m.sb("og", [P, J, ST])
        sg = m.sb("sg", [P, 2, ST])
        kg, v = m.sb("kg", [P, 2, HID]), m.sb("v", [P, 2, HID])
        kT = m.sb("kT", [P, 2, J, P])
        kw = m.sb("kw", [P, HID])
        eg, qe = m.sb("eg", [P, J, P]), m.sb("qe", [P, J, P])
        dm, ad = m.sb("dm", [P, 2, 4, P]), m.sb("ad", [P, 2, 4, P])
        osq, yT, osum = m.sb("osq", [P, J, P]), m.sb("yT", [P, J, P]), m.sb("osum", [P, P])
        state, decayed = m.sb("state", [P, J, P]), m.sb("decayed", [P, J, P])
        psP = m.ps("psP", [P, 2, ST])
        psA, psD = m.ps("psA", [P, 4, P]), m.ps("psD", [P, 4, P])
        psO = m.ps("psO", [P, 2, 4, P])
        psX = m.ps("psX", [P, 4, P])
        psW = m.ps("psW", [P, ST])

        const_in, wkgv_in, w_in, x_in = m.sem("const_in"), m.sem("wkgv_in"), m.sem("w_in"), m.sems("x_in", 2)
        const_set, zero_set, wo_scaled = m.sem("const_set"), m.sem("zero_set"), m.sem("wo_scaled")
        stats, rs_ready, xn_ready, turned, xT_ready = (m.sem(s) for s in ("stats", "rs_ready", "xn_ready", "turned", "xT_ready"))
        stats2, rs2_ready, yn_ready = m.sem("stats2"), m.sem("rs2_ready"), m.sem("yn_ready")
        z_done, decay, soft, g_rows_done, w_done, to_end_ready, gsplit, rows_in = (
            m.sem(s) for s in ("z_done", "decay", "soft", "g_rows_done", "after_done", "to_end_ready", "gsplit", "rows_in"))
        q_done, q_ready, og_done, og_ready = (m.sem(s) for s in ("q_done", "q_ready", "og_done", "og_ready"))
        g_done, sig_ready, k_done, kg_ready, v_done, v_ready = (
            m.sem(s) for s in ("g_done", "sig_ready", "k_done", "kg_ready", "v_done", "v_ready"))
        kt_done, kt_ready, kw_ready = m.sem("kt_done"), m.sem("kt_ready"), m.sem("kw_ready")
        d_done, d_ready, qe_ready, a_done, ad_ready = (m.sem(s) for s in ("d_done", "d_ready", "qe_ready", "a_done", "ad_ready"))
        o_done, yT_ready, osq_ready, osum_ready = (m.sem(s) for s in ("o_done", "yT_ready", "osq_ready", "osum_ready"))
        kv_done, decayed_ready, state_ready, state_zero = (
            m.sem(s) for s in ("kv_done", "decayed_ready", "state_ready", "state_zero"))
        out_done, square_ready, rs3_ready, y_ready = (m.sem(s) for s in ("out_done", "square_ready", "rs3_ready", "y_ready"))
        xo_ready, x_outd = m.sem("xo_ready"), m.sems("x_out", 2)
        xv, ov = tokens(x), tokens(x_out)
        N_CONST, N_ROWS = 16 * 8, 16 * 24
        D_USES = 2 + NHG
        block = ctx.enter_context(nc.Block())

        def wide(a, n):
            return a.to_broadcast([*a.shape[:-1], n])

        @block.sync
        def _(sp):
            sp.dma_start(xin[:, 0, :, :], xv[0]).then_inc(x_in[0], 16)
            sp.dma_start(ident[:, :], ident_d).then_inc(const_in, 16)
            for w, d in ((wg, wg_t), (wk, wk_t), (wv, wv_t)):
                sp.dma_start(w[:, :, :], d.rearrange("(k p) o -> p k o", p=P)).then_inc(wkgv_in, 16)
            sp.dma_start(up_to[:, :], const["up_to"]).then_inc(const_in, 16)
            sp.dma_start(after[:, :], const["after"]).then_inc(const_in, 16)
            sp.dma_start(kg[:, 0, 0:P], const["masked"]).then_inc(const_in, 16)
            sp.dma_start(og[0:96, 0:2, :].rearrange("p a b -> p (a b)"), const["heads"]).then_inc(const_in, 16)
            sp.dma_start(minus[:, :], const["minus"]).then_inc(const_in, 16)
            sp.dma_start(b_d[:, :], row(bd)).then_inc(const_in, 16)
            sp.dma_start(norm_w[:, :], norm_cols).then_inc(const_in, 16)
            for w, d in ((wd, wd_t), (wq, wq_t), (wog, wog_t), (wo, wo_t)):
                sp.dma_start(w[:, :, :], d.rearrange("(k p) o -> p k o", p=P)).then_inc(w_in, 16)

            def body(i, u, last):
                sp.wait_ge(gsplit, 5 * (i + 1))
                for a in range(3):
                    for r in range(4):
                        sp.dma_start(rows_t[4 * a + r:4 * a + r + 97:32, :, r, :],
                                     gparts[32 * a + r:32 * a + r + 13:4, :].rearrange("p (n t) -> p n t", t=P)
                                     ).then_inc(rows_in, 16)
                    for hg in range(NHG):
                        sp.dma_start(rows_s[32 * hg + 12 + 4 * a:32 * hg + 16 + 4 * a, :],
                                     gparts[32 * a + 4 * hg:32 * a + 4 * hg + 4, :]).then_inc(rows_in, 16)
                if not first(i, 1):
                    sp.wait_ge(xo_ready, i)
                    sp.dma_start(ov[i - 1], xo[:, 1 - u, :, :]).then_inc(x_outd[1 - u], 16)
                if not last:
                    sp.dma_start(xin[:, 1 - u, :, :], xv[i + 1]).then_inc(x_in[1 - u], 16)

            over_supertiles(sp, body)
            sp.wait_ge(xo_ready, NST)
            sp.dma_start(ov[NST - 1], xo[:, 1, :, :]).then_inc(x_outd[1], 16)
            for s in x_outd:
                sp.wait_ge(s, 16 * NST // 2)

        @block.tensor
        def _(pe):
            def turn_in(i, k, after_kt):
                if k == 0:
                    pe.wait_ge(xn_ready, NT * (i + 1))
                if k:
                    pe.wait_ge(xT_ready, KD * i + k)
                elif after_kt is not None:
                    pe.wait_ge(kt_ready, after_kt)
                turn(nc, xn, psX[:, :, :].rearrange("p j t -> p (j t)"), ident, k).then_inc(turned, 1)

            def project(bank, w, half, u, n, done):
                for k in range(KD):
                    mm = pe.matmul(psP[:, bank, :], xT[:, u, k, n * P:(n + 1) * P],
                                   w[:, k, half * ST:(half + 1) * ST], start=(k == 0), stop=(k == KD - 1))
                mm.then_inc(done, 1)

            def gate(i, u, n, h):
                c = NC * i + n
                if h:
                    pe.wait_ge(sig_ready, 2 * c + 1)
                elif n == 1:
                    pe.wait_ge(og_ready, J * (i + 1))
                elif not (first(i, 1) and n == 0):
                    pe.wait_ge(v_ready, 2 * c - 1)
                project(0, wg, h, u, n, g_done)

            def key(i, u, n, h):
                c = NC * i + n
                if h:
                    pe.wait_ge(kg_ready, 2 * c + 1)
                elif n != 1 and not (first(i, 1) and n == 0):
                    pe.wait_ge(v_ready, 2 * c)
                project(1, wk, h, u, n, k_done)

            def values(i, u, n, h):
                c = NC * i + n
                pe.wait_ge(sig_ready if h == 0 else kg_ready, 2 * c + 2)
                project(h, wv, h, u, n, v_done)

            def out_project(c):
                pe.wait_ge(yT_ready, 2 * c + 2)
                pe.wait_ge(y_ready, c)
                for j in range(J):
                    pe.matmul(psW[:, 0:D], yT[:, j, :], wo[:, j, :], start=(j == 0), stop=(j == J - 1))
                pe.wait_ge(osum_ready, c + 1)
                pe.matmul(psW[:, D:D + 1], osum[:, :], ones[:, :], start=True, stop=True).then_inc(out_done, 1)

            def supertile(i, u):
                c = NC * i
                if not first(i, 1):
                    out_project(c - 1)
                    pe.wait_ge(y_ready, c)
                pe.wait_ge(xT_ready, KD * (i + 1))
                for n in range(NC):
                    for k in range(KD):
                        mm = pe.matmul(psW[:, n * GH:(n + 1) * GH], xT[:, u, k, n * P:(n + 1) * P], wd[:, k, :],
                                       start=(k == 0), stop=(k == KD - 1))
                mm.then_inc(z_done, 1)

                def tile(j, w, done, taken):
                    if j >= 2:
                        pe.wait_ge(taken, J * i + j - 1)
                    for k in range(KD):
                        mm = pe.matmul(psP[:, j % 2, :], w[:, k, j * P:(j + 1) * P], xT[:, u, k, :],
                                       start=(k == 0), stop=(k == KD - 1))
                    mm.then_inc(done, 1)

                for j in range(J):
                    if j < 2:
                        pe.wait_ge(v_ready, 2 * c + j + 1)
                    tile(j, wq, q_done, q_ready)
                    if j == 3:
                        pe.wait_ge(decay, 4 * (i + 1))
                        for n in range(NC):
                            mm = pe.matmul(psW[0:GH, n * P:(n + 1) * P], glog[:, n, :], up_to[:, :],
                                           start=True, stop=True)
                        mm.then_inc(g_rows_done, 1)
                        if not first(i, 1):
                            pe.wait_ge(state_ready, 2 * c)
                        for n in range(NC):
                            mm = pe.matmul(psX[:, 0, n * GH:(n + 1) * GH], after[:, :], glog[:, n, :],
                                           start=True, stop=True)
                        mm.then_inc(w_done, 1)
                for j in range(J):
                    if j < 2:
                        pe.wait_ge(q_ready, J * i + 7 + j)
                    tile(j, wog, og_done, og_ready)

            def slot(i, u, n, last):
                c = NC * i + n
                ahead = not (last and n == NC - 1)
                nxt = (i, u, n + 1) if n < NC - 1 else (i + 1, 1 - u, 0)
                turning = n == 1 and not last

                def keys_turned(g):
                    pe.wait_ge(kg_ready, 2 * c + g + 1)
                    if g:
                        pe.wait_ge(kt_ready, 2 * c + 1)
                    elif n == 0:
                        pe.wait_ge(to_end_ready, i + 1)
                    else:
                        pe.wait_ge(state_ready, 2 * c)
                    for jj in range(4):
                        j = 4 * g + jj
                        mm = pe.transpose(psX[:, jj, :], kg[:, n % 2, j * P:(j + 1) * P], ident[:, :])
                    mm.then_inc(kt_done, 1)

                def decay_of_channels(g):
                    if g == 0 and n == 0:
                        pe.wait_ge(gsplit, 5 * (i + 1))
                    if not (first(i, 1) and n == 0 and g == 0):
                        pe.wait_ge(d_ready, D_USES * c + g)
                    for jj in range(4):
                        mm = pe.matmul(psD[:, jj, :], heads_b[:, 4 * g + jj, :], gparts[:, n * P:(n + 1) * P],
                                       start=True, stop=True)
                    mm.then_inc(d_done, 1)

                keys_turned(0)
                if ahead:
                    if n == NC - 1:
                        pe.wait_ge(xT_ready, KD * (i + 2))
                    gate(*nxt, 0)
                keys_turned(1)
                if ahead:
                    key(*nxt, 0)
                decay_of_channels(0)
                if turning:
                    turn_in(i + 1, 0, 2 * c + 2)
                if ahead:
                    gate(*nxt, 1)
                decay_of_channels(1)
                if turning:
                    turn_in(i + 1, 1, None)
                if ahead:
                    key(*nxt, 1)
                if n:
                    out_project(c - 1)
                if n == 0:
                    pe.wait_ge(rows_in, N_ROWS * (i + 1))
                    pe.wait_ge(q_ready, J * (i + 1))

                def outputs(hg):
                    g = hg // 2
                    pe.wait_ge(ad_ready, NHG * c + hg + 1)
                    if hg % 2 == 0:
                        pe.wait_ge(qe_ready, 2 * c + g + 1)
                        pe.wait_ge(v_ready, 2 * c + g + 1)
                        if n == 0 and u == 0:
                            pe.wait_ge(state_zero, i + 2)
                        else:
                            pe.wait_ge(state_ready, 2 * c - 1 + g)
                        if not (first(i, 1) and n == 0):
                            pe.wait_ge(osq_ready, 2 * c - 1 + g)
                    for jj in range(2):
                        j = 2 * hg + jj
                        for odd in range(2):
                            h = 2 * j + odd
                            pe.matmul(psO[GD * odd:GD * (odd + 1), g, j % 4, :],
                                      v[:, n % 2, h * GD:(h + 1) * GD], ad[:, hg % 2, 2 * jj + odd, :],
                                      start=True, stop=False, skip_group_check=True)
                        mm = pe.matmul(psO[:, g, j % 4, :], state[:, j, :], qe[:, j, :], start=False, stop=True,
                                       skip_group_check=True)
                    mm.then_inc(o_done, 1)

                def update(g):
                    if g:
                        pe.wait_ge(state_ready, 2 * c + 1)
                    else:
                        pe.wait_ge(kw_ready, c + 1)
                        pe.wait_ge(v_ready, 2 * c + 2)
                        pe.wait_ge(kt_ready, 2 * c + 2)
                        if n == 1 and not last:
                            pe.wait_ge(xT_ready, KD * (i + 2))
                    for jj in range(4):
                        j = 4 * g + jj
                        mm = pe.matmul(psX[:, jj, :], kw[:, j * P:(j + 1) * P], v[:, n % 2, j * P:(j + 1) * P],
                                       start=True, stop=True)
                    mm.then_inc(kv_done, 1)

                for hg in range(NHG):
                    pe.wait_ge(d_ready, D_USES * c + 2 + hg)
                    base = 32 * hg
                    pe.matmul(psD[:, :, :], ident_b[:, :], masked_b[:, :, :], start=True, stop=False)
                    pe.matmul(psD[:, :, :], rows_s[base:base + 24, n * P:(n + 1) * P],
                              rows_t[base:base + 24, n, :, :], start=False, stop=True,
                              tile_position=(base, 0)).then_inc(d_done, 1)
                    if not (first(i, 1) and n == 0 and hg == 0):
                        pe.wait_ge(ad_ready, NHG * c + hg)
                    pe.wait_ge(kt_ready, 2 * c + hg // 2 + 1)
                    for r in range(4):
                        j = 2 * hg + r // 2
                        mm = pe.matmul(psA[:, r, :], kT[:, r % 2, j, :], q[:, j, n * P:(n + 1) * P],
                                       start=True, stop=True)
                    mm.then_inc(a_done, 1)
                    if hg < 2 and ahead:
                        values(*nxt, hg)
                    if hg:
                        outputs(hg - 1)
                update(0)
                outputs(NHG - 1)
                update(1)

            pe.wait_ge(const_in, N_CONST)
            pe.wait_ge(const_set, 7)
            for k in range(KD):
                turn_in(0, k, None)
            pe.wait_ge(wkgv_in, 48)
            pe.wait_ge(xT_ready, KD)
            for h in range(2):
                gate(0, 0, 0, h)
                key(0, 0, 0, h)
            for h in range(2):
                values(0, 0, 0, h)
            pe.wait_ge(w_in, 64)
            pe.wait_ge(zero_set, 1)
            pe.wait_ge(wo_scaled, 2)

            def body(i, u, last):
                supertile(i, u)
                for n in range(NC):
                    slot(i, u, n, last)

            over_supertiles(pe, body)
            out_project(NC * NST - 1)

        @block.scalar
        def _(act):
            def take_turned(i, u, k):
                act.wait_ge(turned, KD * i + k + 1)
                nc.scalar.copy(xT[:, u, k, :], psX[:, :, :].rearrange("p j t -> p (j t)")).then_inc(xT_ready, 1)

            def sigmoid(i, n, h):
                c = NC * i + n
                act.wait_ge(g_done, 2 * c + h + 1)
                if not (first(i, 1) and n == 0):
                    act.wait_ge(kg_ready, 2 * c - 1 + h)
                nc.scalar.activation(sg[:, h, :], psP[:, 0, :], ACT.Tanh, scale=0.5).then_inc(sig_ready, 1)

            def take_values(i, n, h):
                act.wait_ge(v_done, 2 * (NC * i + n) + h + 1)
                nc.scalar.copy(v[:, n % 2, h * ST:(h + 1) * ST], psP[:, h, :]).then_inc(v_ready, 1)

            def supertile(i, u):
                c = NC * i
                act.wait_ge(decay, 4 * i + 2)
                nc.scalar.activation(zexp[:, :, :], zabs[:, :, :], ACT.Exp, scale=-1.0).then_inc(soft, 1)
                act.wait_ge(soft, 2 * i + 1)
                nc.scalar.activation(zexp[:, :, :], zexp[:, :, :], ACT.Ln, bias=1.0).then_inc(soft, 1)
                if not first(i, 1):
                    act.wait_ge(qe_ready, 2 * c)
                for j in range(J):
                    act.wait_ge(q_done, J * i + j + 1)
                    nc.scalar.activation(q[:, j, :], psP[:, j % 2, :], ACT.Copy, scale=0.5).then_inc(q_ready, 1)
                    if j == 3:
                        act.wait_ge(w_done, i + 1)
                        if not first(i, 1):
                            act.wait_ge(kw_ready, c)
                        nc.scalar.activation(to_end[:, :, :].rearrange("p n h -> p (n h)"), psX[:, 0, 0:NC * GH],
                                             ACT.Exp).then_inc(to_end_ready, 1)
                if not first(i, 1):
                    act.wait_ge(yT_ready, 2 * c)
                for j in range(J):
                    act.wait_ge(og_done, J * i + j + 1)
                    nc.scalar.activation(og[:, j, :], psP[:, j % 2, :], ACT.Tanh, scale=0.5).then_inc(og_ready, 1)

            def slot(i, u, n, last):
                c = NC * i + n
                ahead = not (last and n == NC - 1)
                nxt = (i, n + 1) if n < NC - 1 else (i + 1, 0)
                turning = n == 1 and not last

                def keys_taken(g):
                    act.wait_ge(kt_done, 2 * c + g + 1)
                    for odd in range(2):
                        rows = slice(GD * odd, GD * (odd + 1))
                        last_copy = nc.scalar.copy(kT[rows, odd, 4 * g:4 * g + 4, :], psX[rows, :, :])
                    last_copy.then_inc(kt_ready, 1)

                def exp_of_decay(g):
                    act.wait_ge(d_done, D_USES * c + g + 1)
                    if g == 0 and not (first(i, 1) and n == 0):
                        act.wait_ge(decayed_ready, c)
                        act.wait_ge(qe_ready, 2 * c)
                    nc.scalar.activation(eg[:, 4 * g:4 * g + 4, :], psD[:, :, :], ACT.Exp).then_inc(d_ready, 1)

                keys_taken(0)
                if ahead:
                    sigmoid(*nxt, 0)
                keys_taken(1)
                exp_of_decay(0)
                if turning:
                    take_turned(i + 1, 1 - u, 0)
                if ahead:
                    sigmoid(*nxt, 1)
                exp_of_decay(1)
                if turning:
                    take_turned(i + 1, 1 - u, 1)
                for hg in range(NHG):
                    act.wait_ge(d_done, D_USES * c + 3 + hg)
                    if not (first(i, 1) and n == 0 and hg < 2):
                        act.wait_ge(ad_ready, NHG * c + hg - 1)
                    nc.scalar.activation(dm[:, hg % 2, :, :], psD[:, :, :], ACT.Exp).then_inc(d_ready, 1)
                    if hg < 2 and ahead:
                        take_values(*nxt, hg)
                for g in range(2):
                    act.wait_ge(yT_ready, 2 * c + g + 1)
                    if g == 0 and not (first(i, 1) and n == 0):
                        act.wait_ge(osum_ready, c)
                    nc.scalar.activation(osq[:, 4 * g:4 * g + 4, :], psO[:, g, :, :], ACT.Square).then_inc(osq_ready, 1)

            for k in range(KD):
                take_turned(0, 0, k)
            act.wait_ge(const_set, 7)
            for h in range(2):
                sigmoid(0, 0, h)
            for h in range(2):
                take_values(0, 0, h)
            act.wait_ge(zero_set, 1)

            def body(i, u, last):
                supertile(i, u)
                for n in range(NC):
                    slot(i, u, n, last)

            over_supertiles(act, body)

        @block.vector
        def _(dve):
            s, s2, t, dec = Steps(LN), Steps(LN), Steps(5), Steps(4)

            def pre(i, u):
                s.start(i)
                dve.wait_ge(x_in[u], 8 * (i - u) + 16)
                if not first(i, 1):
                    dve.wait_ge(turned, KD * i)
                normalize_tiles(nc, dve, xin[:, u, :, :], xn, st, mv, rs, stats, s, rs_ready, i + 1, xn_ready)
                s.end()

            def gated_keys(i, n, h):
                c = NC * i + n
                dve.wait_ge(k_done, 2 * c + h + 1)
                dve.wait_ge(sig_ready, 2 * c + h + 1)
                if h == 0 and not (first(i, 1) and n < 2):
                    dve.wait_ge(kw_ready, c - 1)
                nc.vector.scalar_tensor_tensor(kg[:, n % 2, h * ST:(h + 1) * ST], sg[:, h, :], 1.0, psP[:, 1, :],
                                               ALU.add, ALU.mult).then_inc(kg_ready, 1)

            def mean_square(c):
                dve.wait_ge(out_done, c + 1)
                nc.vector.tensor_scalar(rs3[:, 0, :], psW[:, D:D + 1], 1.0 / HID, RMS_EPS, ALU.mult,
                                        ALU.add).then_inc(square_ready, 1)

            def take_out(c, n, i_of_y):
                dve.wait_ge(rs3_ready, c + 1)
                if n == 0 and not first(i_of_y, 1):
                    dve.wait_ge(xo_ready, i_of_y)
                nc.vector.tensor_scalar(y[:, n, :], psW[:, 0:D], rs3[:, 1, :], None, ALU.mult).then_inc(y_ready, 1)

            def norm_y(i):
                s2.start(i)
                dve.wait_ge(y_ready, NC * (i + 1))
                normalize_tiles(nc, dve, y, y, st2, mv2, rs2, stats2, s2, rs2_ready, i + 1, yn_ready)
                s2.end()

            def supertile(i, u):
                c = NC * i
                if not first(i, 1):
                    mean_square(c - 1)
                    take_out(c - 1, NC - 1, i - 1)
                dec.start(i)
                dve.wait_ge(z_done, i + 1)
                nc.vector.tensor_tensor(z[:, :, :], psW[:, 0:NC * GH].rearrange("p (n h) -> p n h", h=GH),
                                        b_d[:, :].rearrange("p (n h) -> p n h", n=1).to_broadcast([P, NC, GH]),
                                        ALU.add).then_inc(decay, dec.inc())
                dve.wait_ge(decay, dec.now())
                if not first(i, 1):
                    dve.wait_ge(soft, 2 * i)
                nc.vector.scalar_tensor_tensor(zabs[:, :, :], z[:, :, :], -1.0, z[:, :, :], ALU.mult,
                                               ALU.max).then_inc(decay, dec.inc())
                dve.wait_ge(soft, 2 * i + 2)
                nc.vector.scalar_tensor_tensor(z[:, :, :], z[:, :, :], 0.0, zexp[:, :, :], ALU.max,
                                               ALU.add).then_inc(decay, dec.inc())
                dve.wait_ge(decay, dec.now())
                nc.vector.tensor_scalar(glog[:, :, :], z[:, :, :], -1.0, None, ALU.mult).then_inc(decay, dec.inc())
                dec.end()
                t.start(i)
                dve.wait_ge(g_rows_done, i + 1)
                nc.vector.tensor_copy(gparts[0:GH, :], psW[0:GH, :]).then_inc(gsplit, t.inc())
                dve.wait_ge(gsplit, t.now())
                nc.vector.tensor_tensor(grest[:, :], psW[0:GH, :], gparts[0:GH, :], ALU.subtract).then_inc(gsplit, t.inc())
                dve.wait_ge(gsplit, t.now())
                nc.vector.tensor_copy(gmid[:, :], grest[:, :]).then_inc(gsplit, t.inc())
                dve.wait_ge(gsplit, t.now())
                nc.vector.tensor_copy(gparts[32:32 + GH, :], gmid[:, :]).then_inc(gsplit, t.inc())
                nc.vector.tensor_tensor(gparts[64:64 + GH, :], grest[:, :], gmid[:, :], ALU.subtract).then_inc(gsplit, t.inc())
                t.end()
                if not first(i, 1):
                    norm_y(i - 1)

            def slot(i, u, n, last):
                c = NC * i + n
                ahead = not (last and n == NC - 1)
                nxt = (i, n + 1) if n < NC - 1 else (i + 1, 0)

                def queries_decayed(g):
                    js = slice(4 * g, 4 * g + 4)
                    dve.wait_ge(d_ready, D_USES * c + g + 1)
                    if n == 0 and g == 0:
                        dve.wait_ge(q_ready, J * (i + 1))
                    nc.vector.tensor_tensor(qe[:, js, :], q[:, js, n * P:(n + 1) * P], eg[:, js, :],
                                            ALU.mult).then_inc(qe_ready, 1)

                if ahead:
                    gated_keys(*nxt, 0)
                queries_decayed(0)
                queries_decayed(1)
                if ahead:
                    gated_keys(*nxt, 1)
                if n:
                    mean_square(c - 1)

                def weighted(hg):
                    dve.wait_ge(a_done, NHG * c + hg + 1)
                    dve.wait_ge(d_ready, D_USES * c + 3 + hg)
                    if not (first(i, 1) and n == 0 and hg < 2):
                        dve.wait_ge(o_done, NHG * c + hg - 1)
                    nc.vector.tensor_tensor(ad[:, hg % 2, :, :], psA[:, :, :], dm[:, hg % 2, :, :],
                                            ALU.mult).then_inc(ad_ready, 1)

                def take_outputs(g):
                    js = slice(4 * g, 4 * g + 4)
                    dve.wait_ge(o_done, NHG * c + 2 * g + 2)
                    if n == 0 and g == 0:
                        dve.wait_ge(og_ready, J * (i + 1))
                    if g == 0 and not (first(i, 1) and n == 0):
                        dve.wait_ge(out_done, c)
                    nc.vector.scalar_tensor_tensor(yT[:, js, :], og[:, js, n * P:(n + 1) * P], 1.0, psO[:, g, :, :],
                                                   ALU.add, ALU.mult).then_inc(yT_ready, 1)

                def update(g):
                    js = slice(4 * g, 4 * g + 4)
                    dve.wait_ge(kv_done, 2 * c + g + 1)
                    dve.wait_ge(o_done, NHG * c + 2 * g + 2)
                    if g == 0:
                        dve.wait_ge(decayed_ready, c + 1)
                    for odd in range(2):
                        r = slice(GD * odd, GD * (odd + 1))
                        last_add = nc.vector.tensor_tensor(state[r, js, r], psX[r, :, r], decayed[r, js, r], ALU.add)
                    last_add.then_inc(state_ready, 1)

                weighted(0)
                if n:
                    take_out(c - 1, n - 1, i)
                weighted(1)
                weighted(2)
                take_outputs(0)
                weighted(3)
                update(0)
                take_outputs(1)
                update(1)
                dve.wait_ge(osq_ready, 2 * c + 2)
                nc.vector.tensor_reduce(osum[:, :], osq[:, :, :].rearrange("p j t -> p t j"), AX.X,
                                        ALU.add).then_inc(osum_ready, 1)
                if n == 0 and not last:
                    pre(i + 1, 1 - u)

            nc.vector.memset(ones[:, :], 1.0).then_inc(const_set, 1)
            nc.vector.memset(rows_s[:, :], 1.0).then_inc(const_set, 1)
            pre(0, 0)
            dve.wait_ge(const_in, N_CONST)
            nc.vector.tensor_copy(ident_b[:, :], ident[:, :]).then_inc(const_set, 1)
            nc.vector.tensor_copy(masked_b[:, :, :], kg[:, 0, 0:P].rearrange("p (a t) -> p a t", a=1)
                                  .to_broadcast([P, 4, P])).then_inc(const_set, 1)
            nc.vector.tensor_copy(heads_b[:, :, :].rearrange("p j t -> p (j t)"),
                                  og[0:96, 0:2, :].rearrange("p a b -> p (a b)")).then_inc(const_set, 1)
            nc.vector.memset(gparts[:, :], 0.0).then_inc(const_set, 1)
            nc.vector.tensor_copy(
                rows_t[:, :, :, :],
                minus[:, :].rearrange("p (n r t) -> p n r t", n=1, t=1).to_broadcast([P, NC, 4, P])
            ).then_inc(const_set, 1)
            dve.wait_ge(const_set, 7)
            for h in range(2):
                gated_keys(0, 0, h)

            def body(i, u, last):
                supertile(i, u)
                for n in range(NC):
                    slot(i, u, n, last)

            over_supertiles(dve, body)
            mean_square(NC * NST - 1)
            take_out(NC * NST - 1, NC - 1, NST - 1)
            norm_y(NST - 1)

        @block.gpsimd
        def _(pool):
            def root_square(c):
                pool.wait_ge(square_ready, c + 1)
                nc.gpsimd.tensor_tensor(rs3[:, 1, :], rs3[:, 0, :], half[:, 0:1], ALU.pow).then_inc(rs3_ready, 1)

            def residual(i, u):
                inverse_root(nc, pool, rs2, half, stats2, LN * (i + 1), rs2_ready)
                pool.wait_ge(yn_ready, NT * (i + 1))
                if not first(i, 2):
                    pool.wait_ge(x_outd[u], 8 * (i - u))
                nc.gpsimd.tensor_tensor(xo[:, u, :, :], xin[:, u, :, :], y[:, :, :], ALU.add).then_inc(xo_ready, 1)

            def supertile(i, u):
                c = NC * i
                if not first(i, 1):
                    root_square(c - 1)
                if u == 0:
                    if not first(i, 1):
                        pool.wait_ge(state_ready, 2 * c)
                    nc.gpsimd.memset(state[:, :, :], 0.0).then_inc(state_zero, 2)
                if not first(i, 1):
                    residual(i - 1, 1 - u)

            def slot(i, u, n, last):
                c = NC * i + n
                pool.wait_ge(kg_ready, 2 * c + 2)
                if n == 0:
                    pool.wait_ge(to_end_ready, i + 1)
                if not (first(i, 1) and n == 0):
                    pool.wait_ge(kv_done, 2 * c)
                nc.gpsimd.tensor_tensor(kw[:, :].rearrange("p (h d) -> p h d", d=GD),
                                        kg[:, n % 2, :].rearrange("p (h d) -> p h d", d=GD),
                                        to_end[:, n, :].rearrange("p (h d) -> p h d", d=1).to_broadcast([P, GH, GD]),
                                        ALU.mult).then_inc(kw_ready, 1)
                pool.wait_ge(d_ready, D_USES * c + 2)
                if n == 0 and u == 0:
                    pool.wait_ge(state_zero, i + 2)
                else:
                    pool.wait_ge(state_ready, 2 * c)
                nc.gpsimd.tensor_tensor(decayed[:, :, :], state[:, :, :], eg[:, :, P - 1:P].to_broadcast([P, J, P]),
                                        ALU.mult).then_inc(decayed_ready, 1)
                if n:
                    root_square(c - 1)
                if n == 0 and not last:
                    inverse_root(nc, pool, rs, half, stats, LN * (i + 2), rs_ready)

            minus_half(nc, pool, half, half_set)
            inverse_root(nc, pool, rs, half, stats, LN, rs_ready)
            nc.gpsimd.memset(kT[:, :, :, :], 0.0).then_inc(zero_set, 1)
            pool.wait_ge(const_in, N_CONST)
            pool.wait_ge(w_in, 64)
            nc.gpsimd.tensor_tensor(wo[:, :, :], wo[:, :, :],
                                    norm_w[:, :].rearrange("p (j c) -> p j c", c=1).to_broadcast([P, J, D]),
                                    ALU.mult).then_inc(wo_scaled, 1)
            pool.wait_ge(wo_scaled, 1)
            nc.gpsimd.tensor_scalar(wo[:, :, :], wo[:, :, :], 0.5, None, ALU.mult).then_inc(wo_scaled, 1)

            def body(i, u, last):
                supertile(i, u)
                for n in range(NC):
                    slot(i, u, n, last)

            over_supertiles(pool, body)
            root_square(NC * NST - 1)
            residual(NST - 1, 1)


def sandwich(nc, x, qkv_w_t, qkv_b, qkv_b_cols, out_w_t, out_b, ffn_w1_t, ffn_b1_cols, ffn_w2_t, ffn_b2,
             wq_t, wk_t, wv_t, wo_t, wg_t, wog_t, wd_t, bd, norm_cols,
             gate_w, moe_w1, moe_b1_cols, moe_w2, moe_b2, ws1, bs1_col, ws2, bs2, route_scale,
             ident, up_to, after, masked, heads, minus, out):
    def scratch(name, shape, dt=F32):
        return nc.dram_tensor(name, shape, dt, kind="Internal").ap()

    parts = scratch("qk_parts", [2, NST, NG, 3, HG * AD, ST], BF16)
    v_aug = scratch("values", [NST, NT, NG, P, HG * VW])
    att = scratch("attended", [TOKENS, D])
    x2, x3 = (scratch(f"stream{k}", [TOKENS, D]) for k in (2, 3))
    const = {"up_to": up_to, "after": after, "masked": masked, "heads": heads, "minus": minus}
    phase_qkv(nc, x, qkv_w_t, qkv_b, qkv_b_cols, ident, parts, v_aug)
    phase_attention(nc, parts, v_aug, ident, att)
    phase_project_ffn(nc, x, att, out_w_t, out_b, ffn_w1_t, ffn_b1_cols, ffn_w2_t, ffn_b2, ident, x2)
    phase_gla(nc, x2, wq_t, wk_t, wv_t, wg_t, wog_t, wo_t, wd_t, bd, norm_cols, ident, const, x3)
    phase_experts(nc, x3, gate_w, moe_w1, moe_b1_cols, moe_w2, moe_b2, ws1, bs1_col, ws2, bs2, route_scale,
                  ident, out)



def kernel(**inputs):
    import concourse.bacc as bacc
    from concourse.bass_utils import run_bass_kernel_spmd

    a = {name: np.asarray(v) for name, v in inputs.items()}
    l0a, l0f, l1a, l1f = "L0_attn_", "L0_ffn_", "L1_attn_", "L1_ffn_"

    def columns(v):
        return v.reshape(-1, P).T

    laid_out = {
        "x": a[l0a + "x"].reshape(TOKENS, D),
        "qkv_w_t": a[l0a + "qkv_w"].T,
        "qkv_b": a[l0a + "qkv_b"],
        "qkv_b_cols": columns(a[l0a + "qkv_b"]),
        "out_w_t": a[l0a + "out_w"].T,
        "out_b": a[l0a + "out_b"],
        "ffn_w1_t": a[l0f + "W1"].T,
        "ffn_b1_cols": columns(a[l0f + "b1"]),
        "ffn_w2_t": a[l0f + "W2"].T,
        "ffn_b2": a[l0f + "b2"],
        **{w.lower() + "_t": a[l1a + w].T for w in ("Wq", "Wk", "Wv", "Wo", "Wg", "Wog", "Wd")},
        "bd": a[l1a + "bd"],
        "norm_cols": columns(a[l1a + "norm_w"]),
        "gate_w": a[l1f + "gate_W"],
        "moe_w1": a[l1f + "W1"],
        "moe_b1_cols": a[l1f + "b1"].T,
        "moe_w2": a[l1f + "W2"],
        "moe_b2": a[l1f + "b2"],
        "ws1": a[l1f + "Ws1"],
        "bs1_col": a[l1f + "bs1"].reshape(EH, 1),
        "ws2": a[l1f + "Ws2"],
        "bs2": a[l1f + "bs2"],
        "route_scale": a[l1f + "route_scale"].reshape(1, 1),
        "ident": np.eye(P, dtype=np.float32),
        **gla_constants(),
    }
    nc = bacc.Bacc("TRN2", target_bir_lowering=False, num_devices=1)
    arrays, args = {}, {}
    for name, v in laid_out.items():
        v = np.ascontiguousarray(v)
        arrays[f"in_{name}"] = v
        args[name] = nc.dram_tensor(f"in_{name}", v.shape, mybir.dt.from_np(v.dtype), kind="ExternalInput").ap()
    out = nc.dram_tensor("out", [TOKENS, D], F32, kind="ExternalOutput").ap()
    sandwich(nc, **args, out=out)
    r = run_bass_kernel_spmd(nc, [arrays], core_ids=[0])
    return r.results[0]["out"].reshape(BATCH, SEQ, D)
```

```python
from contextlib import ExitStack

import numpy as np
import concourse.bass as bass
from concourse import mybir

F32 = mybir.dt.float32
F32R = mybir.dt.float32r
BF16 = mybir.dt.bfloat16
ALU = mybir.AluOpType
ACT = mybir.ActivationFunctionType
AX = mybir.AxisListType

P = 128
BATCH, SEQ, D = 4, 1024, 256
TOKENS = BATCH * SEQ
ST = 512
NT = ST // P
NST = TOKENS // ST
KD = D // P
LN_EPS = 1e-5

AH, AD = 16, 16
HG = 4
NG = AH // HG
NBG = BATCH * NG
KT = SEQ // P
QH = SEQ // ST
VW = 32
Q_PART = (0, 1, 2, 0, 0, 1)
K_PART = (0, 1, 0, 1, 2, 0)
STACK = len(Q_PART) * AD
ROWS = STACK + 3

FF = 4 * D
FT = FF // P

GH, GD = 16, 64
HID = GH * GD
J = HID // P
RMS_EPS = float(np.finfo(np.float32).eps)

NE, EH = 8, 128


class Steps:

    def __init__(self, per):
        self.per, self.base, self.k = per, 0, 0

    def start(self, i):
        self.base, self.k = i * self.per, 0

    def inc(self):
        self.k += 1
        return 1

    def now(self):
        return self.base + self.k

    def end(self):
        assert self.k == self.per, (self.k, self.per)


def runs(part):
    found = []
    for block, a in enumerate(part):
        if found and found[-1][1] + found[-1][2] == a:
            found[-1][2] += 1
        else:
            found.append([block, a, 1])
    return found


def over_supertiles(eng, body):
    body(0, 0, False)
    body(1, 1, False)
    with eng.Fori(1, NST // 2 - 1) as k:
        body(2 * k, 0, False)
        body(2 * k + 1, 1, False)
    body(NST - 2, 0, False)
    body(NST - 1, 1, True)


def first(i, n):
    return isinstance(i, int) and i < n


def wait_past(eng, sem, value):
    if not isinstance(value, int) or value > 0:
        eng.wait_ge(sem, value)


def tokens(x):
    return x.rearrange("(i n p) c -> i p n c", p=P, n=NT)


def row(x):
    return x.rearrange("(a c) -> a c", a=1).to_broadcast([P, x.shape[0]])



LN = 2 * NT + 2


def tile_stats(nc, dve, x, st, mv, rs, stats, s):
    for n in range(NT):
        nc.vector.bn_stats(st[:, n, :], x[:, n, :]).then_inc(stats, s.inc())
    dve.wait_ge(stats, s.now())
    nc.vector.memset(rs[:, 0, :], LN_EPS).then_inc(stats, s.inc())
    for n in range(NT):
        nc.vector.bn_aggr(mv[:, n, :], st[:, n, :]).then_inc(stats, s.inc())
    dve.wait_ge(stats, s.now())
    nc.vector.tensor_tensor(rs[:, 0, :], mv[:, :, 1], rs[:, 0, :], ALU.add).then_inc(stats, s.inc())


def normalize_with(nc, dve, x, xn, mv, rs, rs_ready, rs_count, xn_ready):
    dve.wait_ge(rs_ready, rs_count)
    for n in range(NT):
        nc.vector.tensor_scalar(xn[:, n, :], x[:, n, :], mv[:, n, 0:1], rs[:, 1, n:n + 1],
                                ALU.subtract, ALU.mult).then_inc(xn_ready, 1)


def normalize_tiles(nc, dve, x, xn, st, mv, rs, stats, s, rs_ready, rs_count, xn_ready):
    tile_stats(nc, dve, x, st, mv, rs, stats, s)
    normalize_with(nc, dve, x, xn, mv, rs, rs_ready, rs_count, xn_ready)


def inverse_root(nc, pool, rs, half, stats, count, rs_ready):
    pool.wait_ge(stats, count)
    nc.gpsimd.tensor_tensor(rs[:, 1, :], rs[:, 0, :], half[:, 0:rs.shape[2]], ALU.pow).then_inc(rs_ready, 1)


def minus_half(nc, pool, half, half_set):
    nc.gpsimd.memset(half[:, :], -0.5).then_inc(half_set, 1)
    pool.wait_ge(half_set, 1)


def turn(nc, src, ps, ident, k):
    for n in range(NT):
        last = nc.tensor.transpose(ps[:, n * P:(n + 1) * P], src[:, n, k * P:(k + 1) * P], ident[:, :])
    return last


class Place:

    def __init__(self, nc, ctx, name):
        self.nc, self.ctx, self.name, self.taken = nc, ctx, name, []
        ctx.callback(self.clear)

    def clear(self):
        self.nc.clear_and_free_semaphores(self.taken)
        self.nc.all_engine_barrier()

    def sb(self, name, shape, dt=F32):
        return self.ctx.enter_context(self.nc.sbuf_tensor(f"{self.name}_sb_{name}", shape, dt))

    def ps(self, name, shape, dt=F32):
        return self.ctx.enter_context(self.nc.psum_tensor(f"{self.name}_ps_{name}", shape, dt))

    def sem(self, name):
        self.taken.append(self.nc.alloc_semaphore(f"{self.name}_{name}"))
        return self.taken[-1]

    def sems(self, name, n):
        return [self.sem(f"{name}{k}") for k in range(n)]


def phase_qkv(nc, x, w_t, bias, bias_cols, ident_d, parts, v_aug):
    with ExitStack() as ctx:
        m = Place(nc, ctx, "qkv")
        w = m.sb("w", [P, KD, 3 * D])
        ident = m.sb("ident", [P, P])
        b_in = m.sb("b_in", [P, 2 * KD])
        b_qk = m.sb("b_qk", [P, 2 * KD])
        b_v = m.sb("b_v", [P, D])
        xin = m.sb("xin", [P, 2, NT, D])
        xn = m.sb("xn", [P, NT, D])
        xT = m.sb("xT", [P, 2, KD, ST])
        st, mv, rs = m.sb("st", [P, NT, 6]), m.sb("mv", [P, NT, 2]), m.sb("rs", [P, 2, NT])
        half, half_set = m.sb("half", [P, NT]), m.sem("half_set")
        val = m.sb("val", [P, 4, ST])
        rest = m.sb("rest", [P, 4, ST])
        part = m.sb("part", [P, 4, 3, ST], BF16)
        va = m.sb("va", [P, 2, NT, AH, VW])
        psT = m.ps("psT", [P, KD, ST])
        psQ = m.ps("psQ", [P, 4, ST])
        psV = m.ps("psV", [P, NT, D])
        w_in, x_in = m.sem("w_in"), m.sems("x_in", 2)
        ln_step, xn_ready, turned, xT_ready = m.sem("ln_step"), m.sem("xn_ready"), m.sem("turned"), m.sem("xT_ready")
        rs_ready, bias_ready, va_ready0 = m.sem("rs_ready"), m.sem("bias_ready"), m.sem("va_const")
        qk_done, v_done, v_taken = m.sem("qk_done"), m.sem("v_done"), m.sem("v_taken")
        val_ready, mid_ready, rest_ready, lo_ready = (m.sem(s) for s in ("val_ready", "mid_ready", "rest_ready", "lo_ready"))
        part_out, v_out = m.sems("part_out", 4), m.sems("v_out", 2)
        xv = tokens(x)
        block = ctx.enter_context(nc.Block())

        @block.sync
        def _(sp):
            sp.dma_start(xin[:, 0, :, :], xv[0]).then_inc(x_in[0], 16)
            sp.dma_start(ident[:, :], ident_d).then_inc(w_in, 16)
            sp.dma_start(w[:, :, :], w_t.rearrange("(k p) o -> p k o", p=P)).then_inc(w_in, 16)
            sp.dma_start(b_in[:, :], bias_cols[:, 0:2 * KD]).then_inc(w_in, 16)
            sp.dma_start(b_v[:, :], row(bias[2 * D:3 * D])).then_inc(w_in, 16)
            sp.dma_start(xin[:, 1, :, :], xv[1]).then_inc(x_in[1], 16)

            def body(i, u, last):
                if not (isinstance(i, int) and i >= NST - 2):
                    sp.wait_ge(xn_ready, NT * (i + 1))
                    sp.dma_start(xin[:, u, :, :], xv[i + 2]).then_inc(x_in[u], 16)
                for mt in range(4):
                    sp.wait_ge(lo_ready, 4 * i + mt + 1)
                    for g in range(2):
                        sp.dma_start(parts[mt // 2, i, 2 * (mt % 2) + g].rearrange("a c t -> c a t"),
                                     part[64 * g:64 * g + 64, mt, :, :]).then_inc(part_out[mt], 16)
                sp.wait_ge(v_taken, NT * (i + 1))
                for g in range(NG):
                    sp.dma_start(v_aug[i, g], va[:, u, :, HG * g:HG * (g + 1), :].rearrange("p n h c -> p n (h c)")
                                 ).then_inc(v_out[u], 16)

            over_supertiles(sp, body)
            for s in part_out:
                sp.wait_ge(s, 32 * NST)
            for s in v_out:
                sp.wait_ge(s, 16 * NG * NST // 2)

        @block.vector
        def _(dve):
            s = Steps(LN)
            for u in range(2):
                nc.vector.memset(va[:, u, :, :, AD:AD + 1], 1.0).then_inc(va_ready0, 1)
                nc.vector.memset(va[:, u, :, :, AD + 1:VW], 0.0).then_inc(va_ready0, 1)
            dve.wait_ge(w_in, 64)
            nc.vector.tensor_scalar(b_qk[:, 0:KD], b_in[:, 0:KD], AD ** -0.5, None, ALU.mult).then_inc(bias_ready, 1)
            nc.vector.tensor_copy(b_qk[:, KD:2 * KD], b_in[:, KD:2 * KD]).then_inc(bias_ready, 1)
            dve.wait_ge(va_ready0, 4)

            def pre(i, u):
                s.start(i)
                dve.wait_ge(x_in[u], 8 * (i - u) + 16)
                if not first(i, 1):
                    dve.wait_ge(turned, KD * i)
                normalize_tiles(nc, dve, xin[:, u, :, :], xn, st, mv, rs, ln_step, s, rs_ready, i + 1, xn_ready)
                s.end()

            pre(0, 0)

            def body(i, u, last):
                if not last:
                    pre(i + 1, 1 - u)
                for mt in range(4):
                    dve.wait_ge(val_ready, 2 * (4 * i + mt) + 2)
                    if not first(i, 1):
                        dve.wait_ge(lo_ready, 4 * (i - 1) + mt + 1)
                    nc.vector.tensor_tensor(rest[:, mt, :], val[:, mt, :], part[:, mt, 0, :],
                                            ALU.subtract).then_inc(rest_ready, 1)
                for n in range(NT):
                    dve.wait_ge(v_done, 2 * i + n // 2 + 1)
                    if n == 0 and not first(i, 2):
                        dve.wait_ge(v_out[u], 8 * NG * (i - u))
                    nc.vector.tensor_tensor(va[:, u, n, :, 0:AD],
                                            psV[:, n, :].rearrange("p (h d) -> p h d", d=AD),
                                            b_v[:, :].rearrange("p (h d) -> p h d", d=AD),
                                            ALU.add).then_inc(v_taken, 1)

            over_supertiles(dve, body)

        @block.tensor
        def _(pe):
            pe.wait_ge(w_in, 64)

            def turn_in(i):
                pe.wait_ge(xn_ready, NT * (i + 1))
                if not first(i, 1):
                    pe.wait_ge(xT_ready, KD * i)
                for k in range(KD):
                    turn(nc, xn, psT[:, k, :], ident, k).then_inc(turned, 1)

            turn_in(0)

            def body(i, u, last):
                pe.wait_ge(xT_ready, KD * (i + 1))
                for mt in range(4):
                    if not first(i, 1):
                        pe.wait_ge(val_ready, 2 * (4 * (i - 1) + mt) + 2)
                    for k in range(KD):
                        mm = pe.matmul(psQ[:, mt, :], w[:, k, mt * P:(mt + 1) * P], xT[:, u, k, :],
                                       start=(k == 0), stop=(k == KD - 1))
                    mm.then_inc(qk_done, 1)
                if not last:
                    turn_in(i + 1)
                for n in range(NT):
                    if n % 2 == 0 and not first(i, 1):
                        pe.wait_ge(v_taken, NT * (i - 1) + n + 2)
                    for k in range(KD):
                        mm = pe.matmul(psV[:, n, :], xT[:, u, k, n * P:(n + 1) * P], w[:, k, 2 * D:3 * D],
                                       start=(k == 0), stop=(k == KD - 1))
                    if n % 2:
                        mm.then_inc(v_done, 1)

            over_supertiles(pe, body)

        @block.scalar
        def _(act):
            def take_turned(i, u):
                for k in range(KD):
                    act.wait_ge(turned, KD * i + k + 1)
                    nc.scalar.copy(xT[:, u, k, :], psT[:, k, :]).then_inc(xT_ready, 1)

            take_turned(0, 0)
            act.wait_ge(bias_ready, 2)

            def body(i, u, last):
                for mt in range(4):
                    act.wait_ge(qk_done, 4 * i + mt + 1)
                    if not first(i, 1):
                        act.wait_ge(part_out[mt], 32 * i)
                    scale = AD ** -0.5 if mt < KD else 1.0
                    nc.scalar.activation(val[:, mt, :], psQ[:, mt, :], ACT.Identity, bias=b_qk[:, mt:mt + 1],
                                         scale=scale).then_inc(val_ready, 1)
                    nc.scalar.activation(part[:, mt, 0, :], psQ[:, mt, :], ACT.Identity,
                                         bias=b_qk[:, mt:mt + 1], scale=scale).then_inc(val_ready, 1)
                    if mt:
                        act.wait_ge(rest_ready, 4 * i + mt)
                        nc.scalar.copy(part[:, mt - 1, 1, :], rest[:, mt - 1, :]).then_inc(mid_ready, 1)
                act.wait_ge(rest_ready, 4 * i + 4)
                nc.scalar.copy(part[:, 3, 1, :], rest[:, 3, :]).then_inc(mid_ready, 1)
                if not last:
                    take_turned(i + 1, 1 - u)

            over_supertiles(act, body)

        @block.gpsimd
        def _(pool):
            minus_half(nc, pool, half, half_set)
            inverse_root(nc, pool, rs, half, ln_step, LN, rs_ready)

            def body(i, u, last):
                if not last:
                    inverse_root(nc, pool, rs, half, ln_step, LN * (i + 2), rs_ready)
                for mt in range(4):
                    pool.wait_ge(mid_ready, 4 * i + mt + 1)
                    nc.gpsimd.tensor_tensor(part[:, mt, 2, :], rest[:, mt, :], part[:, mt, 1, :],
                                            ALU.subtract).then_inc(lo_ready, 1)

            over_supertiles(pool, body)


def phase_attention(nc, parts, v_aug, ident_d, att):
    with ExitStack() as ctx:
        m = Place(nc, ctx, "att")
        q = m.sb("q", [P, NG, QH, HG, ST], BF16)
        k = m.sb("k", [P, NG, HG, SEQ], BF16)
        v = m.sb("v", [P, NG, KT, HG * VW])
        ident, ident_b = m.sb("ident", [P, P]), m.sb("ident_b", [P, P], BF16)
        pt = m.sb("pt", [P, 2, HG, ST])
        mx = m.sb("mx", [P, HG, NT])
        mrest = m.sb("mrest", [P, HG * NT])
        mparts = m.sb("mparts", [P, 3, 32], BF16)
        mrow = m.sb("mrow", [3 * 32, P], BF16)
        osb = m.sb("osb", [P, ST])
        rden = m.sb("rden", [P, NT, HG])
        o = m.sb("o", [P, NT, HG, AD])
        psM = m.ps("psM", [P, 2, SEQ])
        psS = m.ps("psS", [P, 2, ST])
        psO = m.ps("psO", [P, ST])
        psX = m.ps("psX", [P, NT, P])
        psX_rows = psX[:, 0, :].bitcast(BF16)
        psX_heads = psX[:, :, :].rearrange("p n (j c) -> p n j c", c=VW)
        ident_in, ident_ready, ones_set = m.sem("ident_in"), m.sem("ident_ready"), m.sem("ones_set")
        first_in, second_in = m.sems("first_in", NG), m.sems("second_in", NG)
        maxima_done, maxima_free = m.sem("maxima_done"), m.sem("maxima_free")
        scores_done, exp_done = m.sem("scores_done"), m.sem("exp_done")
        pv_done = m.sem("pv_done")
        split, rows_turned, rows_ready, rows_in = (m.sem(s) for s in ("split", "rows_turned", "rows_ready", "rows_in"))
        osb_ready, o_turned, rden_ready, o_ready, o_out = (
            m.sem(s) for s in ("osb_ready", "o_turned", "rden_ready", "o_ready", "o_out"))
        att_v = tokens(att)
        CREDIT = 2
        OUT_STEP = 5
        OUT_AFTER = 2 * (OUT_STEP + 1)
        TILES = HG * NT
        FIRST = 16 * (QH * len(runs(K_PART)) + len(runs(Q_PART)))
        SECOND = 16 * (len(runs(Q_PART)) + QH)
        block = ctx.enter_context(nc.Block())

        def over_pairs(eng, body):
            for g in range(NG):
                body(0, g, False)
            with eng.Fori(1, BATCH - 1) as b:
                for g in range(NG):
                    body(b, g, False)
            for g in range(NG):
                body(BATCH - 1, g, g == NG - 1)

        def after(b, g):
            return (b, g + 1) if g < NG - 1 else (b + 1, 0)

        @block.sync
        def _(sp):
            sp.dma_start(ident[:, :], ident_d).then_inc(ident_in, 16)

            def load(b, g):
                def stack(t, dst, s, part, sem):
                    for block, a, n in runs(part):
                        sp.dma_start(dst[AD * block:AD * (block + n)],
                                     parts[t, 2 * b + s, g, a:a + n].rearrange("a (c h) t -> (a c) h t", h=HG)
                                     ).then_inc(sem, 16)

                stack(0, q[:, g, 0, :, :], 0, Q_PART, first_in[g])
                for s in range(QH):
                    stack(1, k[:, g, :, s * ST:(s + 1) * ST], s, K_PART, first_in[g])
                stack(0, q[:, g, 1, :, :], 1, Q_PART, second_in[g])
                for s in range(QH):
                    sp.dma_start(v[:, g, s * NT:(s + 1) * NT, :], v_aug[2 * b + s, g]).then_inc(second_in[g], 16)

            def rows(b, g, qh):
                u = 2 * (NG * b + g) + qh
                sp.wait_ge(rows_ready, u + 1)
                for a in range(3):
                    sp.dma_start(q[STACK + a:STACK + a + 1, g, qh, :, :].rearrange("p j t -> p (j t)"),
                                 mrow[32 * a:32 * a + TILES, :]).then_inc(rows_in, 16)

            def out(b, g, qh):
                sp.wait_ge(o_ready, 2 * (NG * b + g) + qh + 1)
                sp.dma_start(att_v[2 * b + qh][:, :, HG * AD * g:HG * AD * (g + 1)],
                             o[:, :, :, :].rearrange("p n j c -> p n (j c)")).then_inc(o_out, 16)

            for g in range(NG - 1):
                load(0, g)
            rows(0, 0, 0)

            def body(b, g, last):
                rows(b, g, 1)
                nb, ng = (b, NG - 1) if g == 0 else (b + 1, g - 1)
                if not (isinstance(nb, int) and nb >= BATCH):
                    sp.wait_ge(pv_done, CREDIT + 2 * KT * (NG * b + g))
                    load(nb, ng)
                if not last:
                    rows(*after(b, g), 0)
                out(b, g, 0)
                out(b, g, 1)

            over_pairs(sp, body)
            sp.wait_ge(o_out, 16 * 2 * NBG)

        @block.vector
        def _(dve):
            nc.vector.memset(mparts[:, :, :], 0.0).then_inc(maxima_free, CREDIT)
            nc.vector.memset(mrest[:, :], 0.0).then_inc(exp_done, CREDIT)
            nc.vector.memset(rden[:, :, :], 0.0).then_inc(pv_done, CREDIT)
            dve.wait_ge(ident_in, 16)
            nc.vector.tensor_copy(ident_b[:, :], ident[:, :]).then_inc(ident_ready, 1)

            def maxima(b, g, qh, tiles):
                u = 2 * (NG * b + g) + qh
                for t in tiles:
                    dve.wait_ge(maxima_done, TILES * u + t + 1)
                    nc.vector.tensor_reduce(mx[:, t // NT, t % NT:t % NT + 1], psM[:, t % 2, :], AX.X,
                                            ALU.max).then_inc(maxima_free, 1)

            def split_maxima(b, g, qh):
                u = 2 * (NG * b + g) + qh
                x = mx[:, :, :].rearrange("p j n -> p (j n)")
                dve.wait_ge(maxima_free, CREDIT + TILES * (u + 1))
                wait_past(dve, rows_turned, u)
                nc.vector.tensor_scalar(mparts[:, 0, 0:TILES], x, -1.0, None, ALU.mult).then_inc(split, 1)
                dve.wait_ge(split, 4 * u + 1)
                nc.vector.scalar_tensor_tensor(mrest[:, :], x, -1.0, mparts[:, 0, 0:TILES], ALU.mult,
                                               ALU.subtract).then_inc(split, 1)
                dve.wait_ge(split, 4 * u + 2)
                nc.vector.tensor_copy(mparts[:, 1, 0:TILES], mrest[:, :]).then_inc(split, 1)
                dve.wait_ge(split, 4 * u + 3)
                nc.vector.tensor_tensor(mparts[:, 2, 0:TILES], mrest[:, :], mparts[:, 1, 0:TILES],
                                        ALU.subtract).then_inc(split, 1)

            def normalize(u):
                dve.wait_ge(o_turned, u + 1)
                nc.vector.reciprocal(rden[:, :, :], psX_heads[:, :, :, AD]).then_inc(rden_ready, 1)
                dve.wait_ge(rden_ready, u + 1)
                wait_past(dve, o_out, 16 * u)
                nc.vector.tensor_tensor(
                    o[:, :, :, :], psX_heads[:, :, :, 0:AD],
                    rden[:, :, :].rearrange("p n (j c) -> p n j c", c=1).to_broadcast([P, NT, HG, AD]),
                    ALU.mult).then_inc(o_ready, 1)

            for qh in range(QH):
                maxima(0, 0, qh, range(TILES))
                split_maxima(0, 0, qh)

            def body(b, g, last):
                nb, ng = after(b, g)
                for qh in range(QH):
                    if not last:
                        maxima(nb, ng, qh, range(OUT_AFTER))
                    if not (isinstance(b, int) and b == 0 and g == 0 and qh == 0):
                        normalize(2 * (NG * b + g) + qh - 1)
                    if not last:
                        maxima(nb, ng, qh, range(OUT_AFTER, TILES))
                        split_maxima(nb, ng, qh)

            over_pairs(dve, body)
            normalize(2 * NBG - 1)

        @block.tensor
        def _(pe):
            def maxima_tile(b, g, qh, t):
                u = 2 * (NG * b + g) + qh
                j, n = t // NT, t % NT
                queries = q[0:STACK, g, qh, j, n * P:(n + 1) * P]

                pe.wait_ge(maxima_free, TILES * u + t + 1)
                for c in range(QH):
                    mm = pe.matmul(psM[:, t % 2, c * ST:(c + 1) * ST], queries,
                                   k[0:STACK, g, j, c * ST:(c + 1) * ST], start=True, stop=True)
                mm.then_inc(maxima_done, 1)

            def scores(g, qh, u, s, j):
                t = 4 * (KT * u + s) + j
                pe.wait_ge(exp_done, t + 1)
                pe.matmul(psS[:, j % 2, :], k[0:ROWS, g, j, s * P:(s + 1) * P],
                          q[0:ROWS, g, qh, j, :], start=True, stop=True).then_inc(scores_done, 1)

            def values(g, u, s):
                pe.wait_ge(exp_done, CREDIT + 4 * (KT * u + s) + 4)
                if s == 0:
                    wait_past(pe, osb_ready, u)
                for j in range(HG):
                    mm = pe.matmul(psO[VW * j:VW * (j + 1), :], v[:, g, s, VW * j:VW * (j + 1)],
                                   pt[:, s % 2, j, :], start=(s == 0), stop=(s == KT - 1),
                                   tile_position=(0, VW * j))
                mm.then_inc(pv_done, 1)

            def turn_rows(u):
                pe.wait_ge(split, 4 * (u + 1))
                pe.transpose(psX_rows[0:3 * 32, 0:P], mparts[:, :, :].rearrange("p a t -> p (a t)"),
                             ident_b[:, :]).then_inc(rows_turned, 1)

            def turn_out(u):
                pe.wait_ge(osb_ready, u + 1)
                for n in range(NT):
                    mm = pe.transpose(psX[:, n, :], osb[:, n * P:(n + 1) * P], ident[:, :])
                mm.then_inc(o_turned, 1)

            pe.wait_ge(ident_ready, 1)
            pe.wait_ge(first_in[0], FIRST)
            for qh in range(QH):
                if qh:
                    pe.wait_ge(second_in[0], SECOND)
                for t in range(TILES):
                    maxima_tile(0, 0, qh, t)
            turn_rows(0)
            pe.wait_ge(ones_set, 1)

            def body(b, g, last):
                p = NG * b + g
                nb, ng = after(b, g)
                start = isinstance(b, int) and b == 0 and g == 0
                if not last:
                    pe.wait_ge(first_in[ng], FIRST * (nb + 1))
                    pe.wait_ge(second_in[ng], SECOND * (nb + 1))
                for qh in range(QH):
                    u = 2 * p + qh
                    final = last and qh == 1
                    pe.wait_ge(rows_in, 16 * 3 * (u + 1))
                    for s in range(KT):
                        if s == 2 and not final:
                            pe.wait_ge(rows_ready, u + 1)
                            if not (start and qh == 0):
                                wait_past(pe, o_ready, u - 1)
                            turn_rows(u + 1)
                        if s == OUT_STEP and not (start and qh == 0):
                            pe.wait_ge(rows_ready, u + 1 if final else u + 2)
                            turn_out(u - 1)
                        for j in range(HG):
                            scores(g, qh, u, s, j)
                            if j % 2 == 0 and not last:
                                maxima_tile(nb, ng, qh, 2 * s + j // 2)
                            if j == 1:
                                if s:
                                    values(g, u, s - 1)
                                elif not (start and qh == 0):
                                    values(g if qh else (g - 1) % NG, u - 1, KT - 1)

            over_pairs(pe, body)
            values(NG - 1, 2 * NBG - 1, KT - 1)
            pe.wait_ge(o_ready, 2 * NBG - 1)
            turn_out(2 * NBG - 1)

        @block.scalar
        def _(act):
            def copy_rows(u):
                act.wait_ge(rows_turned, u + 1)
                wait_past(act, rows_in, 16 * 3 * u)
                nc.scalar.copy(mrow[:, :], psX_rows[0:3 * 32, 0:P]).then_inc(rows_ready, 1)

            copy_rows(0)

            def copy_outputs(u):
                act.wait_ge(pv_done, CREDIT + KT * (u + 1))
                wait_past(act, o_turned, u)
                nc.scalar.copy(osb[:, :], psO[:, :]).then_inc(osb_ready, 1)

            def body(b, g, last):
                for qh in range(QH):
                    u = 2 * (NG * b + g) + qh
                    for s in range(KT):
                        act.wait_ge(pv_done, KT * u + s + 1)
                        for j in range(HG):
                            act.wait_ge(scores_done, 4 * (KT * u + s) + j + 1)
                            nc.scalar.activation(pt[:, s % 2, j, :], psS[:, j % 2, :], ACT.Exp).then_inc(exp_done, 1)
                            if s == 0 and j == 2 and not (isinstance(b, int) and b == 0 and g == 0 and qh == 0):
                                copy_outputs(u - 1)
                        if s == 3 and not (last and qh == 1):
                            copy_rows(u + 1)

            over_pairs(act, body)
            copy_outputs(2 * NBG - 1)

        @block.gpsimd
        def _(pool):
            nc.gpsimd.memset(k[STACK:ROWS, :, :, :], 1.0).then_inc(ones_set, 1)


def phase_project_ffn(nc, x, att, wo_t, bo, w1_t, b1_cols, w2_t, b2, ident_d, x_out):
    with ExitStack() as ctx:
        m = Place(nc, ctx, "ffn")
        wo, b_o = m.sb("wo", [P, KD, D]), m.sb("b_o", [P, D])
        w1, w2 = m.sb("w1", [P, KD * FF]), m.sb("w2", [P, FT * D])
        t1, t2 = m.sb("t1", [P, KD, FF], F32R), m.sb("t2", [P, FT, D], F32R)
        wx = m.sb("wx", [P, FF * KD])
        part_sum, total = m.sb("part_sum", [P, 2, 65]), m.sb("total", [P, 2, 2])
        ones, ident = m.sb("ones", [P, P]), m.sb("ident", [P, P])
        b_h, b_y = m.sb("b_h", [P, FT]), m.sb("b_y", [P, D])
        half, half_set = m.sb("half", [P, NT]), m.sem("half_set")
        xin, ain = m.sb("xin", [P, NT, D]), m.sb("ain", [P, 2, NT, D])
        aT = m.sb("aT", [P, KD, ST])
        st1, mv1, rs1 = m.sb("st1", [P, NT, 6]), m.sb("mv1", [P, NT, 2]), m.sb("rs1", [P, 2, NT])
        st2, mv2, rs2 = m.sb("st2", [P, NT, 6]), m.sb("mv2", [P, NT, 2]), m.sb("rs2", [P, 2, NT])
        st3, mv3, rs3 = m.sb("st3", [P, NT, 6]), m.sb("mv3", [P, NT, 2]), m.sb("rs3", [P, 2, NT])
        a, an, x1 = m.sb("a", [P, NT, D]), m.sb("an", [P, NT, D]), m.sb("x1", [P, 2, NT, D])
        xn = m.sb("xn", [P, NT, D])
        xhi, xlo = m.sb("xhi", [P, 2, KD, ST], F32R), m.sb("xlo", [P, 2, KD, ST], F32R)
        h = m.sb("h", [P, 4, ST])
        hhi, hlo = m.sb("hhi", [P, 2, FT, ST], F32R), m.sb("hlo", [P, 2, FT, ST], F32R)
        y, yn, xo = m.sb("y", [P, NT, D]), m.sb("yn", [P, NT, D]), m.sb("xo", [P, 2, NT, D])
        psT = m.ps("psT", [P, KD, ST])
        psA = m.ps("psA", [P, NT, D])
        psH = m.ps("psH", [P, 2, ST])
        psY = m.ps("psY", [P, NT, D])
        first_in, const_in, w_in, x_in, a_in = m.sem("first_in"), m.sem("const_in"), m.sems("w_in", 2), m.sem("x_in"), m.sems("a_in", 2)
        ones_set, prep, summed, w_ready = m.sem("ones_set"), m.sem("prep"), m.sem("summed"), m.sem("w_ready")
        abs_ready = m.sem("abs_ready")
        a_turned, aT_ready, a_done, a_taken = m.sem("a_turned"), m.sem("aT_ready"), m.sem("a_done"), m.sem("a_taken")
        stats1, rs1_ready, an_ready, x1_ready = m.sem("stats1"), m.sem("rs1_ready"), m.sem("an_ready"), m.sem("x1_ready")
        stats2, rs2_ready, xn_ready = m.sem("stats2"), m.sem("rs2_ready"), m.sem("xn_ready")
        stats3, rs3_ready, yn_ready = m.sem("stats3"), m.sem("rs3_ready"), m.sem("yn_ready")
        x_turned, xhi_ready, xlo_ready = m.sem("x_turned"), m.sem("xhi_ready"), m.sem("xlo_ready")
        h_done, hhi_ready = m.sem("h_done"), m.sem("hhi_ready")
        hlo_even, hlo_odd = m.sem("hlo_even"), m.sem("hlo_odd")
        y_done, y_taken, residual_ready = m.sem("y_done"), m.sem("y_taken"), m.sem("residual_ready")
        xo_ready, x_outd = m.sem("xo_ready"), m.sems("x_out", 2)
        xv, av, ov = tokens(x), tokens(att), tokens(x_out)
        F2 = FT // 2
        N_FIRST, N_CONST = 16 * 3, 16 * 2
        block = ctx.enter_context(nc.Block())

        @block.sync
        def _(sp):
            sp.dma_start(ain[:, 0, :, :], av[0]).then_inc(a_in[0], 16)
            sp.dma_start(ident[:, :], ident_d).then_inc(first_in, 16)
            sp.dma_start(wo[:, :, :], wo_t.rearrange("(k p) o -> p k o", p=P)).then_inc(first_in, 16)
            sp.dma_start(b_o[:, :], row(bo)).then_inc(first_in, 16)
            sp.dma_start(w1[:, :].rearrange("p (k o) -> p k o", k=KD), w1_t.rearrange("(k p) o -> p k o", p=P)
                         ).then_inc(w_in[0], 16)
            sp.dma_start(xin[:, :, :], xv[0]).then_inc(x_in, 16)
            sp.dma_start(ain[:, 1, :, :], av[1]).then_inc(a_in[1], 16)
            sp.dma_start(w2[:, :].rearrange("p (k o) -> p k o", k=FT), w2_t.rearrange("(k p) o -> p k o", p=P)
                         ).then_inc(w_in[1], 16)
            sp.dma_start(b_h[:, :], b1_cols).then_inc(const_in, 16)
            sp.dma_start(b_y[:, :], row(b2)).then_inc(const_in, 16)

            sp.wait_ge(x1_ready, 1)
            sp.dma_start(xin[:, :, :], xv[1]).then_inc(x_in, 16)

            def body(i, u, last):
                more = not (isinstance(i, int) and i >= NST - 2)
                if more:
                    sp.wait_ge(a_turned, KD * (i + 1))
                    sp.dma_start(ain[:, u, :, :], av[i + 2]).then_inc(a_in[u], 16)
                if not first(i, 2):
                    sp.wait_ge(xo_ready, i - 1)
                    sp.dma_start(ov[i - 2], xo[:, u, :, :]).then_inc(x_outd[u], 16)
                if more:
                    sp.wait_ge(x1_ready, i + 2)
                    sp.dma_start(xin[:, :, :], xv[i + 2]).then_inc(x_in, 16)

            over_supertiles(sp, body)
            for i in (NST - 2, NST - 1):
                sp.wait_ge(xo_ready, i + 1)
                sp.dma_start(ov[i], xo[:, i % 2, :, :]).then_inc(x_outd[i % 2], 16)
            for s in x_outd:
                sp.wait_ge(s, 16 * NST // 2)

        @block.vector
        def _(dve):
            s1, s2, s3, t = Steps(LN), Steps(LN), Steps(LN), Steps(0)
            nc.vector.memset(ones[:, :], 1.0).then_inc(ones_set, 1)

            def take_projected(i):
                s1.start(i)
                dve.wait_ge(a_done, i + 1)
                if not first(i, 1):
                    dve.wait_ge(an_ready, NT * i)
                for n in range(NT):
                    nc.vector.tensor_tensor(a[:, n, :], psA[:, n, :], b_o[:, :], ALU.add).then_inc(a_taken, 1)
                dve.wait_ge(a_taken, NT * (i + 1))
                tile_stats(nc, dve, a, st1, mv1, rs1, stats1, s1)
                s1.end()

            def normalize_projected(i):
                if not first(i, 1):
                    dve.wait_ge(x1_ready, i)
                normalize_with(nc, dve, a, an, mv1, rs1, rs1_ready, i + 1, an_ready)

            def stats_of_x1(i, u):
                s2.start(i)
                dve.wait_ge(x1_ready, i + 1)
                tile_stats(nc, dve, x1[:, u, :, :], st2, mv2, rs2, stats2, s2)
                s2.end()

            def normalize_x1(i, u):
                if not first(i, 1):
                    dve.wait_ge(x_turned, KD * i)
                normalize_with(nc, dve, x1[:, u, :, :], xn, mv2, rs2, rs2_ready, i + 1, xn_ready)

            def take_turned(i, u):
                for k in range(KD):
                    dve.wait_ge(xhi_ready, KD * i + k + 1)
                    if k == 0 and not first(i, 2):
                        dve.wait_ge(h_done, FT * (i - 1))
                    nc.vector.tensor_tensor(xlo[:, u, k, :], psT[:, k, :], xhi[:, u, k, :],
                                            ALU.subtract).then_inc(xlo_ready, 1)

            def split_hidden(i, u, f):
                if f % 2 == 0:
                    dve.wait_ge(hhi_ready, FT * i + f + 1)
                    if f == 0 and not first(i, 2):
                        dve.wait_ge(y_done, 2 * (i - 1))
                    nc.vector.tensor_tensor(hlo[:, u, f, :], h[:, f % 4, :], hhi[:, u, f, :],
                                            ALU.subtract).then_inc(hlo_even, 1)

            def ternary(n, w, tern):
                dve.wait_ge(abs_ready, n + 1)
                nc.vector.tensor_reduce(part_sum[:, n, 0:64], wx[:, :].rearrange("p (a b) -> p a b", a=64), AX.X,
                                        ALU.add).then_inc(prep, t.inc())
                dve.wait_ge(prep, t.now())
                nc.vector.tensor_reduce(part_sum[:, n, 64:65], part_sum[:, n, 0:64], AX.X,
                                        ALU.add).then_inc(prep, t.inc())
                dve.wait_ge(summed, n + 1)
                nc.vector.tensor_scalar(total[:, n, 0:1], psY[:, 2 * n, 0:1], 1.0 / (FF * D), 1e-8, ALU.mult,
                                        ALU.max).then_inc(prep, t.inc())
                dve.wait_ge(prep, t.now())
                nc.vector.tensor_scalar(total[:, n, 0:1], total[:, n, 0:1], 0.5, None, ALU.mult).then_inc(prep, t.inc())
                dve.wait_ge(prep, t.now())
                nc.vector.tensor_scalar(total[:, n, 1:2], total[:, n, 0:1], -1.0, None, ALU.mult).then_inc(prep, t.inc())
                dve.wait_ge(prep, t.now())
                nc.vector.tensor_scalar(wx[:, :], w[:, :], total[:, n, 1:2], None, ALU.is_lt).then_inc(prep, t.inc())
                dve.wait_ge(prep, t.now())
                nc.vector.scalar_tensor_tensor(tern, w[:, :], total[:, n, 0:1], wx[:, :], ALU.is_gt,
                                               ALU.subtract).then_inc(w_ready, 1)

            dve.wait_ge(first_in, N_FIRST)
            take_projected(0)
            normalize_projected(0)
            ternary(0, w1, t1[:, :, :].rearrange("p k o -> p (k o)"))
            stats_of_x1(0, 0)
            normalize_x1(0, 0)
            take_turned(0, 0)
            take_projected(1)
            dve.wait_ge(const_in, N_CONST)

            def take_y(i, pair):
                dve.wait_ge(y_done, 2 * i + pair + 1)
                if pair == 0 and not first(i, 1):
                    dve.wait_ge(yn_ready, NT * i)
                tiles = slice(2 * pair, 2 * pair + 2)
                nc.vector.tensor_tensor(y[:, tiles, :], psY[:, tiles, :],
                                        b_y[:, :].rearrange("p (n c) -> p n c", n=1).to_broadcast([P, 2, D]),
                                        ALU.add).then_inc(y_taken, 1)

            def stats_of_y(i):
                s3.start(i)
                dve.wait_ge(y_taken, 2 * (i + 1))
                tile_stats(nc, dve, y, st3, mv3, rs3, stats3, s3)
                s3.end()

            def normalize_y(i):
                if not first(i, 1):
                    dve.wait_ge(xo_ready, i)
                normalize_with(nc, dve, y, yn, mv3, rs3, rs3_ready, i + 1, yn_ready)

            def body(i, u, last):
                if not last:
                    normalize_projected(i + 1)
                for f in range(FT):
                    split_hidden(i, u, f)
                    if f == 2 and not last:
                        stats_of_x1(i + 1, 1 - u)
                    if f == 4 and not last:
                        normalize_x1(i + 1, 1 - u)
                    if f == 5 and not first(i, 1):
                        take_y(i - 1, 0)
                if not last:
                    take_turned(i + 1, 1 - u)
                if not first(i, 1):
                    take_y(i - 1, 1)
                    stats_of_y(i - 1)
                if not (isinstance(i, int) and i >= NST - 2):
                    take_projected(i + 2)
                if not first(i, 1):
                    normalize_y(i - 1)
                else:
                    ternary(1, w2, t2[:, :, :].rearrange("p k o -> p (k o)"))

            over_supertiles(dve, body)
            take_y(NST - 1, 0)
            take_y(NST - 1, 1)
            stats_of_y(NST - 1)
            normalize_y(NST - 1)

        @block.tensor
        def _(pe):
            def turn_projected(i, u):
                pe.wait_ge(a_in[u], 8 * (i - u) + 16)
                if first(i, 2):
                    wait_past(pe, aT_ready, KD * i)
                else:
                    pe.wait_ge(xlo_ready, KD * (i - 1))
                for k in range(KD):
                    turn(nc, ain[:, u, :, :], psT[:, k, :], ident, k).then_inc(a_turned, 1)

            def multiply_projected(i):
                pe.wait_ge(aT_ready, KD * (i + 1))
                if not first(i, 1):
                    pe.wait_ge(a_taken, NT * i)
                for n in range(NT):
                    for k in range(KD):
                        mm = pe.matmul(psA[:, n, :], aT[:, k, n * P:(n + 1) * P], wo[:, k, :],
                                       start=(k == 0), stop=(k == KD - 1))
                mm.then_inc(a_done, 1)

            def turn_x(i):
                pe.wait_ge(xn_ready, NT * (i + 1))
                pe.wait_ge(aT_ready, KD * NST if isinstance(i, int) and i == NST - 1 else KD * (i + 2))
                for k in range(KD):
                    turn(nc, xn, psT[:, k, :], ident, k).then_inc(x_turned, 1)

            def sum_weights(n):
                pe.wait_ge(prep, 6 * n + 2)
                pe.matmul(psY[:, 2 * n, 0:1], ones[:, :], part_sum[:, n, 64:65], start=True,
                          stop=True).then_inc(summed, 1)

            def hidden(i, u, f):
                if not (first(i, 1) and f < 2):
                    pe.wait_ge(hhi_ready, FT * i + f - 1)
                for k in range(KD):
                    w = t1[:, k, f * P:(f + 1) * P]
                    pe.matmul(psH[:, f % 2, :], w, xhi[:, u, k, :], start=(k == 0), stop=False)
                    mm = pe.matmul(psH[:, f % 2, :], w, xlo[:, u, k, :], start=False, stop=(k == KD - 1))
                mm.then_inc(h_done, 1)

            def y_part(i, u, n, part):
                cols = slice(n * P, (n + 1) * P)
                if part == 0 and n % 2 == 0 and not first(i, 1):
                    pe.wait_ge(y_taken, 2 * (i - 1) + n // 2 + 1)
                for f in range(F2 * part, F2 * (part + 1)):
                    if n == 0:
                        pe.wait_ge(hlo_odd if f % 2 else hlo_even, F2 * i + f // 2 + 1)
                    pe.matmul(psY[:, n, :], hhi[:, u, f, cols], t2[:, f, :], start=(f == 0), stop=False)
                    mm = pe.matmul(psY[:, n, :], hlo[:, u, f, cols], t2[:, f, :], start=False, stop=(f == FT - 1))
                if part and n % 2:
                    mm.then_inc(y_done, 1)

            pe.wait_ge(first_in, N_FIRST)
            turn_projected(0, 0)
            multiply_projected(0)
            turn_projected(1, 1)
            pe.wait_ge(ones_set, 1)
            sum_weights(0)
            turn_x(0)
            multiply_projected(1)
            pe.wait_ge(w_ready, 1)
            pe.wait_ge(xlo_ready, KD)

            def body(i, u, last):
                more = not (isinstance(i, int) and i >= NST - 2)
                if not first(i, 1):
                    pe.wait_ge(xlo_ready, KD * (i + 1))
                hidden(i, u, 0)
                for f in range(1, FT):
                    hidden(i, u, f)
                    if f == 3 and more:
                        turn_projected(i + 2, u)
                    if not first(i, 1) and f < FT - 1:
                        y_part(i - 1, 1 - u, (f - 1) // 2, (f - 1) % 2)
                if not last:
                    turn_x(i + 1)
                if not first(i, 1):
                    y_part(i - 1, 1 - u, NT - 1, 0)
                    y_part(i - 1, 1 - u, NT - 1, 1)
                if more:
                    multiply_projected(i + 2)
                if first(i, 1):
                    sum_weights(1)
                    pe.wait_ge(w_ready, 2)

            over_supertiles(pe, body)
            for n in range(NT):
                for part in range(2):
                    y_part(NST - 1, 1, n, part)

        @block.scalar
        def _(act):
            def copy_projected(i):
                for k in range(KD):
                    act.wait_ge(a_turned, KD * i + k + 1)
                    if k == 0 and not first(i, 1):
                        act.wait_ge(a_done, i)
                    nc.scalar.copy(aT[:, k, :], psT[:, k, :]).then_inc(aT_ready, 1)

            def take_turned(i, u):
                for k in range(KD):
                    act.wait_ge(x_turned, KD * i + k + 1)
                    nc.scalar.copy(xhi[:, u, k, :], psT[:, k, :]).then_inc(xhi_ready, 1)

            def copy_residual(i, u):
                act.wait_ge(x1_ready, i + 1)
                if not first(i, 2):
                    act.wait_ge(x_outd[u], 8 * (i - u))
                nc.scalar.copy(xo[:, u, :, :], x1[:, u, :, :]).then_inc(residual_ready, 1)

            copy_projected(0)
            copy_projected(1)
            for n, w in ((0, w1), (1, w2)):
                act.wait_ge(w_in[n], 16)
                if n:
                    act.wait_ge(w_ready, n)
                nc.scalar.activation(wx[:, :], w[:, :], ACT.Abs).then_inc(abs_ready, 1)
                if n == 0:
                    take_turned(0, 0)

            act.wait_ge(const_in, N_CONST)

            def body(i, u, last):
                more = not (isinstance(i, int) and i >= NST - 2)
                for f in range(FT):
                    act.wait_ge(h_done, FT * i + f + 1)
                    if not (first(i, 1) and f < 4):
                        act.wait_ge(hlo_odd if f % 2 else hlo_even, F2 * i + f // 2 - 1)
                    nc.scalar.activation(h[:, f % 4, :], psH[:, f % 2, :], ACT.Gelu, bias=b_h[:, f:f + 1])
                    if f == 0 and not first(i, 2):
                        act.wait_ge(y_done, 2 * (i - 1))
                    nc.scalar.activation(hhi[:, u, f, :], psH[:, f % 2, :], ACT.Gelu,
                                         bias=b_h[:, f:f + 1]).then_inc(hhi_ready, 1)
                    if f == 3 and more:
                        copy_projected(i + 2)
                if not last:
                    take_turned(i + 1, 1 - u)
                copy_residual(i, u)

            over_supertiles(act, body)

        @block.gpsimd
        def _(pool):
            def roots(rs, stats, i, ready):
                inverse_root(nc, pool, rs, half, stats, LN * (i + 1), ready)

            def add_projected(i, u):
                pool.wait_ge(an_ready, NT * (i + 1))
                pool.wait_ge(x_in, 16 * (i + 1))
                if not first(i, 2):
                    pool.wait_ge(residual_ready, i - 1)
                    pool.wait_ge(xn_ready, NT * (i - 1))
                nc.gpsimd.tensor_tensor(x1[:, u, :, :], xin[:, :, :], an[:, :, :], ALU.add).then_inc(x1_ready, 1)

            def split_hidden(i, u, f):
                pool.wait_ge(hhi_ready, FT * i + f + 1)
                nc.gpsimd.tensor_tensor(hlo[:, u, f, :], h[:, f % 4, :], hhi[:, u, f, :], ALU.subtract).then_inc(hlo_odd, 1)

            def add_out(i, u):
                pool.wait_ge(yn_ready, NT * (i + 1))
                pool.wait_ge(residual_ready, i + 1)
                nc.gpsimd.tensor_tensor(xo[:, u, :, :], xo[:, u, :, :], yn[:, :, :], ALU.add).then_inc(xo_ready, 1)

            minus_half(nc, pool, half, half_set)
            roots(rs1, stats1, 0, rs1_ready)
            add_projected(0, 0)
            roots(rs2, stats2, 0, rs2_ready)
            roots(rs1, stats1, 1, rs1_ready)

            def body(i, u, last):
                if not last:
                    add_projected(i + 1, 1 - u)
                split_hidden(i, u, 1)
                if not last:
                    roots(rs2, stats2, i + 1, rs2_ready)
                if not first(i, 2):
                    add_out(i - 2, u)
                split_hidden(i, u, 3)
                split_hidden(i, u, 5)
                split_hidden(i, u, 7)
                if not first(i, 1):
                    roots(rs3, stats3, i - 1, rs3_ready)
                if not (isinstance(i, int) and i >= NST - 2):
                    roots(rs1, stats1, i + 2, rs1_ready)

            over_supertiles(pool, body)
            add_out(NST - 2, 0)
            roots(rs3, stats3, NST - 1, rs3_ready)
            add_out(NST - 1, 1)


def phase_experts(nc, x, gate_w, w1, b1_cols, w2, b2, ws1, bs1_col, ws2, bs2, route_scale, ident_d, x_out):
    BIG = 3.0e38
    with ExitStack() as ctx:
        m = Place(nc, ctx, "moe")
        wg = m.sb("wg", [P, KD, NE])
        wa, wb = m.sb("wa", [P, KD, NE + 1, EH]), m.sb("wb", [P, NE + 1, D])
        wa_hi, wa_lo = m.sb("wa_hi", [P, KD, NE + 1, EH], F32R), m.sb("wa_lo", [P, KD, NE + 1, EH], F32R)
        wb_hi, wb_lo = m.sb("wb_hi", [P, NE + 1, D], F32R), m.sb("wb_lo", [P, NE + 1, D], F32R)
        b_h, b_e, b_s = m.sb("b_h", [P, NE + 1]), m.sb("b_e", [NE, D]), m.sb("b_s", [P, D])
        r_scale, order = m.sb("r_scale", [P, 1]), m.sb("order", [P, NT, NE])
        ident = m.sb("ident", [P, P])
        half, half_set = m.sb("half", [P, NT]), m.sem("half_set")
        xin = m.sb("xin", [P, 2, NT, D])
        xn = m.sb("xn", [P, NT, D])
        xT = m.sb("xT", [P, KD, ST])
        xhi, xlo = m.sb("xhi", [P, 2, KD, ST], F32R), m.sb("xlo", [P, 2, KD, ST], F32R)
        h = m.sb("h", [P, 3, ST])
        hhi, hlo = m.sb("hhi", [P, 2, NE + 1, ST], F32R), m.sb("hlo", [P, 2, NE + 1, ST], F32R)
        st, mv, rs = m.sb("st", [P, NT, 6]), m.sb("mv", [P, NT, 2]), m.sb("rs", [P, 2, NT])
        st2, mv2, rs2 = m.sb("st2", [P, NT, 6]), m.sb("mv2", [P, NT, 2]), m.sb("rs2", [P, 2, NT])
        y, yn, xo = m.sb("y", [P, 2, NT, D]), m.sb("yn", [P, NT, D]), m.sb("xo", [P, 2, NT, D])
        sig, score, pick, sel1, sel2 = (m.sb(s, [P, NT, NE]) for s in ("sig", "score", "pick", "sel1", "sel2"))
        gates, gT = m.sb("gates", [P, 2, NT, NE]), m.sb("gT", [NE, 2, ST])
        best1, best2, rank = (m.sb(s, [P, NT]) for s in ("best1", "best2", "rank"))
        psT = m.ps("psT", [P, ST])
        psH = m.ps("psH", [P, 2, ST])
        psG = m.ps("psG", [P, ST])
        psX = (psT, psG)
        psY = m.ps("psY", [P, 4, 2, D])
        ident_in, const_in, w_in, x_in = m.sem("ident_in"), m.sem("const_in"), m.sems("w_in", 2), m.sems("x_in", 2)
        w_hi_ready, w_lo_ready = m.sem("w_hi_ready"), m.sem("w_lo_ready")
        stats, rs_ready, xn_ready = m.sem("stats"), m.sem("rs_ready"), m.sem("xn_ready")
        stats2, rs2_ready, yn_ready = m.sem("stats2"), m.sem("rs2_ready"), m.sem("yn_ready")
        turned, xT_ready, xlo_ready = m.sem("turned"), m.sem("xT_ready"), m.sem("xlo_ready")
        logits_done, sig_ready, route, gates_ready = m.sem("logits_done"), m.sem("sig_ready"), m.sem("route"), m.sem("gates_ready")
        g_turned, gT_ready, order_set = m.sem("g_turned"), m.sem("gT_ready"), m.sem("order_set")
        h_done, h_ready, hlo_ready = m.sem("h_done"), m.sem("h_ready"), m.sem("hlo_ready")
        y_done, y_added, y_summed, residual_ready = (m.sem(s) for s in ("y_done", "y_added", "y_summed", "residual_ready"))
        y_scaled = m.sem("y_scaled")
        xo_ready, x_outd = m.sem("xo_ready"), m.sems("x_out", 2)
        xv, ov = tokens(x), tokens(x_out)
        E = NE + 1
        N_CONST, UNITS = 16 * 6, 1 + NE // 2
        ADDS = E - 1
        block = ctx.enter_context(nc.Block())

        @block.sync
        def _(sp):
            sp.dma_start(xin[:, 0, :, :], xv[0]).then_inc(x_in[0], 16)
            sp.dma_start(ident[:, :], ident_d).then_inc(ident_in, 16)
            for k in range(KD):
                sp.dma_start(wa[:, k, 0:NE, :], w1[:, k * P:(k + 1) * P, :].rearrange("e p h -> p e h")).then_inc(w_in[0], 16)
            sp.dma_start(wa[:, :, NE, :], ws1.rearrange("(k p) h -> p k h", p=P)).then_inc(w_in[0], 16)
            sp.dma_start(wg[:, :, :], gate_w.rearrange("(k p) e -> p k e", p=P)).then_inc(const_in, 16)
            sp.dma_start(r_scale[:, :], route_scale.to_broadcast([P, 1])).then_inc(const_in, 16)
            sp.dma_start(b_h[:, 0:NE], b1_cols).then_inc(const_in, 16)
            sp.dma_start(b_h[:, NE:NE + 1], bs1_col).then_inc(const_in, 16)
            sp.dma_start(b_e[:, :], b2).then_inc(const_in, 16)
            sp.dma_start(b_s[:, :], row(bs2)).then_inc(const_in, 16)
            sp.dma_start(wb[:, 0:NE, :], w2.rearrange("e h d -> h e d")).then_inc(w_in[1], 16)
            sp.dma_start(wb[:, NE, :], ws2).then_inc(w_in[1], 16)
            sp.dma_start(xin[:, 1, :, :], xv[1]).then_inc(x_in[1], 16)

            def body(i, u, last):
                if not first(i, 2):
                    sp.wait_ge(xo_ready, i - 1)
                    sp.dma_start(ov[i - 2], xo[:, u, :, :]).then_inc(x_outd[u], 16)
                if not (isinstance(i, int) and i >= NST - 2):
                    sp.wait_ge(residual_ready, i + 1)
                    sp.dma_start(xin[:, u, :, :], xv[i + 2]).then_inc(x_in[u], 16)

            over_supertiles(sp, body)
            for i in (NST - 2, NST - 1):
                sp.wait_ge(xo_ready, i + 1)
                sp.dma_start(ov[i], xo[:, i % 2, :, :]).then_inc(x_outd[i % 2], 16)
            for s in x_outd:
                sp.wait_ge(s, 16 * NST // 2)

        @block.vector
        def _(dve):
            ROUTE = 1 + 5 + 2 + 5 + 4
            s, s2, r = Steps(LN), Steps(LN), Steps(ROUTE)
            for e in range(NE):
                nc.vector.memset(order[:, :, e:e + 1], float(NE - e)).then_inc(order_set, 1)

            def pre(i, u):
                s.start(i)
                dve.wait_ge(x_in[u], 8 * (i - u) + 16)
                if not first(i, 1):
                    dve.wait_ge(turned, KD * i)
                normalize_tiles(nc, dve, xin[:, u, :, :], xn, st, mv, rs, stats, s, rs_ready, i + 1, xn_ready)
                s.end()

            def wide(a):
                return a[:, :].rearrange("p (n e) -> p n e", e=1).to_broadcast([P, NT, NE])

            def choose(best, sel):
                nc.vector.tensor_reduce(best[:, :], score[:, :, :], AX.X, ALU.max).then_inc(route, r.inc())
                dve.wait_ge(route, r.now())
                nc.vector.tensor_tensor(pick[:, :, :], score[:, :, :], wide(best), ALU.is_ge).then_inc(route, r.inc())
                dve.wait_ge(route, r.now())
                nc.vector.tensor_tensor(pick[:, :, :], pick[:, :, :], order[:, :, :], ALU.mult).then_inc(route, r.inc())
                dve.wait_ge(route, r.now())
                nc.vector.tensor_reduce(rank[:, :], pick[:, :, :], AX.X, ALU.max).then_inc(route, r.inc())
                dve.wait_ge(route, r.now())
                nc.vector.tensor_tensor(sel[:, :, :], pick[:, :, :], wide(rank), ALU.is_ge).then_inc(route, r.inc())
                dve.wait_ge(route, r.now())

            def route_tokens(i, u):
                r.start(i)
                dve.wait_ge(sig_ready, i + 1)
                nc.vector.tensor_scalar(score[:, :, :], sig[:, :, :], r_scale[:, 0:1], None,
                                        ALU.mult).then_inc(route, r.inc())
                dve.wait_ge(route, r.now())
                choose(best1, sel1)
                if not first(i, 2):
                    dve.wait_ge(y_scaled, NT * (i - 1))
                    dve.wait_ge(g_turned, i - 1)
                nc.vector.tensor_tensor(gates[:, u, :, :], score[:, :, :], sel1[:, :, :], ALU.mult).then_inc(route, r.inc())
                dve.wait_ge(route, r.now())
                nc.vector.scalar_tensor_tensor(score[:, :, :], sel1[:, :, :], -BIG, score[:, :, :], ALU.mult,
                                               ALU.add).then_inc(route, r.inc())
                dve.wait_ge(route, r.now())
                choose(best2, sel2)
                nc.vector.tensor_tensor(sel2[:, :, :], score[:, :, :], sel2[:, :, :], ALU.mult).then_inc(route, r.inc())
                nc.vector.tensor_tensor(rank[:, :], best1[:, :], best2[:, :], ALU.add).then_inc(route, r.inc())
                dve.wait_ge(route, r.now())
                nc.vector.reciprocal(best1[:, :], rank[:, :]).then_inc(route, r.inc())
                nc.vector.tensor_tensor(gates[:, u, :, :], gates[:, u, :, :], sel2[:, :, :], ALU.add).then_inc(route, r.inc())
                dve.wait_ge(route, r.now())
                nc.vector.tensor_tensor(gates[:, u, :, :], gates[:, u, :, :], wide(best1), ALU.mult).then_inc(gates_ready, 1)
                r.end()

            def take_turned(i, u):
                for k in range(KD):
                    dve.wait_ge(xT_ready, KD * i + k + 1)
                    if k == 0 and not first(i, 2):
                        dve.wait_ge(h_done, E * (i - 1))
                    nc.vector.tensor_tensor(xlo[:, u, k, :], psX[k][:, :], xhi[:, u, k, :], ALU.subtract).then_inc(xlo_ready, 1)

            def add_outputs(i, u, n):
                added = NT * ADDS * i + ADDS * n
                if n == 0:
                    if not first(i, 1):
                        dve.wait_ge(yn_ready, NT * i)
                    dve.wait_ge(gates_ready, i + 1)
                for c in range(UNITS):
                    dve.wait_ge(y_done, UNITS * (NT * i + n) + c + 1)
                    bank = (UNITS * n + c) % 4
                    if c == 0:
                        nc.vector.tensor_tensor(y[:, 0, n, :], psY[:, bank, 0, :], b_s[:, :],
                                                ALU.add).then_inc(y_added, 1)
                        continue
                    for hf in range(2):
                        e = 2 * (c - 1) + hf
                        if e == 1:
                            continue
                        if e == 3:
                            dve.wait_ge(y_scaled, NT * i + n + 1)
                        else:
                            dve.wait_ge(y_added, added + {0: 1, 2: 2}.get(e, e - 1))
                        nc.vector.scalar_tensor_tensor(y[:, hf, n, :], psY[:, bank, hf, :], gates[:, u, n, e:e + 1],
                                                       y[:, hf, n, :], ALU.mult, ALU.add).then_inc(y_added, 1)

            def normalize_y(i):
                s2.start(i)
                dve.wait_ge(y_added, NT * ADDS * (i + 1))
                nc.vector.tensor_tensor(y[:, 0, :, :], y[:, 0, :, :], y[:, 1, :, :], ALU.add).then_inc(y_summed, 1)
                dve.wait_ge(y_summed, i + 1)
                if not first(i, 1):
                    dve.wait_ge(xo_ready, i)
                normalize_tiles(nc, dve, y[:, 0, :, :], yn, st2, mv2, rs2, stats2, s2, rs2_ready, i + 1, yn_ready)
                s2.end()

            pre(0, 0)
            for n, (w, hi, lo) in enumerate(((wa, wa_hi, wa_lo), (wb, wb_hi, wb_lo))):
                dve.wait_ge(w_hi_ready, n + 1)
                shape = "p k e h -> p (k e h)" if n == 0 else "p e h -> p (e h)"
                everything = (slice(None),) * len(w.shape)
                nc.vector.tensor_tensor(lo[everything].rearrange(shape), w[everything].rearrange(shape),
                                        hi[everything].rearrange(shape), ALU.subtract).then_inc(w_lo_ready, 1)
                if n == 0:
                    take_turned(0, 0)
            dve.wait_ge(const_in, N_CONST)
            dve.wait_ge(order_set, NE)

            def body(i, u, last):
                before = not first(i, 1)
                if before:
                    add_outputs(i - 1, 1 - u, 0)
                route_tokens(i, u)
                if before:
                    add_outputs(i - 1, 1 - u, 1)
                if not last:
                    pre(i + 1, 1 - u)
                if before:
                    add_outputs(i - 1, 1 - u, 2)
                if not last:
                    take_turned(i + 1, 1 - u)
                if before:
                    add_outputs(i - 1, 1 - u, 3)
                    normalize_y(i - 1)

            over_supertiles(dve, body)
            for n in range(NT):
                add_outputs(NST - 1, 1, n)
            normalize_y(NST - 1)

        @block.tensor
        def _(pe):
            def turn_in(i, k):
                if k == 0:
                    pe.wait_ge(xn_ready, NT * (i + 1))
                if not first(i, 1):
                    if k == 0:
                        pe.wait_ge(xlo_ready, KD * i)
                    else:
                        pe.wait_ge(gT_ready, i)
                turn(nc, xn, psX[k], ident, k).then_inc(turned, 1)

            def hidden(i, u, e):
                c = E * i + e
                if not (first(i, 1) and e < 2):
                    pe.wait_ge(h_ready, c - 1)
                for k in range(KD):
                    for p, (w, v) in enumerate(((wa_hi, xhi), (wa_hi, xlo), (wa_lo, xhi))):
                        mm = pe.matmul(psH[:, (e + u) % 2, :], w[:, k, e, :], v[:, u, k, :],
                                       start=(k == 0 and p == 0), stop=(k == KD - 1 and p == 2))
                mm.then_inc(h_done, 1)

            def outputs(i, u, g):
                n, c = g // UNITS, g % UNITS
                cols, bank = slice(n * P, (n + 1) * P), g % 4
                if g == 0:
                    pe.wait_ge(hlo_ready, E * (i + 1))
                    pe.wait_ge(gT_ready, i + 1)
                if not (first(i, 1) and g < 4):
                    g4 = g - 4 if g >= 4 else UNITS * NT + g - 4
                    before = ADDS * (g4 // UNITS) + max(2 * (g4 % UNITS), 1)
                    pe.wait_ge(y_added, NT * ADDS * (i if g >= 4 else i - 1) + before)
                    if g4 % UNITS == 1:
                        pe.wait_ge(y_scaled, NT * (i if g >= 4 else i - 1) + g4 // UNITS + 1)

                def product(hf, e, start):
                    for p, (v, w) in enumerate(((hhi, wb_hi), (hlo, wb_hi), (hhi, wb_lo))):
                        mm = pe.matmul(psY[:, bank, hf, :], v[:, u, e, cols], w[:, e, :], start=(start and p == 0),
                                       stop=(p == 2))
                    return mm

                if c == 0:
                    pe.matmul(psY[:, bank, 0, :], gT[:, u, cols], b_e[:, :], start=True, stop=False)
                    mm = product(0, NE, False)
                else:
                    for hf in range(2):
                        mm = product(hf, 2 * (c - 1) + hf, True)
                mm.then_inc(y_done, 1)

            pe.wait_ge(ident_in, 16)
            for k in range(KD):
                turn_in(0, k)
            pe.wait_ge(const_in, N_CONST)
            pe.wait_ge(w_lo_ready, 1)

            def body(i, u, last):
                before = not first(i, 1)
                pe.wait_ge(xT_ready, KD * (i + 1))
                pe.wait_ge(xlo_ready, KD * (i + 1))
                for n in range(NT):
                    for k in range(KD):
                        mm = pe.matmul(psG[:, n * NE:(n + 1) * NE], xT[:, k, n * P:(n + 1) * P], wg[:, k, :],
                                       start=(k == 0), stop=(k == KD - 1))
                mm.then_inc(logits_done, 1)
                for e in range(E):
                    hidden(i, u, e)
                    if before:
                        if e:
                            outputs(i - 1, 1 - u, 2 * e - 2)
                            outputs(i - 1, 1 - u, 2 * e - 1)
                    if e == 6:
                        pe.wait_ge(gates_ready, i + 1)
                        for n in range(NT):
                            mm = pe.transpose(psG[0:NE, n * P:(n + 1) * P], gates[:, u, n, :], ident[:, :])
                        mm.then_inc(g_turned, 1)
                    if e >= 7 and not last:
                        turn_in(i + 1, e - 7)
                if first(i, 1):
                    pe.wait_ge(w_lo_ready, 2)
                if before:
                    for g in range(2 * NE, UNITS * NT):
                        outputs(i - 1, 1 - u, g)

            over_supertiles(pe, body)
            for g in range(UNITS * NT):
                outputs(NST - 1, 1, g)

        @block.scalar
        def _(act):
            def take_turned(i, u, k):
                act.wait_ge(turned, KD * i + k + 1)
                if k == 0 and not first(i, 1):
                    act.wait_ge(logits_done, i)
                nc.scalar.copy(xT[:, k, :], psX[k][:, :])
                nc.scalar.copy(xhi[:, u, k, :], psX[k][:, :]).then_inc(xT_ready, 1)

            for n, (w, hi) in enumerate(((wa, wa_hi), (wb, wb_hi))):
                act.wait_ge(w_in[n], 48 if n == 0 else 32)
                everything = (slice(None),) * len(w.shape)
                nc.scalar.copy(hi[everything], w[everything]).then_inc(w_hi_ready, 1)
                if n == 0:
                    for k in range(KD):
                        take_turned(0, 0, k)
            act.wait_ge(const_in, N_CONST)

            def scale_first_odd(i, u, n):
                if n == 0:
                    act.wait_ge(gates_ready, i + 1)
                    if not first(i, 1):
                        act.wait_ge(yn_ready, NT * i)
                act.wait_ge(y_added, ADDS * (NT * i + n) + 2)
                nc.scalar.mul(y[:, 1, n, :], psY[:, (UNITS * n + 1) % 4, 1, :],
                              gates[:, u, n, 1:2]).then_inc(y_scaled, 1)

            def body(i, u, last):
                act.wait_ge(logits_done, i + 1)
                if not first(i, 1):
                    act.wait_ge(gates_ready, i)
                nc.scalar.activation(sig[:, :, :], psG[:, 0:NT * NE].rearrange("p (n e) -> p n e", e=NE),
                                     ACT.Sigmoid).then_inc(sig_ready, 1)
                for e in range(E):
                    act.wait_ge(h_done, E * i + e + 1)
                    if not (first(i, 1) and e < 3):
                        act.wait_ge(hlo_ready, E * i + e - 2)
                    if e == 0 and not first(i, 2):
                        act.wait_ge(y_done, UNITS * NT * (i - 1))
                    nc.scalar.activation(h[:, e % 3, :], psH[:, (e + u) % 2, :], ACT.Gelu, bias=b_h[:, e:e + 1])
                    nc.scalar.activation(hhi[:, u, e, :], psH[:, (e + u) % 2, :], ACT.Gelu,
                                         bias=b_h[:, e:e + 1]).then_inc(h_ready, 1)
                    if e == 6:
                        act.wait_ge(g_turned, i + 1)
                        if not first(i, 2):
                            act.wait_ge(y_done, UNITS * NT * (i - 1))
                        nc.scalar.copy(gT[:, u, :], psG[0:NE, :]).then_inc(gT_ready, 1)
                    if e >= 7 and not last:
                        take_turned(i + 1, 1 - u, e - 7)
                    if e in (2, 5, 7) and not first(i, 1):
                        scale_first_odd(i - 1, 1 - u, (2, 5, 7).index(e))
                if not first(i, 1):
                    scale_first_odd(i - 1, 1 - u, NT - 1)
                act.wait_ge(x_in[u], 8 * (i - u) + 16)
                if not first(i, 2):
                    act.wait_ge(x_outd[u], 8 * (i - u))
                nc.scalar.copy(xo[:, u, :, :], xin[:, u, :, :]).then_inc(residual_ready, 1)

            over_supertiles(act, body)
            for n in range(NT):
                scale_first_odd(NST - 1, 1, n)

        @block.gpsimd
        def _(pool):
            def add_out(i, u):
                pool.wait_ge(yn_ready, NT * (i + 1))
                pool.wait_ge(residual_ready, i + 1)
                nc.gpsimd.tensor_tensor(xo[:, u, :, :], xo[:, u, :, :], yn[:, :, :], ALU.add).then_inc(xo_ready, 1)

            minus_half(nc, pool, half, half_set)
            inverse_root(nc, pool, rs, half, stats, LN, rs_ready)

            def body(i, u, last):
                if not first(i, 2):
                    add_out(i - 2, u)
                for e in range(E):
                    if e == 5 and not last:
                        inverse_root(nc, pool, rs, half, stats, LN * (i + 2), rs_ready)
                    pool.wait_ge(h_ready, E * i + e + 1)
                    if e == 0 and not first(i, 2):
                        pool.wait_ge(y_done, UNITS * NT * (i - 1))
                    nc.gpsimd.tensor_tensor(hlo[:, u, e, :], h[:, e % 3, :], hhi[:, u, e, :],
                                            ALU.subtract).then_inc(hlo_ready, 1)
                if not first(i, 1):
                    inverse_root(nc, pool, rs2, half, stats2, LN * i, rs2_ready)

            over_supertiles(pool, body)
            add_out(NST - 2, 0)
            inverse_root(nc, pool, rs2, half, stats2, LN * NST, rs2_ready)
            add_out(NST - 1, 1)


NHG = GH // 4
HALF = ST // 2
NC = NT
MASKED = -1.0e30


def gla_constants():
    s, t = np.arange(P)[:, None], np.arange(P)[None, :]
    heads = np.zeros((3, 32, J, P), np.float32)
    for h in range(GH):
        heads[:, h, h // 2, GD * (h % 2):GD * (h % 2 + 1)] = 1.0
    minus = np.zeros((NHG, 32, 4), np.float32)
    for a in range(3):
        for r in range(4):
            minus[:, 12 + 4 * a + r, r] = -1.0
    return {
        "up_to": (s <= t).astype(np.float32),
        "after": (s > t).astype(np.float32),
        "masked": np.where(s > t, np.float32(MASKED), np.float32(0)).astype(np.float32),
        "heads": heads.reshape(3 * 32, J * P),
        "minus": minus.reshape(NHG * 32, 4),
    }


def phase_gla(nc, x, wq_t, wk_t, wv_t, wg_t, wog_t, wo_t, wd_t, bd, norm_cols, ident_d, const, x_out):
    with ExitStack() as ctx:
        m = Place(nc, ctx, "gla")
        wg, wk, wv, wq, wog = (m.sb(s, [P, 2, KD, HID], F32R) for s in ("wg", "wk", "wv", "wq", "wog"))
        wo, wd = m.sb("wo", [P, J, D]), m.sb("wd", [P, KD, GH])
        b_d, norm_w = m.sb("b_d", [P, GH]), m.sb("norm_w", [P, J])
        ident, up_to, after = m.sb("ident", [P, P]), m.sb("up_to", [P, P]), m.sb("after", [P, P])
        ident_b, masked_b = m.sb("ident_b", [P, P], BF16), m.sb("masked_b", [P, 4, P], BF16)
        heads_b = m.sb("heads_b", [96, J, P], BF16)
        minus = m.sb("minus", [P, 4])
        ones = m.sb("ones", [P, 1])
        half, half_set = m.sb("half", [P, NT]), m.sem("half_set")
        xin = m.sb("xin", [P, 2, NT, D])
        xn = m.sb("xn", [P, NT, D])
        xhi, xlo = m.sb("xhi", [P, 2, KD, ST], F32R), m.sb("xlo", [P, 2, KD, ST], F32R)
        st, mv, rs = m.sb("st", [P, NT, 6]), m.sb("mv", [P, NT, 2]), m.sb("rs", [P, 2, NT])
        st2, mv2, rs2 = m.sb("st2", [P, NT, 6]), m.sb("mv2", [P, NT, 2]), m.sb("rs2", [P, 2, NT])
        rs3 = m.sb("rs3", [P, 2, 1])
        y = m.sb("y", [P, NT, D])
        z, zabs, zexp, glog = (m.sb(s, [P, NC, GH]) for s in ("z", "zabs", "zexp", "glog"))
        to_end = m.sb("to_end", [P, NC, GH])
        gparts = m.sb("gparts", [96, ST], BF16)
        gmid, grest = m.sb("gmid", [GH, ST], BF16), m.sb("grest", [GH, ST])
        rows_t = m.sb("rows_t", [P, NC, 4, P], BF16)
        rows_s = m.sb("rows_s", [P, ST], BF16)
        q, og = m.sb("q", [P, J, HALF]), m.sb("og", [P, J, HALF])
        sg = m.sb("sg", [P, 2, ST])
        kg, v = m.sb("kg", [P, 2, HID]), m.sb("v", [P, 2, HID])
        kT = m.sb("kT", [P, 2, J, P])
        kw = m.sb("kw", [P, HID])
        eg, qe = m.sb("eg", [P, J, P]), m.sb("qe", [P, J, P])
        dm = m.sb("dm", [P, 2, 4, P])
        osq = qe
        yT, osum = m.sb("yT", [P, J, P]), m.sb("osum", [P, P])
        state = m.sb("state", [P, J, P])
        psP = m.ps("psP", [P, 2, ST])
        psA, psD = m.ps("psA", [P, 4, P]), m.ps("psD", [P, 4, P])
        psO = m.ps("psO", [P, 2, 4, P])
        psX = m.ps("psX", [P, 4, P])
        psW = m.ps("psW", [P, ST])

        ident_in, const_in, w_in, x_in = m.sem("ident_in"), m.sem("const_in"), m.sem("w_in"), m.sems("x_in", 2)
        stage_in, w_hi_ready, w_lo_ready, xlo_ready = m.sems("stage_in", 2), m.sem("w_hi_ready"), m.sem("w_lo_ready"), m.sem("xlo_ready")
        const_set, zero_set, wo_scaled = m.sem("const_set"), m.sem("zero_set"), m.sem("wo_scaled")
        stats, rs_ready, xn_ready, turned, xT_ready = (m.sem(s) for s in ("stats", "rs_ready", "xn_ready", "turned", "xT_ready"))
        stats2, rs2_ready, yn_ready = m.sem("stats2"), m.sem("rs2_ready"), m.sem("yn_ready")
        z_done, decay, soft, g_rows_done, w_done, to_end_ready, gsplit, rows_in = (
            m.sem(s) for s in ("z_done", "decay", "soft", "g_rows_done", "after_done", "to_end_ready", "gsplit", "rows_in"))
        q_done, q_ready, og_done, og_ready = (m.sem(s) for s in ("q_done", "q_ready", "og_done", "og_ready"))
        g_done, sig_ready, k_done, kg_ready, v_done, v_ready = (
            m.sem(s) for s in ("g_done", "sig_ready", "k_done", "kg_ready", "v_done", "v_ready"))
        kt_done, kt_ready, kw_ready = m.sem("kt_done"), m.sem("kt_ready"), m.sem("kw_ready")
        d_done, d_ready, qe_ready, a_done, ad_ready = (m.sem(s) for s in ("d_done", "d_ready", "qe_ready", "a_done", "ad_ready"))
        o_done, yT_ready, osq_ready, osum_ready = (m.sem(s) for s in ("o_done", "yT_ready", "osq_ready", "osum_ready"))
        kv_done, decayed, state_ready, state_zero = (m.sem(s) for s in ("kv_done", "decayed", "state_ready", "state_zero"))
        out_done, square_ready, rs3_ready, y_ready = (m.sem(s) for s in ("out_done", "square_ready", "rs3_ready", "y_ready"))
        xo_ready, x_outd = m.sem("xo_ready"), m.sem("x_out")
        xv, ov = tokens(x), tokens(x_out)
        stages = (q, og)
        N_CONST, N_ROWS = 16 * 7, 16 * 24
        TURNING = 2
        PAIRS = J // 2
        G_AT = 2
        PASSES = ((0, xhi), (0, xlo), (1, xhi))
        D_USES = 2 + NHG
        block = ctx.enter_context(nc.Block())

        def wide(a, n):
            return a.to_broadcast([*a.shape[:-1], n])

        @block.sync
        def _(sp):
            sp.dma_start(xin[:, 0, :, :], xv[0]).then_inc(x_in[0], 16)
            sp.dma_start(ident[:, :], ident_d).then_inc(ident_in, 16)
            for n, d in enumerate((wg_t, wk_t, wv_t, wq_t, wog_t)):
                if n >= 2:
                    sp.wait_ge(w_lo_ready, n - 1)
                sp.dma_start(stages[n % 2][:, :, :].rearrange("p j t -> p (j t)").rearrange("p (k o) -> p k o", k=KD),
                             d.rearrange("(k p) o -> p k o", p=P)).then_inc(stage_in[n % 2], 16)
                if n != 1:
                    continue
                sp.dma_start(up_to[:, :], const["up_to"]).then_inc(const_in, 16)
                sp.dma_start(after[:, :], const["after"]).then_inc(const_in, 16)
                sp.dma_start(kg[:, 0, 0:P], const["masked"]).then_inc(const_in, 16)
                sp.dma_start(v[0:96, 0, :], const["heads"]).then_inc(const_in, 16)
                sp.dma_start(minus[:, :], const["minus"]).then_inc(const_in, 16)
                sp.dma_start(b_d[:, :], row(bd)).then_inc(const_in, 16)
                sp.dma_start(norm_w[:, :], norm_cols).then_inc(const_in, 16)
                for w, dd in ((wd, wd_t), (wo, wo_t)):
                    sp.dma_start(w[:, :, :], dd.rearrange("(k p) o -> p k o", p=P)).then_inc(w_in, 16)

            def body(i, u, last):
                sp.wait_ge(gsplit, 5 * (i + 1))
                for a in range(3):
                    for r in range(4):
                        sp.dma_start(rows_t[4 * a + r:4 * a + r + 97:32, :, r, :],
                                     gparts[32 * a + r:32 * a + r + 13:4, :].rearrange("p (n t) -> p n t", t=P)
                                     ).then_inc(rows_in, 16)
                    for hg in range(NHG):
                        sp.dma_start(rows_s[32 * hg + 12 + 4 * a:32 * hg + 16 + 4 * a, :],
                                     gparts[32 * a + 4 * hg:32 * a + 4 * hg + 4, :]).then_inc(rows_in, 16)
                if not first(i, 1):
                    sp.wait_ge(xo_ready, i)
                    sp.dma_start(ov[i - 1], y[:, :, :]).then_inc(x_outd, 16)
                if not last:
                    sp.dma_start(xin[:, 1 - u, :, :], xv[i + 1]).then_inc(x_in[1 - u], 16)

            over_supertiles(sp, body)
            sp.wait_ge(xo_ready, NST)
            sp.dma_start(ov[NST - 1], y[:, :, :]).then_inc(x_outd, 16)
            sp.wait_ge(x_outd, 16 * NST)

        @block.tensor
        def _(pe):
            def turn_in(i, k, after_kt):
                if k == 0:
                    pe.wait_ge(xn_ready, NT * (i + 1))
                if k:
                    pe.wait_ge(xlo_ready, KD * i + k)
                elif after_kt is not None:
                    pe.wait_ge(kt_ready, after_kt)
                turn(nc, xn, psX[:, :, :].rearrange("p j t -> p (j t)"), ident, k).then_inc(turned, 1)

            def project(bank, w, half, u, n, done):
                for k in range(KD):
                    for p, (part, xp) in enumerate(PASSES):
                        mm = pe.matmul(psP[:, bank, :], xp[:, u, k, n * P:(n + 1) * P],
                                       w[:, part, k, half * ST:(half + 1) * ST], start=(k == 0 and p == 0),
                                       stop=(k == KD - 1 and p == 2))
                mm.then_inc(done, 1)

            def gate(i, u, n, h):
                c = NC * i + n
                if h:
                    pe.wait_ge(sig_ready, 2 * c + 1)
                elif n % 2:
                    pe.wait_ge(og_ready, J * i + PAIRS * (n // 2 + 1))
                elif not (first(i, 1) and n == 0):
                    pe.wait_ge(v_ready, 2 * c - 1)
                project(0, wg, h, u, n, g_done)

            def key(i, u, n, h):
                c = NC * i + n
                if h:
                    pe.wait_ge(kg_ready, 2 * c + 1)
                elif n % 2 == 0 and not (first(i, 1) and n == 0):
                    pe.wait_ge(v_ready, 2 * c)
                project(1, wk, h, u, n, k_done)

            def values(i, u, n, h):
                c = NC * i + n
                pe.wait_ge(sig_ready if h == 0 else kg_ready, 2 * c + 2)
                project(h, wv, h, u, n, v_done)

            def out_project(c):
                pe.wait_ge(yT_ready, 2 * c + 2)
                pe.wait_ge(y_ready, c)
                for j in range(J):
                    pe.matmul(psW[:, 0:D], yT[:, j, :], wo[:, j, :], start=(j == 0), stop=(j == J - 1))
                pe.wait_ge(osum_ready, c + 1)
                pe.matmul(psW[:, D:D + 1], osum[:, :], ones[:, :], start=True, stop=True).then_inc(out_done, 1)

            def decay_inputs(i, u):
                c = NC * i
                if not first(i, 1):
                    pe.wait_ge(state_ready, 2 * c)
                for n in range(NC):
                    for k in range(KD):
                        for p, xp in enumerate((xhi, xlo)):
                            mm = pe.matmul(psX[:, 0, n * GH:(n + 1) * GH],
                                           xp[:, u, k, n * P:(n + 1) * P].bitcast(F32), wd[:, k, :],
                                           start=(k == 0 and p == 0), stop=(k == KD - 1 and p == 1))
                mm.then_inc(z_done, 1)

            def decay_sums(i):
                pe.wait_ge(decay, 4 * (i + 1))
                if not first(i, 1):
                    pe.wait_ge(d_ready, D_USES * NC * i)
                for n in range(NC):
                    mm = pe.matmul(psD[0:GH, n, :], glog[:, n, :], up_to[:, :], start=True, stop=True)
                mm.then_inc(g_rows_done, 1)
                for n in range(NC):
                    mm = pe.matmul(psX[:, 0, n * GH:(n + 1) * GH], after[:, :], glog[:, n, :], start=True, stop=True)
                mm.then_inc(w_done, 1)

            def half_supertile(i, u, hf):
                c = NC * i + 2 * hf
                base = J * i + PAIRS * hf

                def pair(jp, w, done):
                    cols = slice(hf * HALF, (hf + 1) * HALF)
                    for j in (2 * jp, 2 * jp + 1):
                        for k in range(KD):
                            for p, (part, xp) in enumerate(PASSES):
                                mm = pe.matmul(psP[:, jp % 2, (j % 2) * HALF:(j % 2 + 1) * HALF],
                                               w[:, part, k, j * P:(j + 1) * P], xp[:, u, k, cols],
                                               start=(k == 0 and p == 0), stop=(k == KD - 1 and p == 2))
                    mm.then_inc(done, 1)

                if hf == 0:
                    pe.wait_ge(xT_ready, KD * (i + 1))
                    pe.wait_ge(xlo_ready, KD * (i + 1))
                    decay_inputs(i, u)
                for jp in range(PAIRS):
                    if jp < 2:
                        pe.wait_ge(v_ready, 2 * c + jp + 1)
                    else:
                        pe.wait_ge(q_ready, base + jp - 1)
                    pair(jp, wq, q_done)
                    if hf == 0 and jp == G_AT:
                        decay_sums(i)
                        if not first(i, 1):
                            out_project(c - 1)
                for jp in range(PAIRS):
                    if jp < 2:
                        pe.wait_ge(q_ready, base + jp + 3)
                    else:
                        pe.wait_ge(og_ready, base + jp - 1)
                    pair(jp, wog, og_done)

            def slot(i, u, n, last):
                c = NC * i + n
                ahead = not (last and n == NC - 1)
                nxt = (i, u, n + 1) if n < NC - 1 else (i + 1, 1 - u, 0)
                turning = n == TURNING and not last

                def keys_turned(g):
                    pe.wait_ge(kg_ready, 2 * c + g + 1)
                    if g:
                        pe.wait_ge(kt_ready, 2 * c + 1)
                    elif n == 0:
                        pe.wait_ge(to_end_ready, i + 1)
                    else:
                        pe.wait_ge(state_ready, 2 * c)
                    for jj in range(4):
                        j = 4 * g + jj
                        mm = pe.transpose(psX[:, jj, :], kg[:, n % 2, j * P:(j + 1) * P], ident[:, :])
                    mm.then_inc(kt_done, 1)

                def decay_of_channels(g):
                    if g == 0 and n == 0:
                        pe.wait_ge(gsplit, 5 * (i + 1))
                    if g or n:
                        pe.wait_ge(d_ready, D_USES * c + g)
                    for jj in range(4):
                        mm = pe.matmul(psD[:, jj, :], heads_b[:, 4 * g + jj, :], gparts[:, n * P:(n + 1) * P],
                                       start=True, stop=True)
                    mm.then_inc(d_done, 1)

                if n % 2 == 0:
                    keys_turned(0)
                if ahead:
                    if n == NC - 1:
                        pe.wait_ge(xlo_ready, KD * (i + 2))
                    gate(*nxt, 0)
                if n % 2:
                    keys_turned(0)
                if ahead:
                    key(*nxt, 0)
                keys_turned(1)
                decay_of_channels(0)
                if turning:
                    turn_in(i + 1, 0, 2 * c + 2)
                if ahead:
                    gate(*nxt, 1)
                decay_of_channels(1)
                if turning:
                    turn_in(i + 1, 1, None)
                if ahead:
                    key(*nxt, 1)
                if n:
                    out_project(c - 1)
                if n == 0:
                    pe.wait_ge(rows_in, N_ROWS * (i + 1))
                if n % 2 == 0:
                    pe.wait_ge(q_ready, J * i + PAIRS * (n // 2 + 1))
                t = slice((n % 2) * P, (n % 2 + 1) * P)

                def outputs(hg):
                    g = hg // 2
                    pe.wait_ge(ad_ready, NHG * c + hg + 1)
                    if hg % 2 == 0:
                        pe.wait_ge(qe_ready, 2 * c + g + 1)
                        pe.wait_ge(v_ready, 2 * c + g + 1)
                        if n == 0 and u == 0:
                            pe.wait_ge(state_zero, i + 2)
                        else:
                            pe.wait_ge(state_ready, 2 * c - 1 + g)
                        if not (first(i, 1) and n == 0):
                            pe.wait_ge(osq_ready, 2 * c - 1 + g)
                    for jj in range(2):
                        j = 2 * hg + jj
                        for odd in range(2):
                            h = 2 * j + odd
                            pe.matmul(psO[GD * odd:GD * (odd + 1), g, j % 4, :],
                                      v[:, n % 2, h * GD:(h + 1) * GD], dm[:, hg % 2, 2 * jj + odd, :],
                                      start=True, stop=False, skip_group_check=True)
                        mm = pe.matmul(psO[:, g, j % 4, :], state[:, j, :], qe[:, j, :], start=False, stop=True,
                                       skip_group_check=True)
                    mm.then_inc(o_done, 1)

                def update(g):
                    if g:
                        pe.wait_ge(state_ready, 2 * c + 1)
                    else:
                        pe.wait_ge(kw_ready, c + 1)
                        pe.wait_ge(v_ready, 2 * c + 2)
                        pe.wait_ge(kt_ready, 2 * c + 2)
                        if turning:
                            pe.wait_ge(xlo_ready, KD * (i + 2))
                    for jj in range(4):
                        j = 4 * g + jj
                        mm = pe.matmul(psX[:, jj, :], kw[:, j * P:(j + 1) * P], v[:, n % 2, j * P:(j + 1) * P],
                                       start=True, stop=True)
                    mm.then_inc(kv_done, 1)

                for hg in range(NHG):
                    pe.wait_ge(d_ready, D_USES * c + 2 + hg)
                    base = 32 * hg
                    pe.matmul(psD[:, :, :], ident_b[:, :], masked_b[:, :, :], start=True, stop=False)
                    pe.matmul(psD[:, :, :], rows_s[base:base + 24, n * P:(n + 1) * P],
                              rows_t[base:base + 24, n, :, :], start=False, stop=True,
                              tile_position=(base, 0)).then_inc(d_done, 1)
                    if not (first(i, 1) and n == 0 and hg == 0):
                        pe.wait_ge(ad_ready, NHG * c + hg)
                    pe.wait_ge(kt_ready, 2 * c + hg // 2 + 1)
                    for r in range(4):
                        j = 2 * hg + r // 2
                        mm = pe.matmul(psA[:, r, :], kT[:, r % 2, j, :], q[:, j, t],
                                       start=True, stop=True)
                    mm.then_inc(a_done, 1)
                    if hg < 2 and ahead:
                        values(*nxt, hg)
                    if hg:
                        outputs(hg - 1)
                update(0)
                outputs(NHG - 1)
                update(1)

            pe.wait_ge(ident_in, 16)
            for k in range(KD):
                turn_in(0, k, None)
            pe.wait_ge(xlo_ready, KD)
            pe.wait_ge(w_lo_ready, 1)
            for h in range(2):
                gate(0, 0, 0, h)
                pe.wait_ge(w_lo_ready, 2)
                key(0, 0, 0, h)
            pe.wait_ge(w_lo_ready, 3)
            for h in range(2):
                values(0, 0, 0, h)
            pe.wait_ge(w_lo_ready, 5)
            pe.wait_ge(const_in, N_CONST)
            pe.wait_ge(const_set, 7)
            pe.wait_ge(w_in, 32)
            pe.wait_ge(zero_set, 1)
            pe.wait_ge(wo_scaled, 2)

            def body(i, u, last):
                for n in range(NC):
                    if n % 2 == 0:
                        half_supertile(i, u, n // 2)
                    slot(i, u, n, last)

            over_supertiles(pe, body)
            out_project(NC * NST - 1)

        @block.scalar
        def _(act):
            def take_turned(i, u, k):
                act.wait_ge(turned, KD * i + k + 1)
                nc.scalar.copy(xhi[:, u, k, :], psX[:, :, :].rearrange("p j t -> p (j t)")).then_inc(xT_ready, 1)

            def sigmoid(i, n, h):
                c = NC * i + n
                act.wait_ge(g_done, 2 * c + h + 1)
                if not (first(i, 1) and n == 0):
                    act.wait_ge(kg_ready, 2 * c - 1 + h)
                nc.scalar.activation(sg[:, h, :], psP[:, 0, :], ACT.Tanh, scale=0.5).then_inc(sig_ready, 1)

            def take_values(i, n, h):
                act.wait_ge(v_done, 2 * (NC * i + n) + h + 1)
                nc.scalar.copy(v[:, n % 2, h * ST:(h + 1) * ST], psP[:, h, :]).then_inc(v_ready, 1)

            def half_supertile(i, u, hf):
                c = NC * i + 2 * hf
                base = J * i + PAIRS * hf
                if hf == 0:
                    act.wait_ge(decay, 4 * i + 2)
                    nc.scalar.activation(zexp[:, :, :], zabs[:, :, :], ACT.Exp, scale=-1.0).then_inc(soft, 1)
                if not (first(i, 1) and hf == 0):
                    act.wait_ge(qe_ready, 2 * c)
                for jp in range(PAIRS):
                    act.wait_ge(q_done, base + jp + 1)
                    nc.scalar.activation(q[:, 2 * jp:2 * jp + 2, :], psP[:, jp % 2, :].rearrange("p (j t) -> p j t", j=2),
                                         ACT.Copy, scale=0.5).then_inc(q_ready, 1)
                    if hf == 0 and jp == 0:
                        act.wait_ge(soft, 2 * i + 1)
                        nc.scalar.activation(zexp[:, :, :], zexp[:, :, :], ACT.Ln, bias=1.0).then_inc(soft, 1)
                    if hf == 0 and jp == G_AT:
                        act.wait_ge(w_done, i + 1)
                        if not first(i, 1):
                            act.wait_ge(kw_ready, c)
                        nc.scalar.activation(to_end[:, :, :].rearrange("p n h -> p (n h)"), psX[:, 0, 0:NC * GH],
                                             ACT.Exp).then_inc(to_end_ready, 1)
                if not (first(i, 1) and hf == 0):
                    act.wait_ge(yT_ready, 2 * c)
                for jp in range(PAIRS):
                    act.wait_ge(og_done, base + jp + 1)
                    nc.scalar.activation(og[:, 2 * jp:2 * jp + 2, :], psP[:, jp % 2, :].rearrange("p (j t) -> p j t", j=2),
                                         ACT.Tanh, scale=0.5).then_inc(og_ready, 1)

            def slot(i, u, n, last):
                c = NC * i + n
                ahead = not (last and n == NC - 1)
                nxt = (i, n + 1) if n < NC - 1 else (i + 1, 0)
                turning = n == TURNING and not last

                def keys_taken(g):
                    act.wait_ge(kt_done, 2 * c + g + 1)
                    for odd in range(2):
                        rows = slice(GD * odd, GD * (odd + 1))
                        last_copy = nc.scalar.copy(kT[rows, odd, 4 * g:4 * g + 4, :], psX[rows, :, :])
                    last_copy.then_inc(kt_ready, 1)

                def exp_of_decay(g):
                    act.wait_ge(d_done, D_USES * c + g + 1)
                    if g == 0 and not (first(i, 1) and n == 0):
                        act.wait_ge(decayed, 2 * c)
                        act.wait_ge(qe_ready, 2 * c)
                    nc.scalar.activation(eg[:, 4 * g:4 * g + 4, :], psD[:, :, :], ACT.Exp).then_inc(d_ready, 1)

                if ahead:
                    sigmoid(*nxt, 0)
                keys_taken(0)
                keys_taken(1)
                exp_of_decay(0)
                if turning:
                    take_turned(i + 1, 1 - u, 0)
                if ahead:
                    sigmoid(*nxt, 1)
                exp_of_decay(1)
                if turning:
                    take_turned(i + 1, 1 - u, 1)
                for hg in range(NHG):
                    act.wait_ge(d_done, D_USES * c + 3 + hg)
                    if not (first(i, 1) and n == 0 and hg < 2):
                        act.wait_ge(o_done, NHG * c + hg - 1)
                    nc.scalar.activation(dm[:, hg % 2, :, :], psD[:, :, :], ACT.Exp).then_inc(d_ready, 1)
                    if hg < 2 and ahead:
                        take_values(*nxt, hg)
                for g in range(2):
                    act.wait_ge(yT_ready, 2 * c + g + 1)
                    if g == 0 and not (first(i, 1) and n == 0):
                        act.wait_ge(osum_ready, c)
                    nc.scalar.activation(osq[:, 4 * g:4 * g + 4, :], psO[:, g, :, :], ACT.Square).then_inc(osq_ready, 1)

            for n, w in enumerate((wg, wk, wv, wq, wog)):
                act.wait_ge(stage_in[n % 2], 16 * (n // 2 + 1))
                nc.scalar.copy(w[:, 0, :, :].rearrange("p k o -> p (k o)"),
                               stages[n % 2][:, :, :].rearrange("p j t -> p (j t)")).then_inc(w_hi_ready, 1)
                if n < KD:
                    take_turned(0, 0, n)
            act.wait_ge(const_set, 7)
            for h in range(2):
                sigmoid(0, 0, h)
            for h in range(2):
                take_values(0, 0, h)
            act.wait_ge(zero_set, 1)

            def body(i, u, last):
                for n in range(NC):
                    if n % 2 == 0:
                        half_supertile(i, u, n // 2)
                    slot(i, u, n, last)

            over_supertiles(act, body)

        @block.vector
        def _(dve):
            s, s2, t, dec = Steps(LN), Steps(LN), Steps(5), Steps(4)

            def pre(i, u):
                s.start(i)
                dve.wait_ge(x_in[u], 8 * (i - u) + 16)
                if not first(i, 1):
                    dve.wait_ge(turned, KD * i)
                normalize_tiles(nc, dve, xin[:, u, :, :], xn, st, mv, rs, stats, s, rs_ready, i + 1, xn_ready)
                s.end()

            def take_turned(i, u, k):
                dve.wait_ge(xT_ready, KD * i + k + 1)
                nc.vector.tensor_tensor(xlo[:, u, k, :], psX[:, :, :].rearrange("p j t -> p (j t)"), xhi[:, u, k, :],
                                        ALU.subtract).then_inc(xlo_ready, 1)

            def gated_keys(i, n, h):
                c = NC * i + n
                dve.wait_ge(k_done, 2 * c + h + 1)
                dve.wait_ge(sig_ready, 2 * c + h + 1)
                if h == 0 and not (first(i, 1) and n < 2):
                    dve.wait_ge(kw_ready, c - 1)
                nc.vector.scalar_tensor_tensor(kg[:, n % 2, h * ST:(h + 1) * ST], sg[:, h, :], 1.0, psP[:, 1, :],
                                               ALU.add, ALU.mult).then_inc(kg_ready, 1)

            def mean_square(c):
                dve.wait_ge(out_done, c + 1)
                nc.vector.tensor_scalar(rs3[:, 0, :], psW[:, D:D + 1], 1.0 / HID, RMS_EPS, ALU.mult,
                                        ALU.add).then_inc(square_ready, 1)

            def take_out(c, n, i_of_y):
                dve.wait_ge(rs3_ready, c + 1)
                if n == 0 and not first(i_of_y, 1):
                    dve.wait_ge(x_outd, 16 * i_of_y)
                nc.vector.tensor_scalar(y[:, n, :], psW[:, 0:D], rs3[:, 1, :], None, ALU.mult).then_inc(y_ready, 1)

            def norm_y(i):
                s2.start(i)
                dve.wait_ge(y_ready, NC * (i + 1))
                normalize_tiles(nc, dve, y, y, st2, mv2, rs2, stats2, s2, rs2_ready, i + 1, yn_ready)
                s2.end()

            def decays(i, u):
                c = NC * i
                dec.start(i)
                dve.wait_ge(z_done, i + 1)
                nc.vector.tensor_tensor(z[:, :, :], psX[:, 0, 0:NC * GH].rearrange("p (n h) -> p n h", h=GH),
                                        b_d[:, :].rearrange("p (n h) -> p n h", n=1).to_broadcast([P, NC, GH]),
                                        ALU.add).then_inc(decay, dec.inc())
                dve.wait_ge(decay, dec.now())
                if not first(i, 1):
                    dve.wait_ge(soft, 2 * i)
                nc.vector.scalar_tensor_tensor(zabs[:, :, :], z[:, :, :], -1.0, z[:, :, :], ALU.mult,
                                               ALU.max).then_inc(decay, dec.inc())
                dve.wait_ge(soft, 2 * i + 2)
                nc.vector.scalar_tensor_tensor(z[:, :, :], z[:, :, :], 0.0, zexp[:, :, :], ALU.max,
                                               ALU.add).then_inc(decay, dec.inc())
                dve.wait_ge(decay, dec.now())
                nc.vector.tensor_scalar(glog[:, :, :], z[:, :, :], -1.0, None, ALU.mult).then_inc(decay, dec.inc())
                dec.end()
                t.start(i)
                dve.wait_ge(g_rows_done, i + 1)
                g_rows = psD[0:GH, :, :].rearrange("p n t -> p (n t)")
                nc.vector.tensor_copy(gparts[0:GH, :], g_rows).then_inc(gsplit, t.inc())
                dve.wait_ge(gsplit, t.now())
                nc.vector.tensor_tensor(grest[:, :], g_rows, gparts[0:GH, :], ALU.subtract).then_inc(gsplit, t.inc())
                dve.wait_ge(gsplit, t.now())
                nc.vector.tensor_copy(gmid[:, :], grest[:, :]).then_inc(gsplit, t.inc())
                dve.wait_ge(gsplit, t.now())
                nc.vector.tensor_copy(gparts[32:32 + GH, :], gmid[:, :]).then_inc(gsplit, t.inc())
                nc.vector.tensor_tensor(gparts[64:64 + GH, :], grest[:, :], gmid[:, :], ALU.subtract).then_inc(gsplit, t.inc())
                t.end()
                if not first(i, 1):
                    mean_square(c - 1)
                    take_out(c - 1, NC - 1, i - 1)
                if not first(i, 1):
                    norm_y(i - 1)

            def slot(i, u, n, last):
                c = NC * i + n
                ahead = not (last and n == NC - 1)
                nxt = (i, n + 1) if n < NC - 1 else (i + 1, 0)

                def queries_decayed(g):
                    js = slice(4 * g, 4 * g + 4)
                    dve.wait_ge(d_ready, D_USES * c + g + 1)
                    if n % 2 == 0 and g == 0:
                        dve.wait_ge(q_ready, J * i + PAIRS * (n // 2 + 1))
                    if not (first(i, 1) and n == 0) and g == 0:
                        dve.wait_ge(osum_ready, c)
                    nc.vector.tensor_tensor(qe[:, js, :], q[:, js, (n % 2) * P:(n % 2 + 1) * P], eg[:, js, :],
                                            ALU.mult).then_inc(qe_ready, 1)

                turning = n == TURNING and not last
                if ahead:
                    gated_keys(*nxt, 0)
                queries_decayed(0)
                if turning:
                    take_turned(i + 1, 1 - u, 0)
                queries_decayed(1)
                if turning:
                    take_turned(i + 1, 1 - u, 1)
                if ahead:
                    gated_keys(*nxt, 1)
                if n:
                    mean_square(c - 1)

                def weighted(hg):
                    dve.wait_ge(a_done, NHG * c + hg + 1)
                    dve.wait_ge(d_ready, D_USES * c + 3 + hg)
                    nc.vector.tensor_tensor(dm[:, hg % 2, :, :], psA[:, :, :], dm[:, hg % 2, :, :],
                                            ALU.mult).then_inc(ad_ready, 1)

                def take_outputs(g):
                    js = slice(4 * g, 4 * g + 4)
                    dve.wait_ge(o_done, NHG * c + 2 * g + 2)
                    if n % 2 == 0 and g == 0:
                        dve.wait_ge(og_ready, J * i + PAIRS * (n // 2 + 1))
                    if g == 0 and not (first(i, 1) and n == 0):
                        dve.wait_ge(out_done, c)
                    nc.vector.scalar_tensor_tensor(yT[:, js, :], og[:, js, (n % 2) * P:(n % 2 + 1) * P], 1.0, psO[:, g, :, :],
                                                   ALU.add, ALU.mult).then_inc(yT_ready, 1)

                def update(g):
                    js = slice(4 * g, 4 * g + 4)
                    dve.wait_ge(kv_done, 2 * c + g + 1)
                    dve.wait_ge(decayed, 2 * c + g + 1)
                    for odd in range(2):
                        r = slice(GD * odd, GD * (odd + 1))
                        last_add = nc.vector.tensor_tensor(state[r, js, r], psX[r, :, r], state[r, js, r], ALU.add)
                    last_add.then_inc(state_ready, 1)

                weighted(0)
                if n:
                    take_out(c - 1, n - 1, i)
                weighted(1)
                weighted(2)
                take_outputs(0)
                weighted(3)
                update(0)
                take_outputs(1)
                update(1)
                dve.wait_ge(osq_ready, 2 * c + 2)
                nc.vector.tensor_reduce(osum[:, :], osq[:, :, :].rearrange("p j t -> p t j"), AX.X,
                                        ALU.add).then_inc(osum_ready, 1)
                if n == 0 and not last:
                    pre(i + 1, 1 - u)

            nc.vector.memset(ones[:, :], 1.0).then_inc(const_set, 1)
            nc.vector.memset(rows_s[:, :], 1.0).then_inc(const_set, 1)
            pre(0, 0)
            for n, w in enumerate((wg, wk, wv, wq, wog)):
                dve.wait_ge(w_hi_ready, n + 1)
                nc.vector.tensor_tensor(w[:, 1, :, :].rearrange("p k o -> p (k o)"),
                                        stages[n % 2][:, :, :].rearrange("p j t -> p (j t)"),
                                        w[:, 0, :, :].rearrange("p k o -> p (k o)"), ALU.subtract).then_inc(w_lo_ready, 1)
                if n < KD:
                    take_turned(0, 0, n)
            dve.wait_ge(const_in, N_CONST)
            nc.vector.tensor_copy(ident_b[:, :], ident[:, :]).then_inc(const_set, 1)
            nc.vector.tensor_copy(masked_b[:, :, :], kg[:, 0, 0:P].rearrange("p (a t) -> p a t", a=1)
                                  .to_broadcast([P, 4, P])).then_inc(const_set, 1)
            nc.vector.tensor_copy(heads_b[:, :, :].rearrange("p j t -> p (j t)"),
                                  v[0:96, 0, :]).then_inc(const_set, 1)
            nc.vector.memset(gparts[:, :], 0.0).then_inc(const_set, 1)
            nc.vector.tensor_copy(
                rows_t[:, :, :, :],
                minus[:, :].rearrange("p (n r t) -> p n r t", n=1, t=1).to_broadcast([P, NC, 4, P])
            ).then_inc(const_set, 1)
            dve.wait_ge(const_set, 7)
            for h in range(2):
                gated_keys(0, 0, h)

            def body(i, u, last):
                decays(i, u)
                for n in range(NC):
                    slot(i, u, n, last)

            over_supertiles(dve, body)
            mean_square(NC * NST - 1)
            take_out(NC * NST - 1, NC - 1, NST - 1)
            norm_y(NST - 1)

        @block.gpsimd
        def _(pool):
            def root_square(c):
                pool.wait_ge(square_ready, c + 1)
                nc.gpsimd.tensor_tensor(rs3[:, 1, :], rs3[:, 0, :], half[:, 0:1], ALU.pow).then_inc(rs3_ready, 1)

            def residual(i, u):
                inverse_root(nc, pool, rs2, half, stats2, LN * (i + 1), rs2_ready)
                pool.wait_ge(yn_ready, NT * (i + 1))
                nc.gpsimd.tensor_tensor(y[:, :, :], xin[:, u, :, :], y[:, :, :], ALU.add).then_inc(xo_ready, 1)

            def supertile(i, u):
                c = NC * i
                if not first(i, 1):
                    root_square(c - 1)
                if u == 0:
                    if not first(i, 1):
                        pool.wait_ge(state_ready, 2 * c)
                    nc.gpsimd.memset(state[:, :, :], 0.0).then_inc(state_zero, 2)
                if not first(i, 1):
                    residual(i - 1, 1 - u)

            def slot(i, u, n, last):
                c = NC * i + n
                pool.wait_ge(kg_ready, 2 * c + 2)
                if n == 0:
                    pool.wait_ge(to_end_ready, i + 1)
                if not (first(i, 1) and n == 0):
                    pool.wait_ge(kv_done, 2 * c)
                nc.gpsimd.tensor_tensor(kw[:, :].rearrange("p (h d) -> p h d", d=GD),
                                        kg[:, n % 2, :].rearrange("p (h d) -> p h d", d=GD),
                                        to_end[:, n, :].rearrange("p (h d) -> p h d", d=1).to_broadcast([P, GH, GD]),
                                        ALU.mult).then_inc(kw_ready, 1)
                if n:
                    root_square(c - 1)
                for g in range(2):
                    js = slice(4 * g, 4 * g + 4)
                    if g == 0:
                        if n == 0 and u == 0:
                            pool.wait_ge(state_zero, i + 2)
                        else:
                            pool.wait_ge(state_ready, 2 * c)
                    pool.wait_ge(o_done, NHG * c + 2 * g + 2)
                    nc.gpsimd.tensor_tensor(state[:, js, :], state[:, js, :],
                                            eg[:, js, P - 1:P].to_broadcast([P, 4, P]), ALU.mult).then_inc(decayed, 1)
                if n == 0 and not last:
                    inverse_root(nc, pool, rs, half, stats, LN * (i + 2), rs_ready)

            minus_half(nc, pool, half, half_set)
            inverse_root(nc, pool, rs, half, stats, LN, rs_ready)
            nc.gpsimd.memset(kT[:, :, :, :], 0.0).then_inc(zero_set, 1)
            pool.wait_ge(const_in, N_CONST)
            pool.wait_ge(w_in, 32)
            nc.gpsimd.tensor_tensor(wo[:, :, :], wo[:, :, :],
                                    norm_w[:, :].rearrange("p (j c) -> p j c", c=1).to_broadcast([P, J, D]),
                                    ALU.mult).then_inc(wo_scaled, 1)
            pool.wait_ge(wo_scaled, 1)
            nc.gpsimd.tensor_scalar(wo[:, :, :], wo[:, :, :], 0.5, None, ALU.mult).then_inc(wo_scaled, 1)

            def body(i, u, last):
                supertile(i, u)
                for n in range(NC):
                    slot(i, u, n, last)

            over_supertiles(pool, body)
            root_square(NC * NST - 1)
            residual(NST - 1, 1)


def sandwich(nc, x, qkv_w_t, qkv_b, qkv_b_cols, out_w_t, out_b, ffn_w1_t, ffn_b1_cols, ffn_w2_t, ffn_b2,
             wq_t, wk_t, wv_t, wo_t, wg_t, wog_t, wd_t, bd, norm_cols,
             gate_w, moe_w1, moe_b1_cols, moe_w2, moe_b2, ws1, bs1_col, ws2, bs2, route_scale,
             ident, up_to, after, masked, heads, minus, out):
    def scratch(name, shape, dt=F32):
        return nc.dram_tensor(name, shape, dt, kind="Internal").ap()

    parts = scratch("qk_parts", [2, NST, NG, 3, HG * AD, ST], BF16)
    v_aug = scratch("values", [NST, NG, P, NT, HG * VW])
    att = scratch("attended", [TOKENS, D])
    x2, x3 = (scratch(f"stream{k}", [TOKENS, D]) for k in (2, 3))
    const = {"up_to": up_to, "after": after, "masked": masked, "heads": heads, "minus": minus}
    phase_qkv(nc, x, qkv_w_t, qkv_b, qkv_b_cols, ident, parts, v_aug)
    phase_attention(nc, parts, v_aug, ident, att)
    phase_project_ffn(nc, x, att, out_w_t, out_b, ffn_w1_t, ffn_b1_cols, ffn_w2_t, ffn_b2, ident, x2)
    phase_gla(nc, x2, wq_t, wk_t, wv_t, wg_t, wog_t, wo_t, wd_t, bd, norm_cols, ident, const, x3)
    phase_experts(nc, x3, gate_w, moe_w1, moe_b1_cols, moe_w2, moe_b2, ws1, bs1_col, ws2, bs2, route_scale,
                  ident, out)



def kernel(**inputs):
    import concourse.bacc as bacc
    from concourse.bass_utils import run_bass_kernel_spmd

    a = {name: np.asarray(v) for name, v in inputs.items()}
    l0a, l0f, l1a, l1f = "L0_attn_", "L0_ffn_", "L1_attn_", "L1_ffn_"

    def columns(v):
        return v.reshape(-1, P).T

    def heads_in_turn(v):
        qk = v[:2 * D].reshape(2, NG, HG, AD, *v.shape[1:]).swapaxes(2, 3).reshape(2 * D, *v.shape[1:])
        return np.concatenate([qk, v[2 * D:]])

    laid_out = {
        "x": a[l0a + "x"].reshape(TOKENS, D),
        "qkv_w_t": heads_in_turn(a[l0a + "qkv_w"]).T,
        "qkv_b": a[l0a + "qkv_b"],
        "qkv_b_cols": columns(heads_in_turn(a[l0a + "qkv_b"])),
        "out_w_t": a[l0a + "out_w"].T,
        "out_b": a[l0a + "out_b"],
        "ffn_w1_t": a[l0f + "W1"].T,
        "ffn_b1_cols": columns(a[l0f + "b1"]),
        "ffn_w2_t": a[l0f + "W2"].T,
        "ffn_b2": a[l0f + "b2"],
        **{w.lower() + "_t": a[l1a + w].T for w in ("Wq", "Wk", "Wv", "Wo", "Wg", "Wog", "Wd")},
        "bd": a[l1a + "bd"],
        "norm_cols": columns(a[l1a + "norm_w"]),
        "gate_w": a[l1f + "gate_W"],
        "moe_w1": a[l1f + "W1"],
        "moe_b1_cols": a[l1f + "b1"].T,
        "moe_w2": a[l1f + "W2"],
        "moe_b2": a[l1f + "b2"],
        "ws1": a[l1f + "Ws1"],
        "bs1_col": a[l1f + "bs1"].reshape(EH, 1),
        "ws2": a[l1f + "Ws2"],
        "bs2": a[l1f + "bs2"],
        "route_scale": a[l1f + "route_scale"].reshape(1, 1),
        "ident": np.eye(P, dtype=np.float32),
        **gla_constants(),
    }
    nc = bacc.Bacc("TRN2", target_bir_lowering=False, num_devices=1)
    arrays, args = {}, {}
    for name, v in laid_out.items():
        v = np.ascontiguousarray(v)
        arrays[f"in_{name}"] = v
        args[name] = nc.dram_tensor(f"in_{name}", v.shape, mybir.dt.from_np(v.dtype), kind="ExternalInput").ap()
    out = nc.dram_tensor("out", [TOKENS, D], F32, kind="ExternalOutput").ap()
    sandwich(nc, **args, out=out)
    r = run_bass_kernel_spmd(nc, [arrays], core_ids=[0])
    return r.results[0]["out"].reshape(BATCH, SEQ, D)
```
